# Optimizing a Trainium2 kernel written in Bass

```python
import numpy as np
import jax
import jax.numpy as jnp

def _softmax(x, axis=-1):
    return jax.nn.softmax(x, axis=axis)

def _gelu(x):
    return jax.nn.gelu(x, approximate=True)

def _silu(x):
    return jax.nn.silu(x)

def _sigmoid(x):
    return jax.nn.sigmoid(x)

def _layernorm(x, axis=-1, eps=1e-05):
    m = jnp.mean(x, axis=axis, keepdims=True)
    v = jnp.var(x, axis=axis, keepdims=True)
    return (x - m) / jnp.sqrt(v + eps)

def _scatter_add(tgt, idx, src, axis=0):
    return tgt.at[idx].add(src)

def _segment_sum(src, seg, n):
    return jax.ops.segment_sum(src, seg, n)
kernel_name = 'mk_audio_tower_d2_tok_audfeat1024_r4_8943e0'

def setup_inputs(seed: int=0):
    np.random.seed(seed)
    _w = jnp.asarray

    def _rec_inputs():
        import jax
        import jax.numpy as jnp
        _rk = jax.random.key(seed)
        x = -7.10856e-05 + 0.999911 * jax.random.normal(jax.random.fold_in(_rk, 1), (128, 256, 256), jnp.float32)
        return x
    x = _rec_inputs()

    def _L0_tok_setup():
        import jax, jax.numpy as jnp
        import numpy as np
        BLOCK_SIZE = 16
        DIM = 256
        LN_EPS = 1e-05
        VAR_EPS = 1e-08
        key = jax.random.key(seed)
        ks = jax.random.split(key, 4)
        B, N, D = (8, 2048, DIM)
        x = jax.random.normal(ks[0], (B, N, D), dtype=jnp.float32)
        w_proj_w = jax.random.normal(ks[1], (D, 1), dtype=jnp.float32) * (1.0 / np.sqrt(D))
        w_proj_b = jnp.zeros((1,), dtype=jnp.float32)
        s_proj_w = jax.random.normal(ks[2], (3 * D, D), dtype=jnp.float32) * (1.0 / np.sqrt(3 * D))
        s_proj_b = jnp.zeros((D,), dtype=jnp.float32)
        ln_g = jnp.ones((D,), dtype=jnp.float32)
        ln_b = jnp.zeros((D,), dtype=jnp.float32)
        pos_emb = jax.random.normal(ks[3], (4096, D), dtype=jnp.float32)
        return {'x': x, 'w_proj_w': w_proj_w, 'w_proj_b': w_proj_b, 's_proj_w': s_proj_w, 's_proj_b': s_proj_b, 'ln_g': ln_g, 'ln_b': ln_b, 'pos_emb': pos_emb}
    _L0_tok_all = _L0_tok_setup()
    _L0_tok_in = {k: v for k, v in _L0_tok_all.items() if k in ('w_proj_w', 'w_proj_b', 's_proj_w', 's_proj_b', 'ln_g', 'ln_b', 'pos_emb')}
    del _L0_tok_all

    def _L0_attn_setup():
        import jax, jax.numpy as jnp
        import numpy as np
        B, S, E, H = (4, 1024, 256, 16)
        D = E // H

        def _xavier(key, out_f, in_f):
            lim = float(np.sqrt(6.0 / (in_f + out_f)))
            return jax.random.uniform(key, (out_f, in_f), jnp.float32, -lim, lim)

        def _feature_map(t):
            return jax.nn.elu(t) + 1.0
        key = jax.random.key(seed)
        ks = jax.random.split(key, 9)
        x = jax.random.normal(ks[0], (B, S, E), jnp.float32)
        Wq = _xavier(ks[1], E, E)
        Wk = _xavier(ks[2], E, E)
        Wv = _xavier(ks[3], E, E)
        Wo = _xavier(ks[4], E, E)
        bq = jnp.zeros((E,), jnp.float32)
        bk = jnp.zeros((E,), jnp.float32)
        bv = jnp.zeros((E,), jnp.float32)
        bo = jnp.zeros((E,), jnp.float32)
        return {'x': x, 'Wq': Wq, 'bq': bq, 'Wk': Wk, 'bk': bk, 'Wv': Wv, 'bv': bv, 'Wo': Wo, 'bo': bo}
    _L0_attn_all = _L0_attn_setup()
    _L0_attn_in = {k: v for k, v in _L0_attn_all.items() if k in ('Wq', 'bq', 'Wk', 'bk', 'Wv', 'bv', 'Wo', 'bo')}
    del _L0_attn_all

    def _L0_ffn_setup():
        import jax, jax.numpy as jnp
        import numpy as np
        BS, SLEN, DIM = (1, 512, 256)
        NUM_EXPERTS, TOP_K = (8, 2)
        HID = 352

        def _masked_grouped_mm(x, w, onehot):
            g = jnp.einsum('tk,gnk->tgn', x, w, preferred_element_type=jnp.float32)
            return jnp.einsum('tgn,tg->tn', g, onehot)

        def moe_forward(x, gate_w, expert_bias, w_up, w_down, shared_w_up, shared_w_down):
            bs, slen, dim = x.shape
            xf = x.reshape(-1, dim)
            scores = jax.nn.sigmoid((xf @ gate_w.T).astype(jnp.float32))
            biased = scores + expert_bias
            _, sel = jax.lax.top_k(biased, TOP_K)
            top_scores = jnp.take_along_axis(scores, sel, axis=-1)
            flat_sel = sel.reshape(-1)
            counts = jnp.bincount(flat_sel, length=NUM_EXPERTS)
            order = jnp.argsort(flat_sel, stable=True)
            scores_sorted = top_scores.reshape(-1)[order]
            token_ids = order // TOP_K
            routed_in = (xf[token_ids] * scores_sorted[:, None]).astype(x.dtype)
            seg = jnp.repeat(jnp.arange(NUM_EXPERTS), counts, total_repeat_length=flat_sel.shape[0])
            onehot = jax.nn.one_hot(seg, NUM_EXPERTS, dtype=jnp.float32)
            h = _masked_grouped_mm(routed_in.astype(jnp.bfloat16), w_up.astype(jnp.bfloat16), onehot)
            h = jnp.square(jax.nn.relu(h.astype(jnp.bfloat16)))
            routed_out = _masked_grouped_mm(h.astype(jnp.bfloat16), w_down.astype(jnp.bfloat16), onehot)
            routed_out = routed_out.astype(jnp.bfloat16).astype(x.dtype)
            hs = jnp.square(jax.nn.relu(xf @ shared_w_up.T))
            shared_out = hs @ shared_w_down.T
            combined = jnp.zeros((flat_sel.shape[0], dim), routed_out.dtype).at[order].set(routed_out)
            out = combined.reshape(-1, TOP_K, dim).sum(axis=1) + shared_out
            return out.reshape(bs, slen, dim)
        key = jax.random.key(seed)
        k = jax.random.split(key, 6)
        s = 0.02
        return {'x': jax.random.normal(k[0], (BS, SLEN, DIM), jnp.float32), 'gate_w': jax.random.normal(k[1], (NUM_EXPERTS, DIM), jnp.float32) * s, 'expert_bias': jnp.zeros((NUM_EXPERTS,), jnp.float32), 'w_up': jax.random.normal(k[2], (NUM_EXPERTS, HID, DIM), jnp.float32) * s, 'w_down': jax.random.normal(k[3], (NUM_EXPERTS, DIM, HID), jnp.float32) * s, 'shared_w_up': jax.random.normal(k[4], (HID, DIM), jnp.float32) * s, 'shared_w_down': jax.random.normal(k[5], (DIM, HID), jnp.float32) * s}
    _L0_ffn_all = _L0_ffn_setup()
    _L0_ffn_in = {k: v for k, v in _L0_ffn_all.items() if k in ('gate_w', 'expert_bias', 'w_up', 'w_down', 'shared_w_up', 'shared_w_down')}
    del _L0_ffn_all

    def _L1_attn_setup():
        import jax, jax.numpy as jnp
        import numpy as np
        B, L, D_MODEL, H, HD, FD = (1, 256, 256, 16, 64, 64)
        EPS = 1e-12

        def _heads(t):
            b, l, _ = t.shape
            return t.reshape(b, l, H, HD).transpose(0, 2, 1, 3)

        def _feature_map(t, K):
            f = jnp.einsum('hdf,bhld->bhlf', K, t)
            feats = jnp.concatenate([jax.nn.softmax(f, axis=-1), jax.nn.softmax(-f, axis=-1)], axis=-1)
            return jnp.maximum(feats, EPS)
        key = jax.random.key(seed)
        ks = jax.random.split(key, 7)
        s = 1.0 / np.sqrt(D_MODEL)
        return {'x': jax.random.normal(ks[0], (B, L, D_MODEL), jnp.float32), 'Wq': jax.random.normal(ks[1], (D_MODEL, H * HD), jnp.float32) * s, 'Wk': jax.random.normal(ks[2], (D_MODEL, H * HD), jnp.float32) * s, 'Wv': jax.random.normal(ks[3], (D_MODEL, H * HD), jnp.float32) * s, 'Wo': jax.random.normal(ks[4], (H * HD, D_MODEL), jnp.float32) * s, 'Kq': jax.random.normal(ks[5], (H, HD, FD), jnp.float32) * (1.0 / np.sqrt(HD)), 'Kk': jax.random.normal(ks[6], (H, HD, FD), jnp.float32) * (1.0 / np.sqrt(HD))}
    _L1_attn_all = _L1_attn_setup()
    _L1_attn_in = {k: v for k, v in _L1_attn_all.items() if k in ('Wq', 'Wk', 'Wv', 'Wo', 'Kq', 'Kk')}
    del _L1_attn_all

    def _L1_ffn_setup():
        import jax, jax.numpy as jnp
        import numpy as np
        TOP_K = 2

        def _swiglu_mlp(x, wgu, wd, inter):
            gu = x @ wgu
            a = jax.nn.silu(gu[:, :inter]) * gu[:, inter:]
            return a @ wd
        key = jax.random.key(seed)
        ks = jax.random.split(key, 6)
        H, I, E = (256, 704, 8)
        B, S = (2, 256)
        w = 0.02
        return {'x': jax.random.normal(ks[0], (B, S, H), jnp.float32), 'gate_w': jax.random.normal(ks[1], (H, E), jnp.float32) * w, 'base_wgu': jax.random.normal(ks[2], (H, 2 * I), jnp.float32) * w, 'base_wd': jax.random.normal(ks[3], (I, H), jnp.float32) * w, 'exp_wgu': jax.random.normal(ks[4], (E, H, 2 * I), jnp.float32) * w, 'exp_wd': jax.random.normal(ks[5], (E, I, H), jnp.float32) * w}
    _L1_ffn_all = _L1_ffn_setup()
    _L1_ffn_in = {k: v for k, v in _L1_ffn_all.items() if k in ('gate_w', 'base_wgu', 'base_wd', 'exp_wgu', 'exp_wd')}
    del _L1_ffn_all
    return {'x': x, 'L0_tok_w_proj_w': _L0_tok_in['w_proj_w'], 'L0_tok_w_proj_b': _L0_tok_in['w_proj_b'], 'L0_tok_s_proj_w': _L0_tok_in['s_proj_w'], 'L0_tok_s_proj_b': _L0_tok_in['s_proj_b'], 'L0_tok_ln_g': _L0_tok_in['ln_g'], 'L0_tok_ln_b': _L0_tok_in['ln_b'], 'L0_tok_pos_emb': _L0_tok_in['pos_emb'], 'L0_attn_Wq': _L0_attn_in['Wq'], 'L0_attn_bq': _L0_attn_in['bq'], 'L0_attn_Wk': _L0_attn_in['Wk'], 'L0_attn_bk': _L0_attn_in['bk'], 'L0_attn_Wv': _L0_attn_in['Wv'], 'L0_attn_bv': _L0_attn_in['bv'], 'L0_attn_Wo': _L0_attn_in['Wo'], 'L0_attn_bo': _L0_attn_in['bo'], 'L0_ffn_gate_w': _L0_ffn_in['gate_w'], 'L0_ffn_expert_bias': _L0_ffn_in['expert_bias'], 'L0_ffn_w_up': _L0_ffn_in['w_up'], 'L0_ffn_w_down': _L0_ffn_in['w_down'], 'L0_ffn_shared_w_up': _L0_ffn_in['shared_w_up'], 'L0_ffn_shared_w_down': _L0_ffn_in['shared_w_down'], 'L1_attn_Wq': _L1_attn_in['Wq'], 'L1_attn_Wk': _L1_attn_in['Wk'], 'L1_attn_Wv': _L1_attn_in['Wv'], 'L1_attn_Wo': _L1_attn_in['Wo'], 'L1_attn_Kq': _L1_attn_in['Kq'], 'L1_attn_Kk': _L1_attn_in['Kk'], 'L1_ffn_gate_w': _L1_ffn_in['gate_w'], 'L1_ffn_base_wgu': _L1_ffn_in['base_wgu'], 'L1_ffn_base_wd': _L1_ffn_in['base_wd'], 'L1_ffn_exp_wgu': _L1_ffn_in['exp_wgu'], 'L1_ffn_exp_wd': _L1_ffn_in['exp_wd']}

def reference(x, L0_tok_w_proj_w, L0_tok_w_proj_b, L0_tok_s_proj_w, L0_tok_s_proj_b, L0_tok_ln_g, L0_tok_ln_b, L0_tok_pos_emb, L0_attn_Wq, L0_attn_bq, L0_attn_Wk, L0_attn_bk, L0_attn_Wv, L0_attn_bv, L0_attn_Wo, L0_attn_bo, L0_ffn_gate_w, L0_ffn_expert_bias, L0_ffn_w_up, L0_ffn_w_down, L0_ffn_shared_w_up, L0_ffn_shared_w_down, L1_attn_Wq, L1_attn_Wk, L1_attn_Wv, L1_attn_Wo, L1_attn_Kq, L1_attn_Kk, L1_ffn_gate_w, L1_ffn_base_wgu, L1_ffn_base_wd, L1_ffn_exp_wgu, L1_ffn_exp_wd):
    import jax
    import jax.numpy as jnp

    def _L0_tok_ref(x, w_proj_w, w_proj_b, s_proj_w, s_proj_b, ln_g, ln_b, pos_emb):
        import jax, jax.numpy as jnp
        import numpy as np
        BLOCK_SIZE = 16
        DIM = 256
        LN_EPS = 1e-05
        VAR_EPS = 1e-08
        B, N, D = x.shape
        bs = BLOCK_SIZE
        pad = (bs - N % bs) % bs
        if pad > 0:
            x = jnp.pad(x, ((0, 0), (0, pad), (0, 0)))
        n_blocks = x.shape[1] // bs
        blocks = x.reshape(B, n_blocks, bs, D)
        w = jnp.einsum('bnkd,do->bnko', blocks, w_proj_w)[..., 0] + w_proj_b[0]
        w = jax.nn.softmax(w, axis=-1)
        wmean = jnp.einsum('bnk,bnkd->bnd', w, blocks)
        diff = blocks - wmean[:, :, None, :]
        wvar = jnp.einsum('bnk,bnkd->bnd', w, diff * diff)
        wstd = jnp.sqrt(wvar + VAR_EPS)
        bmax = blocks.max(axis=2)
        stats = jnp.concatenate([wmean, wstd, bmax], axis=-1)
        out = jnp.einsum('bnf,fd->bnd', stats, s_proj_w) + s_proj_b
        mu = out.mean(axis=-1, keepdims=True)
        var = out.var(axis=-1, keepdims=True)
        out = (out - mu) * jax.lax.rsqrt(var + LN_EPS) * ln_g + ln_b
        out = out + pos_emb[jnp.arange(n_blocks)]
        return out

    def _L0_attn_ref(x, Wq, bq, Wk, bk, Wv, bv, Wo, bo):
        import jax, jax.numpy as jnp
        import numpy as np
        B, S, E, H = (4, 1024, 256, 16)
        D = E // H

        def _xavier(key, out_f, in_f):
            lim = float(np.sqrt(6.0 / (in_f + out_f)))
            return jax.random.uniform(key, (out_f, in_f), jnp.float32, -lim, lim)

        def _feature_map(t):
            return jax.nn.elu(t) + 1.0
        b, s, _ = x.shape
        Q = (x @ Wq.T + bq).reshape(b, s, H, D)
        K = (x @ Wk.T + bk).reshape(b, s, H, D)
        V = (x @ Wv.T + bv).reshape(b, s, H, D)
        Q = _feature_map(Q)
        K = _feature_map(K)
        KV = jnp.einsum('bshd,bshe->bhde', K, V)
        K_sum = K.sum(axis=1)
        Z = 1.0 / (jnp.einsum('bshd,bhd->bsh', Q, K_sum) + 1e-06)
        out = jnp.einsum('bshd,bhde,bsh->bshe', Q, KV, Z)
        out = out.reshape(b, s, E)
        out = out @ Wo.T + bo
        return out

    def _L0_ffn_ref(x, gate_w, expert_bias, w_up, w_down, shared_w_up, shared_w_down):
        import jax, jax.numpy as jnp
        import numpy as np
        BS, SLEN, DIM = (1, 512, 256)
        NUM_EXPERTS, TOP_K = (8, 2)
        HID = 352

        def _masked_grouped_mm(x, w, onehot):
            g = jnp.einsum('tk,gnk->tgn', x, w, preferred_element_type=jnp.float32)
            return jnp.einsum('tgn,tg->tn', g, onehot)

        def moe_forward(x, gate_w, expert_bias, w_up, w_down, shared_w_up, shared_w_down):
            bs, slen, dim = x.shape
            xf = x.reshape(-1, dim)
            scores = jax.nn.sigmoid((xf @ gate_w.T).astype(jnp.float32))
            biased = scores + expert_bias
            _, sel = jax.lax.top_k(biased, TOP_K)
            top_scores = jnp.take_along_axis(scores, sel, axis=-1)
            flat_sel = sel.reshape(-1)
            counts = jnp.bincount(flat_sel, length=NUM_EXPERTS)
            order = jnp.argsort(flat_sel, stable=True)
            scores_sorted = top_scores.reshape(-1)[order]
            token_ids = order // TOP_K
            routed_in = (xf[token_ids] * scores_sorted[:, None]).astype(x.dtype)
            seg = jnp.repeat(jnp.arange(NUM_EXPERTS), counts, total_repeat_length=flat_sel.shape[0])
            onehot = jax.nn.one_hot(seg, NUM_EXPERTS, dtype=jnp.float32)
            h = _masked_grouped_mm(routed_in.astype(jnp.bfloat16), w_up.astype(jnp.bfloat16), onehot)
            h = jnp.square(jax.nn.relu(h.astype(jnp.bfloat16)))
            routed_out = _masked_grouped_mm(h.astype(jnp.bfloat16), w_down.astype(jnp.bfloat16), onehot)
            routed_out = routed_out.astype(jnp.bfloat16).astype(x.dtype)
            hs = jnp.square(jax.nn.relu(xf @ shared_w_up.T))
            shared_out = hs @ shared_w_down.T
            combined = jnp.zeros((flat_sel.shape[0], dim), routed_out.dtype).at[order].set(routed_out)
            out = combined.reshape(-1, TOP_K, dim).sum(axis=1) + shared_out
            return out.reshape(bs, slen, dim)
        return moe_forward(x, gate_w, expert_bias, w_up, w_down, shared_w_up, shared_w_down)

    def _L1_attn_ref(x, Wq, Wk, Wv, Wo, Kq, Kk):
        import jax, jax.numpy as jnp
        import numpy as np
        B, L, D_MODEL, H, HD, FD = (1, 256, 256, 16, 64, 64)
        EPS = 1e-12

        def _heads(t):
            b, l, _ = t.shape
            return t.reshape(b, l, H, HD).transpose(0, 2, 1, 3)

        def _feature_map(t, K):
            f = jnp.einsum('hdf,bhld->bhlf', K, t)
            feats = jnp.concatenate([jax.nn.softmax(f, axis=-1), jax.nn.softmax(-f, axis=-1)], axis=-1)
            return jnp.maximum(feats, EPS)
        q = _heads(x @ Wq)
        k = _heads(x @ Wk)
        v = _heads(x @ Wv)
        qf = _feature_map(q, Kq)
        kf = _feature_map(k, Kk)
        kv = jnp.cumsum(kf[:, :, :, None, :] * v[..., None], axis=2)
        o = jnp.einsum('bhlf,bhldf->bhld', qf, kv)
        z = jnp.einsum('bhlf,bhlf->bhl', qf, jnp.cumsum(kf, axis=2)) + EPS
        o = o / z[..., None]
        y = o.transpose(0, 2, 1, 3).reshape(x.shape[0], x.shape[1], H * HD)
        return y @ Wo

    def _L1_ffn_ref(x, gate_w, base_wgu, base_wd, exp_wgu, exp_wd):
        import jax, jax.numpy as jnp
        import numpy as np
        TOP_K = 2

        def _swiglu_mlp(x, wgu, wd, inter):
            gu = x @ wgu
            a = jax.nn.silu(gu[:, :inter]) * gu[:, inter:]
            return a @ wd
        orig_shape = x.shape
        H = orig_shape[-1]
        I = base_wd.shape[0]
        E = gate_w.shape[1]
        xt = x.reshape(-1, H)
        T = xt.shape[0]
        base_y = _swiglu_mlp(xt, base_wgu, base_wd, I)
        logits = xt @ gate_w
        probs = jax.nn.softmax(logits.astype(jnp.float32), axis=-1)
        topw, topi = jax.lax.top_k(probs, TOP_K)
        topw = topw / jnp.sum(topw, axis=-1, keepdims=True)
        topw = topw.astype(x.dtype)
        cw = jnp.zeros((T, E), x.dtype).at[jnp.arange(T)[:, None], topi].add(topw)
        out = base_y
        for e in range(E):
            ye = _swiglu_mlp(xt, exp_wgu[e], exp_wd[e], I)
            out = out + cw[:, e:e + 1] * ye
        return out.reshape(orig_shape)
    h = _L0_tok_ref(x, L0_tok_w_proj_w, L0_tok_w_proj_b, L0_tok_s_proj_w, L0_tok_s_proj_b, L0_tok_ln_g, L0_tok_ln_b, L0_tok_pos_emb)
    h = h + _L0_attn_ref(_layernorm(h, axis=-1), L0_attn_Wq, L0_attn_bq, L0_attn_Wk, L0_attn_bk, L0_attn_Wv, L0_attn_bv, L0_attn_Wo, L0_attn_bo)
    h = h + _L0_ffn_ref(_layernorm(h, axis=-1), L0_ffn_gate_w, L0_ffn_expert_bias, L0_ffn_w_up, L0_ffn_w_down, L0_ffn_shared_w_up, L0_ffn_shared_w_down)
    h = h + _L1_attn_ref(_layernorm(h, axis=-1), L1_attn_Wq, L1_attn_Wk, L1_attn_Wv, L1_attn_Wo, L1_attn_Kq, L1_attn_Kk)
    h = h + _L1_ffn_ref(_layernorm(h, axis=-1), L1_ffn_gate_w, L1_ffn_base_wgu, L1_ffn_base_wd, L1_ffn_exp_wgu, L1_ffn_exp_wd)
    return h

_drawn_inputs = setup_inputs


def setup_inputs(seed=0):
    import zlib

    import numpy as np

    out = dict(_drawn_inputs(seed))
    spreads = {'L0_tok_s_proj_b': (0.0, 0.1),
     'L0_tok_ln_g': (1.0, 0.2),
     'L0_tok_ln_b': (0.0, 0.1),
     'L0_attn_bq': (0.0, 0.8),
     'L0_attn_bk': (0.0, 0.8),
     'L0_attn_bv': (0.0, 0.1),
     'L0_attn_bo': (0.0, 0.1),
     'L0_ffn_expert_bias': (0.0, 0.559)}
    factors = {'L0_attn_Wq': 4.11,
     'L0_ffn_gate_w': 5.922,
     'L0_ffn_w_up': 5.582,
     'L0_ffn_w_down': 4.946,
     'L1_attn_Wq': 2.695,
     'L1_ffn_gate_w': 6.276,
     'L1_ffn_base_wgu': 4.669,
     'L1_ffn_base_wd': 4.393,
     'L1_ffn_exp_wgu': 6.266,
     'L1_ffn_exp_wd': 6.455}
    for name, (base, spread) in spreads.items():
        noise = np.random.default_rng([zlib.crc32(name.encode()), seed]).standard_normal(out[name].shape)
        drawn = base * np.exp(spread * noise) if base else spread * noise
        out[name] = jnp.asarray(drawn.astype(out[name].dtype))
    for name, factor in factors.items():
        out[name] = (out[name] * factor).astype(out[name].dtype)
    return out
```

```python
from contextlib import ExitStack

import concourse.bass as bass
from concourse import mybir

P = 128
F32 = mybir.dt.float32
BF16 = mybir.dt.bfloat16
ALU = mybir.AluOpType
ACT = mybir.ActivationFunctionType
AX = mybir.AxisListType.X
ds = bass.ds

D = 256
DC = D // P
BLK = 16
NPOS = 16
TOK = 2048
NT = TOK // P
BPT = P // NPOS
H0, D0 = 16, 16
H1, D1, F1 = 16, 64, 64
E0, HID0 = 8, 352
E1, HID1 = 8, 704
GT = 512
NG = TOK // GT
TPG = GT // P
SB = 256
NB = (2 * TOK + E1 * (SB - 1)) // SB
W1 = DC * 2 * HID1
HF1 = HID1 // P
HT1 = HID1 - HF1 * P
LN_EPS = 1e-5
VAR_EPS = 1e-8
FEAT_EPS = 1e-12


class Chain:

    def __init__(self, eng, sem):
        self.eng, self.sem, self.base, self.n = eng, sem, 0, 0

    def start(self, base):
        self.base, self.n = base, 0

    def done(self, ins):
        ins.then_inc(self.sem, 1)
        self.n += 1
        self.eng.wait_ge(self.sem, self.base + self.n)


def chunks(n):
    return [(c, min(P, n - c * P)) for c in range((n + P - 1) // P)]


class Core:

    def __init__(self, nc, ctx, ins, out):
        self.nc, self.ins, self.out = nc, ins, out
        self.ctx = ctx
        f = lambda name, shape, dt=F32: ctx.enter_context(nc.sbuf_tensor(name, shape, dt))
        self.h = f("h", [P, NT * D])
        self.mv = f("mv", [P, NT, 2])
        self.moments = f("moments", [P, NT * 6])
        self.std = f("std", [P, NT])
        self.rstd = f("rstd", [P, NT])
        self.ident = f("ident", [P, P])
        self.eps_ln = f("eps_ln", [P, 1])
        self.eps_var = f("eps_var", [P, 1])
        self.sems = []
        self.passes = nc.alloc_semaphore("passes")
        self.slots_cleared = nc.alloc_semaphore("slots_cleared")

    def sem(self, name):
        self.sems.append(self.nc.alloc_semaphore(name))
        return self.sems[-1]

    def renew_semaphores(self):
        self.nc.clear_and_free_semaphores(self.sems)
        self.sems = []
        self.nc.all_engine_barrier()

    def hold(self, eng):
        eng.sem_inc(self.passes, 1)



class Turn:

    def __init__(self, turn, k, per):
        self.turn, self.k, self.per = turn, k, per
        self.t = turn * per + k
        self.b = k % 2
        self.half = turn * (per // 2) + k // 2

    def at(self, d):
        q = self.k + d
        return Turn(self.turn + q // self.per, q % self.per, self.per)


def tile(t, per=2):
    return Turn(t // per, t % per, per)


def wait(eng, sem, count):
    if not isinstance(count, int) or count > 0:
        eng.wait_ge(sem, count)


def over(eng, first, last, step, per=2, peel=None):
    lo = max(peel or max(per, 4), first + -first % per)
    hi = max(lo, last - last % per)
    for t in range(first, min(lo, last)):
        step(tile(t, per))
    if hi > lo:
        with eng.Fori(lo // per, hi // per) as i:
            for k in range(per):
                step(Turn(i, k, per))
    for t in range(max(hi, first), last):
        step(tile(t, per))


def stage_statistics(K, stats):
    nc, ins = K.nc, K.ins
    with ExitStack() as ctx:
        sb = lambda name, shape, dt=F32: ctx.enter_context(nc.sbuf_tensor(name, shape, dt))
        x = sb("x", [P, 2, BLK * D])
        diff = sb("diff", [P, 2, BLK * D])
        diag = sb("diag", [P, 2, BLK * P])
        wproj = sb("wproj", [P, D])
        bproj = sb("bproj", [P, 1])
        prod = sb("prod", [P, BLK, D])
        logit = sb("logit", [P, 2, BLK])
        logitb = sb("logitb", [P, 2, BLK])
        nmax = sb("nmax", [P, 2])
        expw = sb("expw", [P, 2, BLK])
        esum = sb("esum", [P, 2])
        rsum = sb("rsum", [P, 2])
        w = sb("w", [P, 2, BLK])
        ps_mean = [ctx.enter_context(nc.psum_tensor(f"ps_mean{b}", [P, 512], F32)) for b in range(2)]
        ps_var = [ctx.enter_context(nc.psum_tensor(f"ps_var{b}", [P, 512], F32)) for b in range(2)]

        const_loaded = K.sem("t_const_loaded")
        ident_steps = K.sem("t_ident_steps")
        x_loaded = [K.sem(f"t_x_loaded{b}") for b in range(2)]
        nmax_ready = K.sem("t_nmax_ready")
        exp_ready = K.sem("t_exp_ready")
        w_ready = K.sem("t_w_ready")
        diag_ready = K.sem("t_diag_ready")
        mean_ready = K.sem("t_mean_ready")
        diff_ready = K.sem("t_diff_ready")
        square_ready = K.sem("t_square_ready")
        var_ready = K.sem("t_var_ready")
        var_copied = K.sem("t_var_copied")
        steps = K.sem("t_vector_steps")
        block = ctx.enter_context(nc.Block())

        @block.sync
        def _(sp):
            sp.dma_start(wproj[:, :], ins["w_proj"].partition_broadcast(P)).then_inc(const_loaded, 16)
            sp.dma_start(bproj[:, :], ins["b_proj"].partition_broadcast(P)).then_inc(const_loaded, 16)

            def load(a):
                wait(sp, diff_ready, a.t - 1)
                sp.dma_start(x[:, a.b, :], ins["x"][ds(a.t * P, P), :]).then_inc(x_loaded[a.b], 16)
            over(sp, 0, NT, load)

        @block.gpsimd
        def _(pool):
            pool.memset(K.eps_ln[:, :], LN_EPS)
            pool.memset(K.eps_var[:, :], VAR_EPS)
            pool.memset(K.ident[:, :], 0.0).then_inc(ident_steps, 1)
            pool.wait_ge(ident_steps, 1)
            pool.affine_select(out=K.ident[:, :], in_=K.ident[:, :], compare_op=ALU.not_equal, fill=1.0,
                               base=0, pattern=[[-1, P]], channel_multiplier=1).then_inc(ident_steps, 1)
            pool.wait_ge(ident_steps, 2)

            def spread(a):
                pool.wait_ge(w_ready, a.t + 1)
                wait(pool, var_ready, a.t - 1)
                pool.tensor_tensor(out=diag[:, a.b, :].rearrange("p (k m) -> p k m", k=BLK),
                                   in0=K.ident[:, :].rearrange("p (a m) -> p a m", a=1).broadcast_to([P, BLK, P]),
                                   in1=w[:, a.b, :].rearrange("p (k a) -> p k a", a=1).broadcast_to([P, BLK, P]),
                                   op=ALU.mult).then_inc(diag_ready, 1)
            over(pool, 0, NT, spread)

        @block.vector
        def _(dve):
            chain = Chain(dve, steps)
            dve.wait_ge(const_loaded, 32)

            def head(a):
                chain.start(a.t * 3)
                dve.wait_ge(x_loaded[a.b], a.half * 16 + 16)
                for k in range(BLK):
                    last = dve.tensor_tensor_reduce(out=prod[:, k, :], in0=x[:, a.b, k * D:(k + 1) * D], in1=wproj[:, :],
                                                    scale=1.0, scalar=0.0, op0=ALU.mult, op1=ALU.add,
                                                    accum_out=logit[:, a.b, k:k + 1])
                chain.done(last)
                chain.done(dve.tensor_scalar(out=logitb[:, a.b, :], in0=logit[:, a.b, :], scalar1=bproj[:, 0:1],
                                             scalar2=None, op0=ALU.add))
                dve.tensor_reduce(out=nmax[:, a.b:a.b + 1], in_=logitb[:, a.b, :], axis=AX, op=ALU.max,
                                  negate=True).then_inc(nmax_ready, 1)
                dve.tensor_reduce(out=stats[:, ds(a.t * 3 * D + 2 * D, D)],
                                  in_=x[:, a.b, :].rearrange("p (k d) -> p d k", k=BLK), axis=AX, op=ALU.max)
                dve.wait_ge(exp_ready, a.t + 1)
                wait(dve, diag_ready, a.t - 1)
                chain.done(dve.reciprocal(rsum[:, a.b:a.b + 1], esum[:, a.b:a.b + 1]))
                dve.tensor_scalar(out=w[:, a.b, :], in0=expw[:, a.b, :], scalar1=rsum[:, a.b:a.b + 1],
                                  scalar2=None, op0=ALU.mult).then_inc(w_ready, 1)

            def deviations(a):
                dve.wait_ge(mean_ready, a.t + 1)
                wait(dve, var_ready, a.t - 1)
                dve.tensor_tensor(out=diff[:, a.b, :].rearrange("p (k d) -> p k d", k=BLK),
                                  in0=x[:, a.b, :].rearrange("p (k d) -> p k d", k=BLK),
                                  in1=ps_mean[a.b][:, 0:D].rearrange("p (a d) -> p a d", a=1).broadcast_to([P, BLK, D]),
                                  op=ALU.subtract).then_inc(diff_ready, 1)

            def step(a):
                head(a)
                deviations(a.at(-1))
            head(tile(0))
            over(dve, 1, NT, step)
            deviations(tile(NT - 1))

        @block.scalar
        def _(act):
            def weights(a):
                act.wait_ge(nmax_ready, a.t + 1)
                act.activation(expw[:, a.b, :], logitb[:, a.b, :], ACT.Exp, bias=nmax[:, a.b:a.b + 1],
                               accum_out=esum[:, a.b:a.b + 1]).then_inc(exp_ready, 1)

            def squares(a):
                act.wait_ge(diff_ready, a.t + 1)
                act.activation(stats[:, ds(a.t * 3 * D, D)], ps_mean[a.b][:, 0:D], ACT.Copy)
                act.activation(diff[:, a.b, :], diff[:, a.b, :], ACT.Square).then_inc(square_ready, 1)

            def variance(a):
                act.wait_ge(var_ready, a.t + 1)
                act.activation(stats[:, ds(a.t * 3 * D + D, D)], ps_var[a.b][:, 0:D], ACT.Copy).then_inc(var_copied, 1)

            def step(a):
                weights(a)
                squares(a.at(-1))
                variance(a.at(-2))
            weights(tile(0))
            weights(tile(1))
            squares(tile(0))
            over(act, 2, NT, step)
            squares(tile(NT - 1))
            variance(tile(NT - 2))
            variance(tile(NT - 1))

        @block.tensor
        def _(pe):
            def mean(a):
                pe.wait_ge(diag_ready, a.t + 1)
                wait(pe, square_ready, a.t - 1)
                for k in range(BLK):
                    last = pe.matmul(ps_mean[a.b][:, 0:D], diag[:, a.b, k * P:(k + 1) * P], x[:, a.b, k * D:(k + 1) * D],
                                     start=(k == 0), stop=(k == BLK - 1))
                last.then_inc(mean_ready, 1)

            def variance(a):
                pe.wait_ge(square_ready, a.t + 1)
                wait(pe, var_copied, a.t - 1)
                for k in range(BLK):
                    last = pe.matmul(ps_var[a.b][:, 0:D], diag[:, a.b, k * P:(k + 1) * P], diff[:, a.b, k * D:(k + 1) * D],
                                     start=(k == 0), stop=(k == BLK - 1))
                last.then_inc(var_ready, 1)

            def step(a):
                mean(a)
                variance(a.at(-1))
            mean(tile(0))
            over(pe, 1, NT, step)
            variance(tile(NT - 1))


def stage_projection(K, stats):
    nc, ins = K.nc, K.ins
    SC = 3 * DC
    with ExitStack() as ctx:
        sb = lambda name, shape, dt=F32: ctx.enter_context(nc.sbuf_tensor(name, shape, dt))
        wsp = sb("wsp", [P, SC, D])
        bsp = sb("bsp", [P, D])
        st = sb("st", [P, 2, 3 * D])
        sT = sb("sT", [P, 2, SC * P])
        ps_t = [ctx.enter_context(nc.psum_tensor(f"ps_t{b}", [P, 1024], F32)) for b in range(2)]
        ps_o = [ctx.enter_context(nc.psum_tensor(f"ps_o{b}", [P, 512], F32)) for b in range(2)]
        w_loaded = K.sem("p_w_loaded")
        st_ready = K.sem("p_st_ready")
        transposed = K.sem("p_transposed")
        sT_ready = K.sem("p_sT_ready")
        out_ready = K.sem("p_out_ready")
        out_read = K.sem("p_out_read")
        block = ctx.enter_context(nc.Block())

        @block.sync
        def _(sp):
            sp.dma_start(wsp[:, :, :], ins["s_proj_w"].rearrange("(c p) n -> p c n", p=P)).then_inc(w_loaded, 16)
            sp.dma_start(bsp[:, :], ins["s_proj_b"].partition_broadcast(P)).then_inc(w_loaded, 16)

        @block.scalar
        def _(act):
            def stage(a):
                wait(act, transposed, a.t - 1)
                act.activation(st[:, a.b, 0:D], stats[:, ds(a.t * 3 * D, D)], ACT.Copy)
                act.activation(st[:, a.b, D:2 * D], stats[:, ds(a.t * 3 * D + D, D)], ACT.Sqrt, bias=K.eps_var[:, 0:1])
                act.activation(st[:, a.b, 2 * D:3 * D], stats[:, ds(a.t * 3 * D + 2 * D, D)], ACT.Copy).then_inc(st_ready, 1)

            def evacuate(a):
                act.wait_ge(transposed, a.t + 1)
                wait(act, out_ready, a.t - 1)
                act.activation(sT[:, a.b, :], ps_t[a.b][:, 0:SC * P], ACT.Copy).then_inc(sT_ready, 1)

            def step(a):
                stage(a)
                evacuate(a.at(-1))
            stage(tile(0))
            over(act, 1, NT, step)
            evacuate(tile(NT - 1))

        @block.tensor
        def _(pe):
            def transposes(a):
                pe.wait_ge(st_ready, a.t + 1)
                wait(pe, sT_ready, a.t - 1)
                for c in range(SC):
                    last = pe.transpose(ps_t[a.b][:, c * P:(c + 1) * P], st[:, a.b, c * P:(c + 1) * P], K.ident[:, :])
                last.then_inc(transposed, 1)

            def project(a):
                pe.wait_ge(sT_ready, a.t + 1)
                wait(pe, out_read, a.t - 1)
                for c in range(SC):
                    last = pe.matmul(ps_o[a.b][:, 0:D], sT[:, a.b, c * P:(c + 1) * P], wsp[:, c, :],
                                     start=(c == 0), stop=(c == SC - 1))
                last.then_inc(out_ready, 1)

            def step(a):
                transposes(a)
                project(a.at(-1))
            pe.wait_ge(w_loaded, 32)
            transposes(tile(0))
            over(pe, 1, NT, step)
            project(tile(NT - 1))

        @block.vector
        def _(dve):
            dve.wait_ge(w_loaded, 32)

            def finish(a):
                dve.wait_ge(out_ready, a.t + 1)
                dve.tensor_tensor(out=K.h[:, ds(a.t * D, D)], in0=ps_o[a.b][:, 0:D], in1=bsp[:, :],
                                  op=ALU.add).then_inc(out_read, 1)
                take_moments(K, dve, a, out_read, a.t + 1)
            over(dve, 0, NT, finish)


def take_moments(K, dve, a, sem, count):
    dve.wait_ge(sem, count)
    K.hold(dve)
    dve.bn_stats(out=K.moments[:, ds(a.t * 6, 6)], in_=K.h[:, ds(a.t * D, D)])


def prepare_norm(K, dve, sems):
    gathered, std_ready, rstd_ready = sems
    for t in range(NT):
        last = dve.bn_aggr(out=K.mv[:, t, :], in_=K.moments[:, t * 6:t * 6 + 6])
    last.then_inc(gathered, 1)
    dve.wait_ge(std_ready, 1)
    dve.reciprocal(K.rstd[:, :], K.std[:, :]).then_inc(rstd_ready, 1)
    dve.wait_ge(rstd_ready, 1)


def root_norm(K, act, sems):
    gathered, std_ready, _ = sems
    act.wait_ge(gathered, 1)
    act.activation(K.std[:, :], K.mv[:, :, 1], ACT.Sqrt, bias=K.eps_ln[:, 0:1]).then_inc(std_ready, 1)


def norm_sems(K, stage):
    return [K.sem(f"{stage}_{n}") for n in ("gathered", "std_ready", "rstd_ready")]


def normalise(K, dve, a, out):
    return dve.tensor_scalar(out=out, in0=K.h[:, ds(a.t * D, D)], scalar1=K.mv[:, ds(a.t, 1), 0],
                             scalar2=K.rstd[:, ds(a.t, 1)], op0=ALU.subtract, op1=ALU.mult)


def stage_token_norm(K):
    nc, ins = K.nc, K.ins
    with ExitStack() as ctx:
        sb = lambda name, shape, dt=F32: ctx.enter_context(nc.sbuf_tensor(name, shape, dt))
        gain = sb("gain", [P, D])
        shift = sb("shift", [P, D])
        pos = sb("pos", [P, D])
        xn = sb("n_xn", [P, 2, D])
        xg = sb("n_xg", [P, 2, D])
        loaded = K.sem("n_loaded")
        norm = norm_sems(K, "n")
        shift_ready = K.sem("n_shift_ready")
        normed = K.sem("n_normed")
        scaled = K.sem("n_scaled")
        added = K.sem("n_added")
        block = ctx.enter_context(nc.Block())

        @block.sync
        def _(sp):
            sp.dma_start(gain[:, :], ins["ln_g"].partition_broadcast(P)).then_inc(loaded, 16)
            sp.dma_start(shift[:, :], ins["ln_b"].partition_broadcast(P)).then_inc(loaded, 16)
            for j in range(BPT):
                sp.dma_start(pos[j * NPOS:(j + 1) * NPOS, :], ins["pos_emb"][0:NPOS, :]).then_inc(loaded, 16)

        @block.scalar
        def _(act):
            root_norm(K, act, norm)

        @block.gpsimd
        def _(pool):
            pool.wait_ge(loaded, 16 * (2 + BPT))
            pool.tensor_tensor(out=shift[:, :], in0=shift[:, :], in1=pos[:, :], op=ALU.add).then_inc(shift_ready, 1)
            pool.wait_ge(shift_ready, 1)

            def scale(a):
                pool.wait_ge(normed, a.t + 1)
                wait(pool, added, a.t - 1)
                pool.tensor_tensor(out=xg[:, a.b, :], in0=xn[:, a.b, :], in1=gain[:, :], op=ALU.mult).then_inc(scaled, 1)
            over(pool, 0, NT, scale)

        @block.vector
        def _(dve):
            prepare_norm(K, dve, norm)
            dve.wait_ge(shift_ready, 1)

            def centre(a):
                wait(dve, scaled, a.t - 1)
                normalise(K, dve, a, xn[:, a.b, :]).then_inc(normed, 1)

            def finish(a):
                dve.wait_ge(scaled, a.t + 1)
                dve.tensor_tensor(out=K.h[:, ds(a.t * D, D)], in0=xg[:, a.b, :], in1=shift[:, :], op=ALU.add).then_inc(added, 1)
                take_moments(K, dve, a, added, a.t + 1)

            def step(a):
                centre(a)
                finish(a.at(-1))
            centre(tile(0))
            over(dve, 1, NT, step)
            finish(tile(NT - 1))


def stage_attention0(K):
    nc, ins = K.nc, K.ins
    HC = P // D0
    VW = D0 + 1
    with ExitStack() as ctx:
        sb = lambda name, shape, dt=F32: ctx.enter_context(nc.sbuf_tensor(name, shape, dt))
        wq, wk, wv, wo = (sb("a_" + n, [P, DC, D]) for n in ("wq", "wk", "wv", "wo"))
        bqk = sb("a_bqk", [P, 2 * DC])
        bv, bo = sb("a_bv", [P, D]), sb("a_bo", [P, D])
        same = sb("a_same", [P, 4, P])
        head = sb("a_head", [P, HC])
        xn = sb("a_xn", [P, 2, D])
        xT = sb("a_xT", [P, 2, D])
        qk = sb("a_qk", [P, 2, 4, P])
        low = sb("a_low", [P, 2, 4, P])
        q = sb("a_q", [P, 2, DC, P])
        k = sb("a_k", [P, 2, DC, P])
        kh = sb("a_kh", [P, 2, DC * HC, P])
        v = sb("a_v", [P, 2, H0, VW])
        sc = sb("a_sc", [P, 2, 4, P])
        den = sb("a_den", [P, 2, H0])
        rden = sb("a_rden", [P, 2, H0])
        y = sb("a_y", [P, 2, D])
        yT = sb("a_yT", [P, 2, D])
        ps = lambda name: ctx.enter_context(nc.psum_tensor(name, [P, 512], F32))
        ps_x, ps_qk, ps_v, ps_o, ps_yT, ps_w = (ps("a_ps_" + n) for n in ("x", "qk", "v", "o", "yT", "w"))
        ps_s = [ps(f"a_ps_s{b}") for b in range(2)]
        loaded, masks, ones_set = K.sem("a_loaded"), K.sem("a_masks"), K.sem("a_ones_set")
        norm = norm_sems(K, "a")
        names = ("xn_ready xT_ps xT_ready qk_ps v_ps qk_ready low_in low_ready q_ready k_ready kh_ready v_ready "
                 "s_ps s_ready o_ps o_read y_ready yT_ps yT_ready w_ps h_ready moved steps").split()
        S = {n: K.sem("a_" + n) for n in names}
        block = ctx.enter_context(nc.Block())

        @block.sync
        def _(sp):
            for t, n in ((wq, "a0_wqT"), (wk, "a0_wkT"), (wv, "a0_wvT"), (wo, "a0_woT")):
                sp.dma_start(t[:, :, :], ins[n].rearrange("(c p) n -> p c n", p=P)).then_inc(loaded, 16)
            with nc.allow_non_contiguous_dma(reason="512 biases, once"):
                sp.dma_start(bqk[:, 0:DC], ins["a0_bq"].rearrange("(c p) -> p c", p=P)).then_inc(loaded, 16)
                sp.dma_start(bqk[:, DC:2 * DC], ins["a0_bk"].rearrange("(c p) -> p c", p=P)).then_inc(loaded, 16)
            sp.dma_start(bv[:, :], ins["a0_bv"].partition_broadcast(P)).then_inc(loaded, 16)
            sp.dma_start(bo[:, :], ins["a0_bo"].partition_broadcast(P)).then_inc(loaded, 16)

        @block.gpsimd
        def _(pool):
            batch_mask(pool, same, NPOS, masks, causal=False)
            head_mask(pool, head, HC, D0, masks, 3)
            pool.memset(v[:, :, :, D0:VW], 1.0).then_inc(ones_set, 1)

            def spread(a):
                pool.wait_ge(S["k_ready"], a.t + 1)
                wait(pool, S["s_ps"], (a.t - 1) * 4)
                for c in range(DC):
                    last = pool.tensor_tensor(out=kh[:, a.b, c * HC:(c + 1) * HC, :],
                                              in0=k[:, a.b, c:c + 1, :].broadcast_to([P, HC, P]),
                                              in1=head[:, :].rearrange("p (h a) -> p h a", a=1).broadcast_to([P, HC, P]), op=ALU.mult)
                last.then_inc(S["kh_ready"], 1)
            over(pool, 0, NT, spread)

        @block.scalar
        def _(act):
            root_norm(K, act, norm)

            def take_xT(a):
                act.wait_ge(S["xT_ps"], a.t + 1)
                wait(act, S["v_ps"], a.t - 1)
                act.activation(xT[:, a.b, :], ps_x[:, 0:D], ACT.Copy).then_inc(S["xT_ready"], 1)

            def exps(a):
                act.wait_ge(S["low_in"], a.t + 1)
                act.activation(low[:, a.b, :, :], low[:, a.b, :, :], ACT.Exp).then_inc(S["low_ready"], 1)

            def take_yT(a):
                act.wait_ge(S["yT_ps"], a.t + 1)
                wait(act, S["w_ps"], a.t - 1)
                act.activation(yT[:, a.b, :], ps_yT[:, 0:D], ACT.Copy).then_inc(S["yT_ready"], 1)

            def step(a):
                take_xT(a)
                exps(a)
                take_yT(a.at(-2))
            take_xT(tile(0))
            exps(tile(0))
            take_xT(tile(1))
            exps(tile(1))
            over(act, 2, NT, step)
            take_yT(tile(NT - 2))
            take_yT(tile(NT - 1))

        @block.tensor
        def _(pe):
            pe.wait_ge(loaded, 128)

            def front(a):
                pe.wait_ge(S["xn_ready"], a.t + 1)
                wait(pe, S["xT_ready"], a.t)
                for c in range(DC):
                    last = pe.transpose(ps_x[:, c * P:(c + 1) * P], xn[:, a.b, c * P:(c + 1) * P], K.ident[:, :])
                last.then_inc(S["xT_ps"], 1)
                pe.wait_ge(S["xT_ready"], a.t + 1)
                wait(pe, S["qk_ready"], a.t)
                for j, wt in enumerate((wq, wk)):
                    for m in range(DC):
                        for c in range(DC):
                            last = pe.matmul(ps_qk[:, (j * DC + m) * P:(j * DC + m + 1) * P], wt[:, c, m * P:(m + 1) * P],
                                             xT[:, a.b, c * P:(c + 1) * P], start=(c == 0), stop=(c == DC - 1))
                last.then_inc(S["qk_ps"], 1)
                wait(pe, S["v_ready"], a.t)
                for c in range(DC):
                    last = pe.matmul(ps_v[:, 0:D], xT[:, a.b, c * P:(c + 1) * P], wv[:, c, :], start=(c == 0), stop=(c == DC - 1))
                last.then_inc(S["v_ps"], 1)

            def scores(a, g):
                n = a.t * 4 + g
                wait(pe, S["s_ready"], n - 1)
                for j in range(4):
                    hd = g * 4 + j
                    last = pe.matmul(ps_s[g % 2][:, j * P:(j + 1) * P], kh[:, a.b, hd, :], q[:, a.b, hd // HC, :], start=True, stop=True)
                last.then_inc(S["s_ps"], 1)

            def values(a, g):
                n = a.t * 4 + g
                pe.wait_ge(S["s_ready"], n + 1)
                if g == 0:
                    wait(pe, S["o_read"], a.t)
                for j in range(4):
                    hd = g * 4 + j
                    last = pe.matmul(ps_o[:, hd * VW:(hd + 1) * VW], sc[:, g % 2, j, :], v[:, a.b, hd, :], start=True, stop=True)
                last.then_inc(S["o_ps"], 1)

            def attend(a):
                pe.wait_ge(S["kh_ready"], a.t + 1)
                pe.wait_ge(S["q_ready"], a.t + 1)
                pe.wait_ge(S["v_ready"], a.t + 1)
                scores(a, 0)
                for g in range(1, 4):
                    scores(a, g)
                    values(a, g - 1)
                values(a, 3)

            def back(a):
                pe.wait_ge(S["y_ready"], a.t + 1)
                wait(pe, S["yT_ready"], a.t)
                for c in range(DC):
                    last = pe.transpose(ps_yT[:, c * P:(c + 1) * P], y[:, a.b, c * P:(c + 1) * P], K.ident[:, :])
                last.then_inc(S["yT_ps"], 1)
                pe.wait_ge(S["yT_ready"], a.t + 1)
                wait(pe, S["h_ready"], a.t)
                for c in range(DC):
                    last = pe.matmul(ps_w[:, 0:D], yT[:, a.b, c * P:(c + 1) * P], wo[:, c, :], start=(c == 0), stop=(c == DC - 1))
                last.then_inc(S["w_ps"], 1)

            def step(a):
                front(a)
                back(a.at(-2))
                attend(a.at(-1))
            front(tile(0))
            front(tile(1))
            attend(tile(0))
            over(pe, 2, NT, step)
            back(tile(NT - 2))
            attend(tile(NT - 1))
            back(tile(NT - 1))

        @block.vector
        def _(dve):
            chain = Chain(dve, S["steps"])
            prepare_norm(K, dve, norm)
            dve.wait_ge(loaded, 128)
            dve.wait_ge(masks, 6)
            dve.wait_ge(ones_set, 1)

            def centre(a):
                wait(dve, S["xT_ps"], a.t - 1)
                normalise(K, dve, a, xn[:, a.b, :]).then_inc(S["xn_ready"], 1)

            def features(a):
                dve.wait_ge(S["qk_ps"], a.t + 1)
                wait(dve, S["s_ps"], (a.t - 1) * 4)
                wait(dve, S["kh_ready"], a.t - 1)
                dve.tensor_tensor(out=qk[:, a.b, :, :], in0=ps_qk[:, :].rearrange("p (c m) -> p c m", c=4),
                                  in1=bqk[:, :].rearrange("p (c a) -> p c a", a=1).broadcast_to([P, 4, P]),
                                  op=ALU.add).then_inc(S["qk_ready"], 1)
                dve.wait_ge(S["qk_ready"], a.t + 1)
                dve.tensor_scalar(out=low[:, a.b, :, :], in0=qk[:, a.b, :, :], scalar1=0.0, scalar2=None, op0=ALU.min).then_inc(S["low_in"], 1)
                dve.wait_ge(S["v_ps"], a.t + 1)
                wait(dve, S["o_ps"], (a.t - 1) * 4)
                dve.tensor_tensor(out=v[:, a.b, :, 0:D0], in0=ps_v[:, 0:D].rearrange("p (h e) -> p h e", h=H0),
                                  in1=bv[:, :].rearrange("p (h e) -> p h e", h=H0), op=ALU.add).then_inc(S["v_ready"], 1)
                dve.wait_ge(S["low_ready"], a.t + 1)
                dve.scalar_tensor_tensor(out=k[:, a.b, :, :], in0=qk[:, a.b, 2:4, :], scalar=0.0, in1=low[:, a.b, 2:4, :],
                                         op0=ALU.max, op1=ALU.add).then_inc(S["k_ready"], 1)
                dve.scalar_tensor_tensor(out=q[:, a.b, :, :], in0=qk[:, a.b, 0:2, :], scalar=0.0, in1=low[:, a.b, 0:2, :],
                                         op0=ALU.max, op1=ALU.add).then_inc(S["q_ready"], 1)

            def masked(a):
                for g in range(4):
                    n = a.t * 4 + g
                    dve.wait_ge(S["s_ps"], n + 1)
                    wait(dve, S["o_ps"], n - 1)
                    dve.tensor_tensor(out=sc[:, g % 2, :, :], in0=ps_s[g % 2][:, :].rearrange("p (j m) -> p j m", j=4),
                                      in1=same[:, :, :], op=ALU.mult).then_inc(S["s_ready"], 1)

            def normed(a):
                chain.start(a.t * 2)
                dve.wait_ge(S["o_ps"], a.t * 4 + 4)
                wait(dve, S["yT_ps"], a.t - 1)
                o = ps_o[:, 0:H0 * VW].rearrange("p (h e) -> p h e", h=H0)
                chain.done(dve.tensor_scalar(out=den[:, a.b, :], in0=o[:, :, D0], scalar1=1e-6, scalar2=None, op0=ALU.add))
                chain.done(dve.reciprocal(rden[:, a.b, :], den[:, a.b, :]))
                dve.tensor_tensor(out=y[:, a.b, :].rearrange("p (h e) -> p h e", h=H0), in0=o[:, :, 0:D0],
                                  in1=rden[:, a.b, :].rearrange("p (h a) -> p h a", a=1).broadcast_to([P, H0, D0]),
                                  op=ALU.mult).then_inc(S["y_ready"], 1)
                dve.wait_ge(S["y_ready"], a.t + 1)
                dve.sem_inc(S["o_read"], 1)

            def residual(a):
                dve.wait_ge(S["w_ps"], a.t + 1)
                hs = K.h[:, ds(a.t * D, D)]
                dve.tensor_tensor(out=hs, in0=ps_w[:, 0:D], in1=hs, op=ALU.add).then_inc(S["h_ready"], 1)
                dve.wait_ge(S["h_ready"], a.t + 1)
                dve.tensor_tensor(out=hs, in0=hs, in1=bo[:, :], op=ALU.add).then_inc(S["moved"], 1)
                take_moments(K, dve, a, S["moved"], a.t + 1)

            def step(a):
                centre(a)
                features(a)
                masked(a.at(-1))
                normed(a.at(-1))
                residual(a.at(-2))
            centre(tile(0))
            features(tile(0))
            centre(tile(1))
            features(tile(1))
            masked(tile(0))
            normed(tile(0))
            over(dve, 2, NT, step)
            masked(tile(NT - 1))
            normed(tile(NT - 1))
            residual(tile(NT - 2))
            residual(tile(NT - 1))


def batch_mask(pool, m, width, sem, causal):
    pool.memset(m[:, :, :], 1.0).then_inc(sem, 1)
    pool.wait_ge(sem, 1)
    v = m[:, :, :].rearrange("p a (g s) -> p a g s", s=width)
    G = P // width
    pool.affine_select(out=v, in_=v, compare_op=ALU.is_ge, fill=0.0, base=0,
                       pattern=[[0, 4], [-width, G], [0, width]], channel_multiplier=1).then_inc(sem, 1)
    pool.wait_ge(sem, 2)
    pool.affine_select(out=v, in_=v, compare_op=ALU.is_ge, fill=0.0, base=0 if causal else width - 1,
                       pattern=[[0, 4], [width, G], [1 if causal else 0, width]], channel_multiplier=-1).then_inc(sem, 1)


def head_mask(pool, m, heads, width, sem, n):
    pool.memset(m[:, :], 1.0).then_inc(sem, 1)
    pool.wait_ge(sem, n + 1)
    pool.affine_select(out=m[:, :], in_=m[:, :], compare_op=ALU.is_ge, fill=0.0, base=0,
                       pattern=[[-width, heads]], channel_multiplier=1).then_inc(sem, 1)
    pool.wait_ge(sem, n + 2)
    pool.affine_select(out=m[:, :], in_=m[:, :], compare_op=ALU.is_ge, fill=0.0, base=width - 1,
                       pattern=[[width, heads]], channel_multiplier=-1).then_inc(sem, 1)


def stage_gate(K, name, experts, route, xT, plan=None):
    nc, ins = K.nc, K.ins
    E = experts
    with ExitStack() as ctx:
        sb = lambda n, shape, dt=F32: ctx.enter_context(nc.sbuf_tensor(name + n, shape, dt))
        wg = sb("wg", [P, DC, E])
        bias = sb("bias", [P, E])
        rev = sb("rev", [P, E])
        xn = sb("xn", [P, 2, D])
        xt = sb("xt", [P, 2, D])
        work = {n: sb(n, [P, NT, E]) for n in ("score", "left", "eq", "place", "sel1", "sel2")}
        one = {n: sb(n, [P, NT]) for n in ("top", "last", "sum", "rsum")}
        ps_x = [ctx.enter_context(nc.psum_tensor(f"{name}ps_x{b}", [P, 512], F32)) for b in range(2)]
        ps_g = ctx.enter_context(nc.psum_tensor(name + "ps_g", [P, 512], F32))
        ps_r = ctx.enter_context(nc.psum_tensor(name + "ps_r", [P, 512], F32))
        loaded, rev_set = K.sem(name + "loaded"), K.sem(name + "rev_set")
        norm = norm_sems(K, name)
        S = {n: K.sem(name + n) for n in
             "xn_ready xT_ps xt_ready g_ps kept exp_in exp_ready steps hi_ready lo_ready hiT_ready sel_ready rank_ps".split()}
        if plan:
            plan.allocate(sb)
            plan.sel = work["eq"]
        block = ctx.enter_context(nc.Block())

        @block.sync
        def _(sp):
            with nc.allow_non_contiguous_dma(reason="a gate of 8 columns, once"):
                sp.dma_start(wg[:, :, :], ins[name + "gate"].rearrange("(c p) e -> p c e", p=P)).then_inc(loaded, 16)
            if name + "gate_bias" in ins:
                sp.dma_start(bias[:, :], ins[name + "gate_bias"].partition_broadcast(P)).then_inc(loaded, 16)

        @block.gpsimd
        def _(pool):
            for e in range(E):
                last = pool.memset(rev[:, e:e + 1], float(E - e))
            last.then_inc(rev_set, 1)
            if plan:
                plan.constants(pool)

            def lows(a):
                pool.wait_ge(S["hi_ready"], a.t + 1)
                K.hold(pool)
                row = a.t * 2 * D
                pool.tensor_tensor(out=plan.rows[:, ds(row + D, D)], in0=xn[:, a.b, :], in1=plan.rows[:, ds(row, D)],
                                   op=ALU.subtract).then_inc(S["lo_ready"], 1)
                pool.wait_ge(S["hiT_ready"], a.t + 1)
                K.hold(pool)
                pool.tensor_tensor(out=xT[:, 1, :, ds(a.t * P, P)], in0=xt[:, a.b, :].rearrange("p (c m) -> p c m", c=DC),
                                   in1=xT[:, 0, :, ds(a.t * P, P)], op=ALU.subtract).then_inc(S["kept"], 1)

            def keep(a):
                pool.wait_ge(S["xt_ready"], a.t + 1)
                K.hold(pool)
                src = xt[:, a.b, :].rearrange("p (c m) -> p c m", c=DC)
                pool.tensor_copy(out=xT[:, :, ds(a.t * P, P)], in_=src).then_inc(S["kept"], 1)
            over(pool, 0, NT, lows if plan else keep)

        @block.scalar
        def _(act):
            root_norm(K, act, norm)

            def take(a):
                act.wait_ge(S["xT_ps"], a.t + 1)
                wait(act, S["g_ps"], a.t - 1)
                wait(act, S["kept"], a.t - 1)
                act.activation(xt[:, a.b, :], ps_x[a.b][:, 0:D], ACT.Copy).then_inc(S["xt_ready"], 1)
                if plan:
                    act.activation(xT[:, 0, :, ds(a.t * P, P)], ps_x[a.b][:, 0:D].rearrange("p (c m) -> p c m", c=DC),
                                   ACT.Copy).then_inc(S["hiT_ready"], 1)
            over(act, 0, NT, take)
            act.wait_ge(S["exp_in"], 1)
            act.activation(work["score"][:, :, :], work["score"][:, :, :], ACT.Exp).then_inc(S["exp_ready"], 1)

        @block.tensor
        def _(pe):
            pe.wait_ge(loaded, 16)

            def transposes(a):
                pe.wait_ge(S["xn_ready"], a.t + 1)
                wait(pe, S["hiT_ready" if plan else "xt_ready"], a.t - 1)
                for c in range(DC):
                    last = pe.transpose(ps_x[a.b][:, c * P:(c + 1) * P], xn[:, a.b, c * P:(c + 1) * P], K.ident[:, :])
                last.then_inc(S["xT_ps"], 1)

            def logits(a):
                pe.wait_ge(S["xt_ready"], a.t + 1)
                for c in range(DC):
                    last = pe.matmul(ps_g[:, ds(a.t * E, E)], xt[:, a.b, c * P:(c + 1) * P], wg[:, c, :],
                                     start=(c == 0), stop=(c == DC - 1))
                last.then_inc(S["g_ps"], 1)

            def step(a):
                transposes(a)
                logits(a.at(-1))
            transposes(tile(0))
            over(pe, 1, NT, step)
            logits(tile(NT - 1))
            if plan:
                plan.ranks(pe, ps_r, S)

        @block.vector
        def _(dve):
            chain = Chain(dve, S["steps"])
            prepare_norm(K, dve, norm)
            dve.wait_ge(loaded, 16 * (1 + (name + "gate_bias" in ins)))
            dve.wait_ge(rev_set, 1)

            def centre(a):
                wait(dve, S["xT_ps"], a.t - 1)
                if plan:
                    wait(dve, S["lo_ready"], a.t - 1)
                normalise(K, dve, a, xn[:, a.b, :]).then_inc(S["xn_ready"], 1)
                if plan:
                    dve.wait_ge(S["xn_ready"], a.t + 1)
                    dve.tensor_scalar(out=plan.rows[:, ds(a.t * 2 * D, D)], in0=xn[:, a.b, :], scalar1=1.0, scalar2=None,
                                      op0=ALU.mult).then_inc(S["hi_ready"], 1)
            over(dve, 0, NT, centre)
            dve.wait_ge(S["g_ps"], NT)
            logit = ps_g[:, 0:NT * E].rearrange("p (t e) -> p t e", t=NT)
            route(dve, chain, logit, bias, rev, work, one, S)
            if plan:
                plan.make(dve, chain, work, ps_r, S)


def per_token(m):
    t, e = NT, E0
    return m[:, :].rearrange("p (t a) -> p t a", a=1).broadcast_to([P, t, e])


def top_two(dve, chain, value, rev, work, one):
    left, eq, place = work["left"], work["eq"], work["place"]
    revs = rev[:, :].rearrange("p (a e) -> p a e", a=1).broadcast_to([P, NT, E0])
    for n, sel in enumerate((work["sel1"], work["sel2"])):
        src = value if n == 0 else left
        chain.done(dve.tensor_reduce(out=one["top"][:, :], in_=src[:, :, :], axis=AX, op=ALU.max))
        chain.done(dve.tensor_tensor(out=eq[:, :, :], in0=src[:, :, :], in1=per_token(one["top"]), op=ALU.is_ge))
        chain.done(dve.tensor_tensor(out=place[:, :, :], in0=eq[:, :, :], in1=revs, op=ALU.mult))
        chain.done(dve.tensor_reduce(out=one["last"][:, :], in_=place[:, :, :], axis=AX, op=ALU.max))
        chain.done(dve.tensor_tensor(out=sel[:, :, :], in0=place[:, :, :], in1=per_token(one["last"]), op=ALU.is_equal))
        if n == 0:
            chain.done(dve.scalar_tensor_tensor(out=left[:, :, :], in0=sel[:, :, :], scalar=-1e30, in1=value[:, :, :],
                                                op0=ALU.mult, op1=ALU.add))
    chain.done(dve.tensor_tensor(out=eq[:, :, :], in0=work["sel1"][:, :, :], in1=work["sel2"][:, :, :], op=ALU.add))
    return eq


def route0(gate):
    def route(dve, chain, logit, bias, rev, work, one, S):
        score, left = work["score"], work["sel2"]
        dve.tensor_scalar(out=score[:, :, :], in0=logit, scalar1=-1.0, scalar2=None, op0=ALU.mult).then_inc(S["exp_in"], 1)
        dve.wait_ge(S["exp_ready"], 1)
        chain.done(dve.tensor_scalar(out=left[:, :, :], in0=score[:, :, :], scalar1=1.0, scalar2=None, op0=ALU.add))
        chain.done(dve.reciprocal(score[:, :, :], left[:, :, :]))
        biased = work["left"]
        chain.done(dve.tensor_tensor(out=biased[:, :, :], in0=score[:, :, :],
                                     in1=bias[:, :].rearrange("p (a e) -> p a e", a=1).broadcast_to([P, NT, E0]), op=ALU.add))
        sel = top_two(dve, chain, biased, rev, work, one)
        dve.tensor_tensor(out=gate[:, :, :].rearrange("p e t -> p t e"), in0=score[:, :, :], in1=sel[:, :, :], op=ALU.mult)
    return route


def route1():
    def route(dve, chain, logit, bias, rev, work, one, S):
        score, prob = work["score"], work["left"]
        chain.done(dve.tensor_reduce(out=one["top"][:, :], in_=logit, axis=AX, op=ALU.max))
        dve.tensor_tensor(out=score[:, :, :], in0=logit, in1=per_token(one["top"]), op=ALU.subtract).then_inc(S["exp_in"], 1)
        dve.wait_ge(S["exp_ready"], 1)
        chain.done(dve.tensor_reduce(out=one["sum"][:, :], in_=score[:, :, :], axis=AX, op=ALU.add))
        chain.done(dve.reciprocal(one["rsum"][:, :], one["sum"][:, :]))
        chain.done(dve.tensor_tensor(out=prob[:, :, :], in0=score[:, :, :], in1=per_token(one["rsum"]), op=ALU.mult))
        chain.done(dve.tensor_copy(out=score[:, :, :], in_=prob[:, :, :]))
        sel = top_two(dve, chain, prob, rev, work, one)
        dve.sem_inc(S["sel_ready"], 1)
        chain.done(dve.tensor_tensor(out=work["place"][:, :, :], in0=score[:, :, :], in1=sel[:, :, :], op=ALU.mult))
        chain.done(dve.tensor_reduce(out=one["sum"][:, :], in_=work["place"][:, :, :], axis=AX, op=ALU.add))
        chain.done(dve.reciprocal(one["rsum"][:, :], one["sum"][:, :]))
        chain.done(dve.tensor_tensor(out=prob[:, :, :], in0=work["place"][:, :, :], in1=per_token(one["rsum"]), op=ALU.mult))
    return route


class Plan:

    def __init__(self, nc, ctx, K):
        sb = lambda n, shape, dt=F32: ctx.enter_context(nc.sbuf_tensor("plan_" + n, shape, dt))
        self.rows = sb("rows", [P, NT * 2 * D], BF16)
        self.slot = sb("slot", [P, 2 * NT], mybir.dt.uint32)
        self.weight = sb("weight", [P, 2 * NT])
        self.expert = sb("expert", [P, NB], mybir.dt.int32)
        self.ready = K.sem("plan_constants")

    def allocate(self, sb):
        self.before = sb("before", [P, P])
        self.ones = sb("ones", [P, P])
        self.index = sb("index", [P, NB])
        self.edge = sb("edge", [P, TOK // SB])
        self.total = sb("total", [P, NT, E1])
        self.run = sb("run", [P, NT + 1, E1])
        self.over = sb("over", [P, E1, TOK // SB])
        self.blocks = sb("blocks", [P, E1])
        self.first = sb("first", [P, E1 + 1])
        self.place = sb("place2", [P, NT, E1])
        self.slotf = sb("slotf", [P, 2, NT])
        self.past = sb("past", [P, NB, E1])
        self.expertf = sb("expertf", [P, NB])

    def constants(self, pool):
        pool.memset(self.ones[:, :], 1.0).then_inc(self.ready, 1)
        pool.wait_ge(self.ready, 1)
        pool.affine_select(out=self.before[:, :], in_=self.ones[:, :], compare_op=ALU.is_gt, fill=0.0, base=0,
                           pattern=[[1, P]], channel_multiplier=-1)
        for j in range(NB):
            pool.memset(self.index[:, j:j + 1], float(j))
        for j in range(TOK // SB):
            last = pool.memset(self.edge[:, j:j + 1], float(j * SB))
        last.then_inc(self.ready, 1)

    def ranks(self, pe, ps_r, S):
        pe.wait_ge(self.ready, 2)
        pe.wait_ge(S["sel_ready"], 1)
        sel = self.sel[:, :, :].rearrange("p t e -> p (t e)")
        pe.matmul(ps_r[:, 0:NT * E1], self.before[:, :], sel, start=True, stop=True)
        pe.matmul(ps_r[:, NT * E1:2 * NT * E1], self.ones[:, :], sel, start=True, stop=True).then_inc(S["rank_ps"], 1)

    def make(self, dve, chain, work, ps_r, S):
        dve.wait_ge(S["rank_ps"], 1)
        dve.wait_ge(self.ready, 2)
        rank = ps_r[:, 0:NT * E1].rearrange("p (t e) -> p t e", t=NT)
        chain.done(dve.tensor_copy(out=self.total[:, :, :], in_=ps_r[:, NT * E1:2 * NT * E1].rearrange("p (t e) -> p t e", t=NT)))
        chain.done(dve.memset(self.run[:, 0, :], 0.0))
        for t in range(NT):
            chain.done(dve.tensor_tensor(out=self.run[:, t + 1, :], in0=self.run[:, t, :], in1=self.total[:, t, :], op=ALU.add))
        J = TOK // SB
        chain.done(dve.tensor_tensor(out=self.over[:, :, :], in0=self.run[:, NT, :].rearrange("p (e a) -> p e a", a=1).broadcast_to([P, E1, J]),
                                     in1=self.edge[:, :].rearrange("p (a j) -> p a j", a=1).broadcast_to([P, E1, J]), op=ALU.is_gt))
        chain.done(dve.tensor_reduce(out=self.blocks[:, :], in_=self.over[:, :, :], axis=AX, op=ALU.add))
        chain.done(dve.memset(self.first[:, 0:1], 0.0))
        for e in range(E1):
            chain.done(dve.tensor_tensor(out=self.first[:, e + 1:e + 2], in0=self.first[:, e:e + 1], in1=self.blocks[:, e:e + 1], op=ALU.add))
        firsts = self.first[:, 0:E1].rearrange("p (a e) -> p a e", a=1).broadcast_to([P, NT, E1])
        chain.done(dve.scalar_tensor_tensor(out=self.place[:, :, :], in0=firsts, scalar=float(SB), in1=self.run[:, 0:NT, :],
                                            op0=ALU.mult, op1=ALU.add))
        chain.done(dve.tensor_tensor(out=self.place[:, :, :], in0=rank, in1=self.place[:, :, :], op=ALU.add))
        for k, sel in enumerate((work["sel1"], work["sel2"])):
            chain.done(dve.tensor_tensor(out=work["place"][:, :, :], in0=sel[:, :, :], in1=self.place[:, :, :], op=ALU.mult))
            chain.done(dve.tensor_reduce(out=self.slotf[:, k, :], in_=work["place"][:, :, :], axis=AX, op=ALU.add))
            chain.done(dve.tensor_tensor(out=work["place"][:, :, :], in0=sel[:, :, :], in1=work["left"][:, :, :], op=ALU.mult))
            chain.done(dve.tensor_reduce(out=self.weight[:, k * NT:(k + 1) * NT], in_=work["place"][:, :, :], axis=AX, op=ALU.add))
        dve.tensor_copy(out=self.slot[:, :], in_=self.slotf[:, :, :].rearrange("p k t -> p (k t)"))
        chain.done(dve.tensor_tensor(out=self.past[:, :, :], in0=self.index[:, :].rearrange("p (n a) -> p n a", a=1).broadcast_to([P, NB, E1]),
                                     in1=self.first[:, 1:E1 + 1].rearrange("p (a e) -> p a e", a=1).broadcast_to([P, NB, E1]), op=ALU.is_ge))
        chain.done(dve.tensor_reduce(out=self.expertf[:, :], in_=self.past[:, :, :], axis=AX, op=ALU.add))
        dve.tensor_scalar(out=self.expert[:, :], in0=self.expertf[:, :], scalar1=float(E1 - 1), scalar2=None, op0=ALU.min)


def stage_experts0(K, xT, gate):
    nc, ins = K.nc, K.ins
    HB = chunks(HID0)
    NH = len(HB)
    NO = TPG // 2
    with ExitStack() as ctx:
        sb = lambda n, shape, dt=F32: ctx.enter_context(nc.sbuf_tensor("e_" + n, shape, dt))
        wu_f, wd_f = sb("wu_f", [P, 2, DC, HID0]), sb("wd_f", [P, 2, NH, D])
        wu, wd = sb("wu", [P, 2, DC, HID0], BF16), sb("wd", [P, 2, NH, D], BF16)
        gT = sb("gT", [P, P])
        grow = sb("grow", [P, 2, TOK])
        xe = sb("xe", [P, 2, DC, GT], BF16)
        pos = sb("pos", [P, 4, GT], BF16)
        hid = sb("hid", [P, 2, NH, GT], BF16)
        rnd = sb("rnd", [P, 4, 2 * D], BF16)
        ps = lambda n: ctx.enter_context(nc.psum_tensor("e_" + n, [P, 512], F32))
        ps_u = [ps(f"u{b}") for b in range(4)]
        ps_d = [ps(f"d{b}") for b in range(4)]
        gates = nc.dram_tensor("gates", (E0, TOK), F32).ap()
        loaded = [K.sem(f"e_loaded{b}") for b in range(2)]
        grow_loaded = [K.sem(f"e_grow_loaded{b}") for b in range(2)]
        S = {n: K.sem("e_" + n) for n in
             "gT_ps gT_ready gates_stored cast_up cast xe_ready up_ps relu_ready hid_ready down_ps rnd_ready added".split()}
        block = ctx.enter_context(nc.Block())

        def units(eng, step):
            over(eng, 0, E0 * NG, step, per=2 * NG)

        @block.sync
        def _(sp):
            sp.wait_ge(S["gT_ready"], 1)
            sp.dma_start(gates.rearrange("e (t m) -> (e t) m", t=NT), gT[:, :]).then_inc(S["gates_stored"], 16)
            sp.wait_ge(S["gates_stored"], 16)

            def load(e):
                wait(sp, S["xe_ready"], (e.t - 1) * NG)
                sp.dma_start(grow[:, e.b, :], gates[ds(e.t, 1), :].rearrange("a m -> (a m)").partition_broadcast(P)).then_inc(grow_loaded[e.b], 16)
                wait(sp, S["cast"], e.t - 1)
                last = HB[-1][1]
                for dst, src in ((wu_f[:, e.b, :, :], ins["f0_up"][ds(e.t * D, D), :].rearrange("(c p) n -> p c n", p=P)),
                                 (wd_f[:, e.b, 0:NH - 1, :], ins["f0_down"][ds(e.t * HID0, (NH - 1) * P), :].rearrange("(c p) n -> p c n", p=P)),
                                 (wd_f[0:last, e.b, NH - 1, :], ins["f0_down"][ds(e.t * HID0 + (NH - 1) * P, last), :])):
                    sp.dma_start(dst, src).then_inc(loaded[e.b], 16)
            over(sp, 0, E0, load)

        @block.gpsimd
        def _(pool):
            def step(n):
                eb, g = n.k // NG, n.k % NG
                if g == 0:
                    pool.wait_ge(loaded[eb], n.turn * 48 + 48)
                    wait(pool, S["down_ps"], (n.t - NG) * NO)
                    K.hold(pool)
                    last = HB[-1][1]
                    pool.tensor_copy(out=wu[:, eb, :, :], in_=wu_f[:, eb, :, :]).then_inc(S["cast_up"], 1)
                    pool.tensor_copy(out=wd[:, eb, 0:NH - 1, :], in_=wd_f[:, eb, 0:NH - 1, :])
                    pool.tensor_copy(out=wd[0:last, eb, NH - 1, :], in_=wd_f[0:last, eb, NH - 1, :]).then_inc(S["cast"], 1)
                if not (isinstance(n.t, int) and n.t == 0):
                    add(n.at(-1))

            def add(n):
                g = n.k % NG
                for j in range(NO):
                    q, t = n.t * NO + j, g * TPG + 2 * j
                    pool.wait_ge(S["rnd_ready"], q + 1)
                    wait(pool, S["added"], q - NG * NO + 1)
                    hs = K.h[:, t * D:(t + 2) * D]
                    pool.tensor_tensor(out=hs, in0=hs, in1=rnd[:, (n.k * NO + j) % 4, :], op=ALU.add).then_inc(S["added"], 1)
            units(pool, step)
            add(tile(E0 * NG - 1, 2 * NG))

        @block.tensor
        def _(pe):
            pe.transpose(ps_d[0][:, 0:P], gate[:, :, :].rearrange("p e t -> p (e t)"), K.ident[:, :]).then_inc(S["gT_ps"], 1)

            def up(n):
                eb, g = n.k // NG, n.k % NG
                if g == 0:
                    pe.wait_ge(S["cast_up"], n.turn * 2 + eb + 1)
                pe.wait_ge(S["xe_ready"], n.t + 1)
                for c, (m, w) in enumerate(HB):
                    q = n.t * NH + c
                    wait(pe, S["relu_ready"], q - 3)
                    for kc in range(DC):
                        last = pe.matmul(ps_u[(n.k * NH + c) % 4][0:w, :], wu[:, eb, kc, m * P:m * P + w], xe[:, n.b, kc, :],
                                         start=(kc == 0), stop=(kc == DC - 1))
                    last.then_inc(S["up_ps"], 1)

            def down(n):
                eb, g = n.k // NG, n.k % NG
                if g == 0:
                    pe.wait_ge(S["cast"], n.turn * 2 + eb + 1)
                pe.wait_ge(S["hid_ready"], n.t * NH + NH)
                for j in range(NO):
                    wait(pe, S["rnd_ready"], n.t * NO + j - 3)
                    for i in range(2):
                        for c, (m, w) in enumerate(HB):
                            last = pe.matmul(ps_d[(n.k * NO + j) % 4][:, i * D:(i + 1) * D],
                                             hid[0:w, n.b, c, (2 * j + i) * P:(2 * j + i + 1) * P], wd[0:w, eb, c, :],
                                             start=(c == 0), stop=(c == NH - 1))
                    last.then_inc(S["down_ps"], 1)

            def step(n):
                up(n)
                if not (isinstance(n.t, int) and n.t == 0):
                    down(n.at(-1))
            units(pe, step)
            down(tile(E0 * NG - 1, 2 * NG))

        @block.scalar
        def _(act):
            act.wait_ge(S["gT_ps"], 1)
            act.activation(gT[:, :], ps_d[0][:, 0:P], ACT.Copy).then_inc(S["gT_ready"], 1)

            def relus(n):
                for c, (m, w) in enumerate(HB):
                    q, slot = n.t * NH + c, (n.k * NH + c) % 4
                    act.wait_ge(S["up_ps"], q + 1)
                    wait(act, S["hid_ready"], q - 3)
                    act.activation(pos[0:w, slot, :], ps_u[slot][0:w, :], ACT.Relu).then_inc(S["relu_ready"], 1)

            def rounds(n):
                for j in range(NO):
                    q, slot = n.t * NO + j, (n.k * NO + j) % 4
                    act.wait_ge(S["down_ps"], q + 1)
                    wait(act, S["added"], q - 3)
                    act.activation(rnd[:, slot, :], ps_d[slot][:, :], ACT.Copy).then_inc(S["rnd_ready"], 1)

            def step(n):
                relus(n)
                if not (isinstance(n.t, int) and n.t == 0):
                    rounds(n.at(-1))
            units(act, step)
            rounds(tile(E0 * NG - 1, 2 * NG))

        @block.vector
        def _(dve):
            def scale(n):
                eb, g = n.k // NG, n.k % NG
                if g == 0:
                    dve.wait_ge(grow_loaded[eb], n.turn * 16 + 16)
                wait(dve, S["up_ps"], (n.t - 1) * NH)
                dve.tensor_tensor(out=xe[:, n.b, :, :], in0=xT[:, :, g * GT:(g + 1) * GT],
                                  in1=grow[:, eb:eb + 1, g * GT:(g + 1) * GT].broadcast_to([P, DC, GT]),
                                  op=ALU.mult).then_inc(S["xe_ready"], 1)

            def square(n):
                for c, (m, w) in enumerate(HB):
                    q, slot = n.t * NH + c, (n.k * NH + c) % 4
                    dve.wait_ge(S["relu_ready"], q + 1)
                    if c == 0:
                        wait(dve, S["down_ps"], (n.t - 1) * NO)
                    dve.tensor_tensor(out=hid[0:w, n.b, c, :], in0=pos[0:w, slot, :], in1=pos[0:w, slot, :],
                                      op=ALU.mult).then_inc(S["hid_ready"], 1)

            def step(n):
                scale(n)
                if not (isinstance(n.t, int) and n.t == 0):
                    square(n.at(-1))
            units(dve, step)
            square(tile(E0 * NG - 1, 2 * NG))


def stage_shared0(K, xT):
    nc, ins = K.nc, K.ins
    HB = chunks(HID0)
    NH = len(HB)
    with ExitStack() as ctx:
        sb = lambda n, shape, dt=F32: ctx.enter_context(nc.sbuf_tensor("s_" + n, shape, dt))
        wu, wd = sb("wu", [P, DC, HID0]), sb("wd", [P, NH, D])
        pos = sb("pos", [P, 4, GT])
        hid = sb("hid", [P, 2, NH, GT])
        ps = lambda n: ctx.enter_context(nc.psum_tensor("s_" + n, [P, 512], F32))
        ps_u = [ps(f"u{b}") for b in range(4)]
        ps_d = [ps(f"d{b}") for b in range(TPG)]
        S = {n: K.sem("s_" + n) for n in "loaded up_ps relu_ready hid_ready down_ps added".split()}
        block = ctx.enter_context(nc.Block())

        @block.sync
        def _(sp):
            last = HB[-1][1]
            sp.dma_start(wu[:, :, :], ins["f0_shared_up"].rearrange("(c p) n -> p c n", p=P)).then_inc(S["loaded"], 16)
            sp.dma_start(wd[:, 0:NH - 1, :], ins["f0_shared_down"][0:(NH - 1) * P, :].rearrange("(c p) n -> p c n", p=P)).then_inc(S["loaded"], 16)
            sp.dma_start(wd[0:last, NH - 1, :], ins["f0_shared_down"][(NH - 1) * P:HID0, :]).then_inc(S["loaded"], 16)

        @block.tensor
        def _(pe):
            pe.wait_ge(S["loaded"], 48)

            def up(g):
                for c, (m, w) in enumerate(HB):
                    q = g * NH + c
                    wait(pe, S["relu_ready"], q - 3)
                    for kc in range(DC):
                        last = pe.matmul(ps_u[q % 4][0:w, :], wu[:, kc, m * P:m * P + w], xT[:, kc, g * GT:(g + 1) * GT],
                                         start=(kc == 0), stop=(kc == DC - 1))
                    last.then_inc(S["up_ps"], 1)

            def down(g):
                pe.wait_ge(S["hid_ready"], g * NH + NH)
                for j in range(TPG):
                    wait(pe, S["added"], g * TPG + j - 3)
                    for c, (m, w) in enumerate(HB):
                        last = pe.matmul(ps_d[j][:, 0:D], hid[0:w, g % 2, c, j * P:(j + 1) * P], wd[0:w, c, :],
                                         start=(c == 0), stop=(c == NH - 1))
                    last.then_inc(S["down_ps"], 1)
            up(0)
            for g in range(1, NG):
                up(g)
                down(g - 1)
            down(NG - 1)

        @block.scalar
        def _(act):
            for g in range(NG):
                for c, (m, w) in enumerate(HB):
                    q = g * NH + c
                    act.wait_ge(S["up_ps"], q + 1)
                    wait(act, S["hid_ready"], q - 3)
                    act.activation(pos[0:w, q % 4, :], ps_u[q % 4][0:w, :], ACT.Relu).then_inc(S["relu_ready"], 1)

        @block.vector
        def _(dve):
            def square(g):
                for c, (m, w) in enumerate(HB):
                    q = g * NH + c
                    dve.wait_ge(S["relu_ready"], q + 1)
                    if c == 0:
                        wait(dve, S["down_ps"], (g - 1) * TPG)
                    dve.tensor_tensor(out=hid[0:w, g % 2, c, :], in0=pos[0:w, q % 4, :], in1=pos[0:w, q % 4, :],
                                      op=ALU.mult).then_inc(S["hid_ready"], 1)

            def add(g):
                for j in range(TPG):
                    t = g * TPG + j
                    dve.wait_ge(S["down_ps"], t + 1)
                    hs = K.h[:, t * D:(t + 1) * D]
                    dve.tensor_tensor(out=hs, in0=ps_d[j][:, 0:D], in1=hs, op=ALU.add).then_inc(S["added"], 1)
                    dve.wait_ge(S["added"], t + 1)
                    dve.bn_stats(out=K.moments[:, t * 6:t * 6 + 6], in_=hs)
            square(0)
            for g in range(1, NG):
                square(g)
                add(g - 1)
            add(NG - 1)


def stage_fused_weights(K, wf):
    nc, ins = K.nc, K.ins
    with ExitStack() as ctx:
        sb = lambda n, shape, dt=F32: ctx.enter_context(nc.sbuf_tensor("w_" + n, shape, dt))
        wT = sb("wT", [D1, 2, H1, D])
        kk = sb("kk", [D1, 2, H1, F1])
        ps = [ctx.enter_context(nc.psum_tensor(f"w_ps{b}", [P, 512], F32)) for b in range(2)]
        loaded, ps_ready, read = K.sem("w_loaded"), K.sem("w_ps_ready"), K.sem("w_read")
        block = ctx.enter_context(nc.Block())
        HB = 512 // F1
        banks = [(j, c, hb) for j in range(2) for c in range(DC) for hb in range(H1 // HB)]

        @block.sync
        def _(sp):
            for j, n in enumerate("qk"):
                sp.dma_start(wT[:, j, :, :], ins[f"a1_w{n}T"].rearrange("(h p) d -> p h d", p=D1)).then_inc(loaded, 16)
                sp.dma_start(kk[:, j, :, :], ins[f"a1_k{n}"].rearrange("h p f -> p h f")).then_inc(loaded, 16)

        @block.tensor
        def _(pe):
            pe.wait_ge(loaded, 64)
            for n, (j, c, hb) in enumerate(banks):
                wait(pe, read, n - 1)
                for i in range(HB):
                    hd = hb * HB + i
                    last = pe.matmul(ps[n % 2][:, i * F1:(i + 1) * F1], wT[:, j, hd, c * P:(c + 1) * P], kk[:, j, hd, :],
                                     start=True, stop=True)
                last.then_inc(ps_ready, 1)

        @block.scalar
        def _(act):
            for n, (j, c, hb) in enumerate(banks):
                act.wait_ge(ps_ready, n + 1)
                act.activation(wf[:, j, c, hb * 512:(hb + 1) * 512], ps[n % 2][:, :], ACT.Copy).then_inc(read, 1)


def stage_attention1(K, wf):
    nc, ins = K.nc, K.ins
    W = H1 * D1
    VW = D1 + 1
    FT = 2 * F1
    G, HG = 4, 4
    YC = W // P
    with ExitStack() as ctx:
        sb = lambda n, shape, dt=F32: ctx.enter_context(nc.sbuf_tensor("b_" + n, shape, dt))
        wv, wo = sb("wv", [P, DC, W]), sb("wo", [P, YC, D])
        causal = sb("causal", [P, 4, P])
        xn, xT = sb("xn", [P, 2, D]), sb("xT", [P, 2, D])
        feat = sb("feat", [P, 4, H1, 2, F1])
        ext = sb("ext", [P, 4, 2, H1])
        fsum = sb("fsum", [P, 4, H1 * 2])
        frec = sb("frec", [P, 4, H1 * 2])
        v = sb("v", [P, 2, H1, VW])
        fT = sb("fT", [P, 2, 2, HG, P])
        sc = sb("sc", [P, 2, HG, P])
        den, rden = sb("den", [P, 2, HG]), sb("rden", [P, 2, HG])
        y, yT = sb("y", [P, 2, W]), sb("yT", [P, 2, W])
        ps = lambda n: ctx.enter_context(nc.psum_tensor("b_ps_" + n, [P, 512], F32))
        ps_f = [ctx.enter_context(nc.psum_tensor(f"b_ps_f{b}", [P, 1024], F32)) for b in range(2)]
        ps_t = [ps(f"t{b}") for b in range(2)]
        ps_s, ps_o = ps("s"), ps("o")
        loaded, mask, ones_set = K.sem("b_loaded"), K.sem("b_mask"), K.sem("b_ones_set")
        norm = norm_sems(K, "b")
        names = ("xn_ready f_ps f_read ext_ready shift_ready exp_ready rec_ready mul_ready feat_ready v_ready "
                 "t_ps t_read s_ps s_ready o_ps o_read y_ready w_ps h_ready steps").split()
        S = {n: K.sem("b_" + n) for n in names}
        block = ctx.enter_context(nc.Block())
        TPT = 1 + 2 + 2 * G

        @block.sync
        def _(sp):
            sp.dma_start(wv[:, :, :], ins["a1_wv"].rearrange("(c p) n -> p c n", p=P)).then_inc(loaded, 16)
            sp.dma_start(wo[:, :, :], ins["a1_wo"].rearrange("(c p) n -> p c n", p=P)).then_inc(loaded, 16)

        def use(a, slot):
            n = a.t * TPT - 12 + slot + 1
            if isinstance(n, int):
                if a.t < 2:
                    n = 1 if a.t == 0 else 2 + max(slot - 2, 0)
                elif a.t >= NT:
                    n -= a.t - NT + 1
                return n, (n - 1) % 2
            return n, (a.k + slot) % 2

        use_x = lambda a: use(a, 0)
        use_y = lambda a, j: use(a.at(2), 1 + j)
        use_f = lambda a, g, j: use(a.at(1), 3 + 2 * g + j)

        @block.gpsimd
        def _(pool):
            batch_mask(pool, causal, NPOS, mask, causal=True)
            pool.memset(v[:, :, :, D1:VW], 1.0).then_inc(ones_set, 1)

            def scale(a):
                for j in range(2):
                    s = a.b * 2 + j
                    pool.wait_ge(S["rec_ready"], a.t * 2 + j + 1)
                    f = feat[:, s, :, :, :].rearrange("p h s f -> p (h s) f")
                    pool.tensor_tensor(out=f, in0=f, in1=frec[:, s, :].rearrange("p (h a) -> p h a", a=1).broadcast_to([P, 2 * H1, F1]),
                                       op=ALU.mult).then_inc(S["mul_ready"], 1)
            over(pool, 0, NT, scale)

        def passes(eng, front, attend, back):
            front(tile(0))
            eng_pass = lambda a: (front(a), back(a.at(-2)), attend(a.at(-1)))
            front(tile(1))
            attend(tile(0))
            over(eng, 2, NT, eng_pass)
            back(tile(NT - 2))
            attend(tile(NT - 1))
            back(tile(NT - 1))

        @block.scalar
        def _(act):
            root_norm(K, act, norm)

            def front(a):
                n, b = use_x(a)
                act.wait_ge(S["t_ps"], use_x(a)[0])
                wait(act, S["f_ps"], (a.t - 1) * 3)
                act.activation(xT[:, a.b, :], ps_t[b][:, 0:D], ACT.Copy).then_inc(S["t_read"], 1)
                for j in range(2):
                    s = a.b * 2 + j
                    act.wait_ge(S["shift_ready"], a.t * 2 + j + 1)
                    act.activation(feat[:, s, :, :, :], feat[:, s, :, :, :], ACT.Exp).then_inc(S["exp_ready"], 1)
                act.wait_ge(S["f_ps"], a.t * 3 + 3)
                wait(act, S["o_ps"], (a.t - 1) * G)
                act.activation(v[:, a.b, :, 0:D1], ps_f[(a.k * 3 + 2) % 2][:, :].rearrange("p (h e) -> p h e", h=H1),
                               ACT.Copy).then_inc(S["v_ready"], 1)

            def attend(a):
                for g in range(G):
                    for j in range(2):
                        n, b = use_f(a, g, j)
                        act.wait_ge(S["t_ps"], use_f(a, g, j)[0])
                        wait(act, S["s_ps"], a.t * G + g - 1)
                        act.activation(fT[:, g % 2, j, :, :], ps_t[b][:, :].rearrange("p (h m) -> p h m", h=HG),
                                       ACT.Copy).then_inc(S["t_read"], 1)

            def back(a):
                for j in range(2):
                    n, b = use_y(a, j)
                    act.wait_ge(S["t_ps"], use_y(a, j)[0])
                    wait(act, S["w_ps"], a.t - 1)
                    act.activation(yT[:, a.b, j * 512:(j + 1) * 512], ps_t[b][:, :], ACT.Copy).then_inc(S["t_read"], 1)
            passes(act, front, attend, back)

        @block.tensor
        def _(pe):
            pe.wait_ge(loaded, 32)

            def free_t(count):
                wait(pe, S["t_read"], count - 2)

            def front(a):
                n, b = use_x(a)
                pe.wait_ge(S["xn_ready"], a.t + 1)
                free_t(use_x(a)[0])
                for c in range(DC):
                    last = pe.transpose(ps_t[b][:, c * P:(c + 1) * P], xn[:, a.b, c * P:(c + 1) * P], K.ident[:, :])
                last.then_inc(S["t_ps"], 1)
                pe.wait_ge(S["t_read"], use_x(a)[0])
                for j in range(3):
                    q = a.t * 3 + j
                    if j == 2:
                        pe.wait_ge(S["f_read"], a.t * 2 + 1)
                    elif j == 0:
                        wait(pe, S["f_read"], a.t * 2)
                    else:
                        wait(pe, S["v_ready"], a.t)
                    out = ps_f[(a.k * 3 + j) % 2]
                    for half in range(2):
                        for c in range(DC):
                            rhs = wv[:, c, half * 512:(half + 1) * 512] if j == 2 else wf[:, j, c, half * 512:(half + 1) * 512]
                            last = pe.matmul(out[:, half * 512:(half + 1) * 512], xT[:, a.b, c * P:(c + 1) * P], rhs,
                                             start=(c == 0), stop=(c == DC - 1))
                    last.then_inc(S["f_ps"], 1)

            def features(a, g):
                for j in range(2):
                    n, b = use_f(a, g, j)
                    free_t(use_f(a, g, j)[0])
                    for i in range(HG):
                        last = pe.transpose(ps_t[b][:, i * P:(i + 1) * P],
                                            feat[:, a.b * 2 + j, g * HG + i, :, :].rearrange("p s f -> p (s f)"), K.ident[:, :])
                    last.then_inc(S["t_ps"], 1)

            def scores(a, g):
                pe.wait_ge(S["t_read"], use_f(a, g, 1)[0])
                wait(pe, S["s_ready"], a.t * G + g)
                for i in range(HG):
                    last = pe.matmul(ps_s[:, i * P:(i + 1) * P], fT[:, g % 2, 1, i, :], fT[:, g % 2, 0, i, :], start=True, stop=True)
                last.then_inc(S["s_ps"], 1)

            def values(a, g):
                pe.wait_ge(S["s_ready"], a.t * G + g + 1)
                wait(pe, S["o_read"], a.t * G + g)
                if g == 0:
                    wait(pe, S["h_ready"], a.t - 1)
                for i in range(HG):
                    last = pe.matmul(ps_o[:, i * VW:(i + 1) * VW], sc[:, g % 2, i, :], v[:, a.b, g * HG + i, :], start=True, stop=True)
                last.then_inc(S["o_ps"], 1)

            def attend(a):
                pe.wait_ge(S["feat_ready"], a.t * 2 + 2)
                pe.wait_ge(S["v_ready"], a.t + 1)
                features(a, 0)
                for g in range(G):
                    if g + 1 < G:
                        features(a, g + 1)
                    scores(a, g)
                    if g:
                        values(a, g - 1)
                values(a, G - 1)

            def back(a):
                pe.wait_ge(S["y_ready"], a.t * G + G)
                for j in range(2):
                    n, b = use_y(a, j)
                    free_t(use_y(a, j)[0])
                    for i in range(4):
                        last = pe.transpose(ps_t[b][:, i * P:(i + 1) * P], y[:, a.b, (j * 4 + i) * P:(j * 4 + i + 1) * P], K.ident[:, :])
                    last.then_inc(S["t_ps"], 1)
                pe.wait_ge(S["t_read"], use_y(a, 1)[0])
                for c in range(YC):
                    last = pe.matmul(ps_o[:, 0:D], yT[:, a.b, c * P:(c + 1) * P], wo[:, c, :], start=(c == 0), stop=(c == YC - 1))
                last.then_inc(S["w_ps"], 1)
            passes(pe, front, attend, back)

        @block.vector
        def _(dve):
            chain = Chain(dve, S["steps"])
            prepare_norm(K, dve, norm)
            dve.wait_ge(mask, 3)
            dve.wait_ge(ones_set, 1)
            PER = 1 + 2 * G

            def front(a):
                wait(dve, S["f_ps"], (a.t - 1) * 3)
                normalise(K, dve, a, xn[:, a.b, :]).then_inc(S["xn_ready"], 1)
                for j in range(2):
                    s, n = a.b * 2 + j, a.t * 2 + j
                    f = ps_f[(a.k * 3 + j) % 2][:, :].rearrange("p (h f) -> p h f", h=H1)
                    bc = lambda m: ext[:, s, m, :].rearrange("p (h a) -> p h a", a=1).broadcast_to([P, H1, F1])
                    dve.wait_ge(S["f_ps"], a.t * 3 + j + 1)
                    dve.tensor_reduce(out=ext[:, s, 0, :], in_=f, axis=AX, op=ALU.max)
                    dve.tensor_reduce(out=ext[:, s, 1, :], in_=f, axis=AX, op=ALU.min).then_inc(S["ext_ready"], 1)
                    dve.wait_ge(S["ext_ready"], n + 1)
                    wait(dve, S["s_ps"], (a.t - 1) * G)
                    dve.tensor_tensor(out=feat[:, s, :, 0, :], in0=f, in1=bc(0), op=ALU.subtract)
                    dve.tensor_tensor(out=feat[:, s, :, 1, :], in0=bc(1), in1=f, op=ALU.subtract).then_inc(S["shift_ready"], 1)
                    dve.wait_ge(S["shift_ready"], n + 1)
                    dve.sem_inc(S["f_read"], 1)
                for j in range(2):
                    s, n = a.b * 2 + j, a.t * 2 + j
                    dve.wait_ge(S["exp_ready"], n + 1)
                    chain.start(a.t * 2 + j)
                    chain.done(dve.tensor_reduce(out=fsum[:, s, :], in_=feat[:, s, :, :, :].rearrange("p h s f -> p (h s) f"), axis=AX, op=ALU.add))
                    dve.reciprocal(frec[:, s, :], fsum[:, s, :]).then_inc(S["rec_ready"], 1)
                for j in range(2):
                    s, n = a.b * 2 + j, a.t * 2 + j
                    dve.wait_ge(S["mul_ready"], n + 1)
                    f = feat[:, s, :, :, :]
                    dve.tensor_scalar(out=f, in0=f, scalar1=FEAT_EPS, scalar2=None, op0=ALU.max).then_inc(S["feat_ready"], 1)

            chain2 = Chain(dve, K.sem("b_steps2"))

            def masked(a, g):
                n = a.t * G + g
                dve.wait_ge(S["s_ps"], n + 1)
                wait(dve, S["o_ps"], n - 1)
                dve.tensor_tensor(out=sc[:, g % 2, :, :], in0=ps_s[:, :].rearrange("p (h m) -> p h m", h=HG), in1=causal[:, :, :],
                                  op=ALU.mult).then_inc(S["s_ready"], 1)

            def normed(a, g):
                n = a.t * G + g
                dve.wait_ge(S["o_ps"], n + 1)
                if g == 0:
                    wait(dve, S["w_ps"], a.t - 1)
                o = ps_o[:, 0:HG * VW].rearrange("p (h e) -> p h e", h=HG)
                chain2.start(n * 2)
                chain2.done(dve.tensor_scalar(out=den[:, g % 2, :], in0=o[:, :, D1], scalar1=FEAT_EPS, scalar2=None, op0=ALU.add))
                chain2.done(dve.reciprocal(rden[:, g % 2, :], den[:, g % 2, :]))
                dve.tensor_tensor(out=y[:, a.b, g * HG * D1:(g + 1) * HG * D1].rearrange("p (h e) -> p h e", h=HG), in0=o[:, :, 0:D1],
                                  in1=rden[:, g % 2, :].rearrange("p (h a) -> p h a", a=1).broadcast_to([P, HG, D1]),
                                  op=ALU.mult).then_inc(S["y_ready"], 1)
                dve.wait_ge(S["y_ready"], n + 1)
                dve.sem_inc(S["o_read"], 1)

            def attend(a):
                masked(a, 0)
                for g in range(1, G):
                    masked(a, g)
                    normed(a, g - 1)
                normed(a, G - 1)

            def back(a):
                dve.wait_ge(S["w_ps"], a.t + 1)
                hs = K.h[:, ds(a.t * D, D)]
                dve.tensor_tensor(out=hs, in0=ps_o[:, 0:D], in1=hs, op=ALU.add).then_inc(S["h_ready"], 1)
                take_moments(K, dve, a, S["h_ready"], a.t + 1)
            passes(dve, front, attend, back)


def stage_clear_slots(K, slots):
    nc = K.nc
    with ExitStack() as ctx:
        zero = ctx.enter_context(nc.sbuf_tensor("zero", [P, 2 * D], BF16))
        zeroed, cleared = K.sem("z_zeroed"), K.slots_cleared
        block = ctx.enter_context(nc.Block())

        @block.gpsimd
        def _(pool):
            pool.memset(zero[:, :], 0.0).then_inc(zeroed, 1)

        @block.sync
        def _(sp):
            sp.wait_ge(zeroed, 1)
            sp.dma_start(slots.rearrange("(n p) m -> p n m", p=P),
                         zero[:, :].rearrange("p (a m) -> p a m", a=1).broadcast_to([P, NB * SB // P, 2 * D])).then_inc(cleared, 16)
            sp.wait_ge(cleared, 16)


def stage_experts1(K, xT, plan, slots):
    nc, ins = K.nc, K.ins
    U = TOK // SB
    HU = U // 2
    N = U + NB
    assert HU % 2 == 0
    NH = HF1 + 1
    TU = SB // P
    WD = HF1 * D
    WT = W1 + WD + D
    with ExitStack() as ctx:
        sb = lambda n, shape, dt=F32: ctx.enter_context(nc.sbuf_tensor("g_" + n, shape, dt))
        wf = sb("wf", [P, 2, WT])
        wb = sb("wb", [P, 3, 2, WT], BF16)
        xr = sb("xr", [P, 2, TU, 2 * D], BF16)
        xg = sb("xg", [P, 2, 2, DC, SB], BF16)
        silu = sb("silu", [P, 2, SB])
        hf = sb("hf", [P, 2, NH, SB])
        hb = sb("hb", [P, 2, 2, NH, SB], BF16)
        y = sb("y", [P, 2, TU * D])
        fetched = sb("fetched", [P, 2, 2, D])
        ps = lambda n, dt=F32: ctx.enter_context(nc.psum_tensor("g_" + n, [P, 2048 // mybir.dt.size(dt)], dt))
        ps_u = [ps(f"u{b}") for b in range(4)]
        ps_d = [ps(f"d{b}") for b in range(2)]
        ps_t = [ps(f"t{b}", BF16) for b in range(2)]
        outs = nc.dram_tensor("expert_outputs", (NB * SB, D), F32).ap()
        identb = sb("identb", [P, P], BF16)
        wf_loaded = [K.sem(f"g_wf_loaded{b}") for b in range(2)]
        xr_loaded = [K.sem(f"g_xr_loaded{b}") for b in range(2)]
        got = [K.sem(f"g_got{b}") for b in range(2)]
        y_stored = [K.sem(f"g_y_stored{b}") for b in range(2)]
        S = {n: K.sem("g_" + n) for n in
             ("identb_ready sent w_high w_high2 w_low w_low2 t_ps xg_ready up_ps silu_ready hf_ready hb_high hb_low down_ps "
              "y_ready combined1 combined").split()}
        block = ctx.enter_context(nc.Block())

        def base_unit(n):
            return n if n < HU else n - NB

        def blocks(eng, step):
            over(eng, HU, HU + NB, step, peel=HU + 4)

        def load_weights(eng, row, s, sem):
            eng.dma_start(wf[:, s, 0:W1], ins["f1_up"][row[0], :]).then_inc(sem, 16)
            eng.dma_start(wf[:, s, W1:W1 + WD], ins["f1_down"][row[0], :]).then_inc(sem, 16)
            eng.dma_start(wf[0:HT1, s, W1 + WD:WT], ins["f1_rest"][row[1], :]).then_inc(sem, 16)

        @block.sync
        def _(sp):
            load_weights(sp, (ds(E1 * P, P), ds(E1 * HT1, HT1)), 0, wf_loaded[0])

            def fetch(n):
                b = n.t - HU
                expert = sp.value_load(plan.expert[0:1, ds(b, 1)], min_val=0, max_val=E1 - 1)
                use = b + 1
                wait(sp, S["w_low2"], use - 1)
                wait(sp, S["w_high2"], use - 1)
                load_weights(sp, (ds(expert * P, P), ds(expert * HT1, HT1)), 1 - n.b, wf_loaded[1 - n.b])
                if isinstance(n.t, int) and n.t == HU:
                    sp.wait_ge(S["sent"], 16 * 2 * NT)
                wait(sp, S["t_ps"], b - 1)
                sp.dma_start(xr[:, n.b, :, :], slots[ds(b * SB, SB), :].rearrange("(p a) m -> p a m", a=TU)).then_inc(xr_loaded[n.b], 16)
            blocks(sp, fetch)

        def low_weights(pool, use, s, slot, rounds):
            pool.wait_ge(wf_loaded[s], rounds * 48)
            pool.wait_ge(S["w_high"], use + 1)
            K.hold(pool)
            pool.tensor_tensor(out=wb[:, slot, 1, 0:W1], in0=wf[:, s, 0:W1], in1=wb[:, slot, 0, 0:W1], op=ALU.subtract).then_inc(S["w_low"], 1)
            pool.wait_ge(S["w_high2"], use + 1)
            K.hold(pool)
            pool.tensor_tensor(out=wb[:, slot, 1, W1:W1 + WD], in0=wf[:, s, W1:W1 + WD], in1=wb[:, slot, 0, W1:W1 + WD], op=ALU.subtract)
            pool.tensor_tensor(out=wb[0:HT1, slot, 1, W1 + WD:WT], in0=wf[0:HT1, s, W1 + WD:WT], in1=wb[0:HT1, slot, 0, W1 + WD:WT],
                               op=ALU.subtract).then_inc(S["w_low2"], 1)

        @block.gpsimd
        def _(pool):
            for k in range(2):
                for t in range(NT):
                    pool.indirect_dma_start(out=slots[:, :], out_offset=bass.IndirectOffsetOnAxis(ap=plan.slot[:, k * NT + t:k * NT + t + 1], axis=0),
                                            in_=plan.rows[:, t * 2 * D:(t + 1) * 2 * D], in_offset=None).then_inc(S["sent"], 16)
                if k == 0:
                    low_weights(pool, 0, 0, 2, 1)

            def step(n):
                b = n.t - HU
                low_weights(pool, b + 1, 1 - n.b, n.b, n.half - HU // 2 + 1 + n.b)
            blocks(pool, step)
            for b in range(2):
                pool.wait_ge(y_stored[b], 16 * ((NB + 1 - b) // 2))
            for t in range(NT):
                wait(pool, S["combined"], t - 1)
                for k in range(2):
                    pool.indirect_dma_start(out=fetched[:, t % 2, k, :], out_offset=None, in_=outs[:, :],
                                            in_offset=bass.IndirectOffsetOnAxis(ap=plan.slot[:, k * NT + t:k * NT + t + 1], axis=0))\
                        .then_inc(got[t % 2], 16)

        @block.tensor
        def _(pe):
            def transposes(n):
                b = n.t - HU
                pe.wait_ge(xr_loaded[n.b], (n.half - HU // 2) * 16 + 16)
                wait(pe, S["xg_ready"], b - 1)
                for hl in range(2):
                    for c in range(DC):
                        for a in range(TU):
                            i = (hl * DC + c) * TU + a
                            last = pe.transpose(ps_t[n.b][:, i * P:(i + 1) * P],
                                                xr[:, n.b, a, hl * D + c * P:hl * D + (c + 1) * P], identb[:, :])
                last.then_inc(S["t_ps"], 1)

            def up(n, x, slot):
                for c in range(NH):
                    q, bank = n.t * NH + c, (n.k * NH + c) % 4
                    wait(pe, S["hf_ready"], q - 3)
                    for half in range(2 if c < HF1 else 1):
                        col = (half * HF1 + c) * P if c < HF1 else 2 * HF1 * P
                        parts = [(wh, xh, kc) for wh, xh in ((0, 0), (1, 0), (0, 1)) for kc in range(DC)]
                        for i, (wh, xh, kc) in enumerate(parts):
                            w0 = kc * 2 * HID1 + col
                            last = pe.matmul(ps_u[bank][:, half * SB:(half + 1) * SB], wb[:, slot, wh, w0:w0 + P], x(xh, kc),
                                             start=(i == 0), stop=(i == len(parts) - 1))
                    last.then_inc(S["up_ps"], 1)

            def down(n, slot):
                if not isinstance(n.t, int) or HU <= n.t < HU + NB:
                    pe.wait_ge(S["w_low2"], n.t - HU + 2)
                pe.wait_ge(S["hb_high"], n.t + 1)
                pe.wait_ge(S["hb_low"], n.t + 1)
                wait(pe, S["y_ready"], n.t - 1)
                for a in range(TU):
                    parts = [(hh, wh, c) for hh, wh in ((0, 0), (1, 0), (0, 1)) for c in range(NH)]
                    for i, (hh, wh, c) in enumerate(parts):
                        w, w0 = (P, W1 + c * D) if c < HF1 else (HT1, W1 + WD)
                        last = pe.matmul(ps_d[n.b][:, a * D:(a + 1) * D], hb[0:w, n.b, hh, c, a * P:(a + 1) * P],
                                         wb[0:w, slot, wh, w0:w0 + D], start=(i == 0), stop=(i == len(parts) - 1))
                last.then_inc(S["down_ps"], 1)

            def up_base(n):
                u = base_unit(n.t)
                up(n, lambda hl, kc: xT[:, hl, kc, u * SB:(u + 1) * SB], 2)

            def up_block(n):
                b = n.t - HU
                pe.wait_ge(S["w_low"], b + 2)
                pe.wait_ge(S["xg_ready"], b + 1)
                up(n, lambda hl, kc: xg[:, n.b, hl, kc, :], n.b)

            pe.wait_ge(S["identb_ready"], 1)
            pe.wait_ge(S["w_low"], 1)
            pe.wait_ge(S["w_low2"], 1)
            up_base(tile(0))
            for n in range(1, HU):
                up_base(tile(n))
                down(tile(n - 1), 2)
            transposes(tile(HU))
            up_block(tile(HU))
            transposes(tile(HU + 1))
            down(tile(HU - 1), 2)

            def step(n):
                up_block(n)
                transposes(n.at(1))
                down(n.at(-1), 1 - n.b)
            over(pe, HU + 1, HU + NB - 1, step, peel=HU + 4)
            last = tile(HU + NB - 1)
            up_block(last)
            down(last.at(-1), 1 - last.b)
            for n in range(HU + NB, N):
                up_base(tile(n))
                down(tile(n - 1), last.b if n == HU + NB else 2)
            down(tile(N - 1), 2)

        @block.scalar
        def _(act):
            act.activation(identb[:, :], K.ident[:, :], ACT.Copy).then_inc(S["identb_ready"], 1)

            def high_up(s, slot, rounds, kc):
                act.wait_ge(wf_loaded[s], rounds * 48)
                w0, w1 = kc * 2 * HID1, (kc + 1) * 2 * HID1
                ins = act.activation(wb[:, slot, 0, w0:w1], wf[:, s, w0:w1], ACT.Copy)
                if kc == DC - 1:
                    ins.then_inc(S["w_high"], 1)

            def high_down(s, slot):
                act.activation(wb[:, slot, 0, W1:W1 + WD], wf[:, s, W1:W1 + WD], ACT.Copy)
                act.activation(wb[0:HT1, slot, 0, W1 + WD:WT], wf[0:HT1, s, W1 + WD:WT], ACT.Copy).then_inc(S["w_high2"], 1)

            def prepare_up(n, kc):
                wait(act, S["up_ps"], (n.t - 1) * NH)
                high_up(1 - n.b, n.b, n.half - HU // 2 + 1 + n.b, kc)

            def prepare_tokens(n):
                b = n.t - HU
                act.wait_ge(S["t_ps"], b + 1)
                wait(act, S["up_ps"], (n.t - 1) * NH)
                act.activation(xg[:, n.b, :, :, :].rearrange("p h c m -> p (h c m)"), ps_t[n.b][:, :], ACT.Copy).then_inc(S["xg_ready"], 1)

            def prepare_down(n):
                wait(act, S["down_ps"], n.t - 1)
                high_down(1 - n.b, n.b)

            def silus(n, between=None):
                for c in range(NH):
                    w = P if c < HF1 else HT1
                    q, bank = n.t * NH + c, (n.k * NH + c) % 4
                    act.wait_ge(S["up_ps"], q + 1)
                    wait(act, S["hf_ready"], q - 1)
                    act.activation(silu[0:w, c % 2, :], ps_u[bank][0:w, 0:SB], ACT.Silu).then_inc(S["silu_ready"], 1)
                    if between and c % 2 == 1 and c // 2 < DC:
                        between(c // 2)

            def highs(n):
                act.wait_ge(S["hf_ready"], n.t * NH + NH)
                wait(act, S["down_ps"], n.t - 1)
                act.activation(hb[:, n.b, 0, 0:HF1, :], hf[:, n.b, 0:HF1, :], ACT.Copy)
                act.activation(hb[0:HT1, n.b, 0, HF1, :], hf[0:HT1, n.b, HF1, :], ACT.Copy).then_inc(S["hb_high"], 1)

            def store(n):
                b = n.t - HU
                act.wait_ge(S["y_ready"], n.t + 1)
                act.dma_start(outs[ds(b * SB, SB), :].rearrange("(p a) m -> p (a m)", a=TU), y[:, n.b, :]).then_inc(y_stored[n.b], 16)

            for kc in range(DC):
                high_up(0, 2, 1, kc)
            high_down(0, 2)
            for n in range(HU - 1):
                silus(tile(n))
                highs(tile(n))

            def step(n):
                if not isinstance(n.t, int) or n.t >= HU + 2:
                    store(n.at(-2))
                silus(n, lambda kc: prepare_up(n.at(1), kc))
                prepare_tokens(n.at(1))
                highs(n)
                prepare_down(n.at(1))
            over(act, HU - 1, HU + NB - 1, step, peel=HU + 4)
            for n in range(HU + NB - 1, N):
                if n < HU + NB + 2:
                    store(tile(n - 2))
                silus(tile(n))
                highs(tile(n))

        @block.vector
        def _(dve):
            def gated(n):
                for c in range(NH):
                    w = P if c < HF1 else HT1
                    q, bank = n.t * NH + c, (n.k * NH + c) % 4
                    dve.wait_ge(S["silu_ready"], q + 1)
                    if c == 0:
                        wait(dve, S["hb_high"], n.t - 1)
                        wait(dve, S["hb_low"], n.t - 1)
                    other = ps_u[bank][:, SB:2 * SB] if c < HF1 else ps_u[bank][HT1:2 * HT1, 0:SB]
                    dve.tensor_tensor(out=hf[0:w, n.b, c, :], in0=silu[0:w, c % 2, :], in1=other, op=ALU.mult).then_inc(S["hf_ready"], 1)

            def lows(n):
                dve.wait_ge(S["hb_high"], n.t + 1)
                dve.tensor_tensor(out=hb[:, n.b, 1, 0:HF1, :], in0=hf[:, n.b, 0:HF1, :], in1=hb[:, n.b, 0, 0:HF1, :], op=ALU.subtract)
                dve.tensor_tensor(out=hb[0:HT1, n.b, 1, HF1, :], in0=hf[0:HT1, n.b, HF1, :], in1=hb[0:HT1, n.b, 0, HF1, :],
                                  op=ALU.subtract).then_inc(S["hb_low"], 1)

            def take_block(n):
                dve.wait_ge(S["down_ps"], n.t + 1)
                wait(dve, y_stored[n.b], (n.half - HU // 2) * 16)
                dve.tensor_scalar(out=y[:, n.b, :], in0=ps_d[n.b][:, :], scalar1=1.0, scalar2=None, op0=ALU.mult).then_inc(S["y_ready"], 1)

            def take_base(n):
                u = base_unit(n.t)
                dve.wait_ge(S["down_ps"], n.t + 1)
                hs = K.h[:, u * TU * D:(u + 1) * TU * D]
                dve.tensor_tensor(out=hs, in0=ps_d[n.b][:, :], in1=hs, op=ALU.add).then_inc(S["y_ready"], 1)

            def combine(t):
                dve.wait_ge(got[t % 2], (t // 2 + 1) * 32)
                dve.wait_ge(S["y_ready"], N)
                hs = K.h[:, t * D:(t + 1) * D]
                for k in range(2):
                    wgt = plan.weight[:, k * NT + t:k * NT + t + 1]
                    dve.scalar_tensor_tensor(out=hs, in0=fetched[:, t % 2, k, :], scalar=wgt, in1=hs, op0=ALU.mult, op1=ALU.add)\
                       .then_inc(S["combined1" if k == 0 else "combined"], 1)
                    if k == 0:
                        dve.wait_ge(S["combined1"], t + 1)

            gated(tile(0))
            lows(tile(0))
            for n in range(1, HU):
                gated(tile(n))
                lows(tile(n))
                take_base(tile(n - 1))
            gated(tile(HU))
            lows(tile(HU))
            take_base(tile(HU - 1))

            def step(n):
                gated(n)
                lows(n)
                take_block(n.at(-1))
            over(dve, HU + 1, HU + NB, step, peel=HU + 4)
            for n in range(HU + NB, N):
                gated(tile(n))
                lows(tile(n))
                (take_block if n == HU + NB else take_base)(tile(n - 1))
            take_base(tile(N - 1))
            for t in range(NT):
                combine(t)


def stage_output(K):
    nc = K.nc
    with ExitStack() as ctx:
        stored = K.sem("o_stored")
        block = ctx.enter_context(nc.Block())

        @block.sync
        def _(sp):
            sp.dma_start(K.out.rearrange("(t p) d -> p t d", p=P),
                         K.h[:, :].rearrange("p (t d) -> p t d", t=NT)).then_inc(stored, 16)
            sp.wait_ge(stored, 16)


def build(nc, ins, out):
    with ExitStack() as ctx:
        K = Core(nc, ctx, ins, out)
        with nc.sbuf_tensor("stats", [P, NT * 3 * D], F32) as stats:
            stage_statistics(K, stats)
            stage_projection(K, stats)
        stage_token_norm(K)
        stage_attention0(K)
        with nc.sbuf_tensor("xT", [P, DC, TOK], F32) as xT, nc.sbuf_tensor("gate", [P, E0, NT], F32) as gate:
            stage_gate(K, "f0_", E0, route0(gate), xT)
            stage_experts0(K, xT, gate)
            stage_shared0(K, xT)
        with nc.sbuf_tensor("wf", [P, 2, DC, H1 * F1], F32) as wf:
            stage_fused_weights(K, wf)
            stage_attention1(K, wf)
        K.renew_semaphores()
        slots = nc.dram_tensor("slots", (NB * SB, 2 * D), BF16).ap()
        stage_clear_slots(K, slots)
        with nc.sbuf_tensor("xT1", [P, 2, DC, TOK], BF16) as xT, ExitStack() as moe:
            plan = Plan(nc, moe, K)
            stage_gate(K, "f1_", E1, route1(), xT, plan)
            stage_experts1(K, xT, plan, slots)
        stage_output(K)


def arranged(i):
    import numpy as np

    up = np.concatenate([i["L1_ffn_exp_wgu"], i["L1_ffn_base_wgu"][None]])
    down = np.concatenate([i["L1_ffn_exp_wd"], i["L1_ffn_base_wd"][None]])
    whole = HF1 * P
    up = np.concatenate([up[..., :whole], up[..., HID1:HID1 + whole], up[..., whole:HID1], up[..., HID1 + whole:]], axis=-1)
    return {
        "x": i["x"].reshape(TOK, BLK * D),
        "w_proj": i["L0_tok_w_proj_w"].reshape(D),
        "b_proj": i["L0_tok_w_proj_b"],
        "s_proj_w": i["L0_tok_s_proj_w"],
        "s_proj_b": i["L0_tok_s_proj_b"],
        "ln_g": i["L0_tok_ln_g"],
        "ln_b": i["L0_tok_ln_b"],
        "pos_emb": i["L0_tok_pos_emb"],
        **{f"a0_w{n}T": i[f"L0_attn_W{n}"].T for n in "qkvo"},
        **{f"a0_b{n}": i[f"L0_attn_b{n}"] for n in "qkvo"},
        "a1_wqT": i["L1_attn_Wq"].T,
        "a1_wkT": i["L1_attn_Wk"].T,
        "a1_kq": i["L1_attn_Kq"],
        "a1_kk": i["L1_attn_Kk"],
        "a1_wv": i["L1_attn_Wv"],
        "a1_wo": i["L1_attn_Wo"],
        "f1_gate": i["L1_ffn_gate_w"],
        "f1_up": up.reshape(E1 + 1, DC, P, 2 * HID1).transpose(0, 2, 1, 3).reshape((E1 + 1) * P, W1),
        "f1_down": down[:, :whole].reshape(E1 + 1, HF1, P, D).transpose(0, 2, 1, 3).reshape((E1 + 1) * P, HF1 * D),
        "f1_rest": down[:, whole:].reshape((E1 + 1) * HT1, D),
        "f0_gate": i["L0_ffn_gate_w"].T,
        "f0_gate_bias": i["L0_ffn_expert_bias"],
        "f0_up": i["L0_ffn_w_up"].transpose(0, 2, 1).reshape(E0 * D, HID0),
        "f0_down": i["L0_ffn_w_down"].transpose(0, 2, 1).reshape(E0 * HID0, D),
        "f0_shared_up": i["L0_ffn_shared_w_up"].T,
        "f0_shared_down": i["L0_ffn_shared_w_down"].T,
    }


def kernel(**inputs):
    import numpy as np
    from concourse import bacc
    from concourse.bass_utils import run_bass_kernel_spmd

    nc = bacc.Bacc("TRN2", target_bir_lowering=False, num_devices=1)
    arrays, args = {}, {}
    for name, a in arranged({k: np.asarray(v) for k, v in inputs.items()}).items():
        a = np.ascontiguousarray(a)
        arrays["in_" + name] = a
        args[name] = nc.dram_tensor("in_" + name, a.shape, mybir.dt.from_np(a.dtype), kind="ExternalInput").ap()
    out = nc.dram_tensor("out_0_dram", (TOK // NPOS, NPOS, D), F32, kind="ExternalOutput").ap()
    build(nc, args, out.rearrange("b s d -> (b s) d"))
    r = run_bass_kernel_spmd(nc, [arrays], core_ids=[0])
    return r.results[0]["out_0_dram"]
```

```python
from contextlib import ExitStack

import concourse.bass as bass
from concourse import mybir

P = 128
F32 = mybir.dt.float32
BF16 = mybir.dt.bfloat16
ALU = mybir.AluOpType
ACT = mybir.ActivationFunctionType
AX = mybir.AxisListType.X
ds = bass.ds

D = 256
DC = D // P
BLK = 16
NPOS = 16
TOK = 2048
NT = TOK // P
BPT = P // NPOS
H0, D0 = 16, 16
H1, D1, F1 = 16, 64, 64
E0, HID0 = 8, 352
E1, HID1 = 8, 704
GT = 512
NG = TOK // GT
TPG = GT // P
SB = 256
NB = (2 * TOK + E1 * (SB - 1)) // SB
W1 = DC * 2 * HID1
HF1 = HID1 // P
HT1 = HID1 - HF1 * P
LN_EPS = 1e-5
VAR_EPS = 1e-8
FEAT_EPS = 1e-12


class Chain:

    def __init__(self, eng, sem):
        self.eng, self.sem, self.base, self.n = eng, sem, 0, 0

    def start(self, base):
        self.base, self.n = base, 0

    def done(self, ins):
        ins.then_inc(self.sem, 1)
        self.n += 1
        self.eng.wait_ge(self.sem, self.base + self.n)


def chunks(n):
    return [(c, min(P, n - c * P)) for c in range((n + P - 1) // P)]


class Core:

    def __init__(self, nc, ctx, ins, out):
        self.nc, self.ins, self.out = nc, ins, out
        self.ctx = ctx
        f = lambda name, shape, dt=F32: ctx.enter_context(nc.sbuf_tensor(name, shape, dt))
        self.h = f("h", [P, NT * D])
        self.mv = f("mv", [P, NT, 2])
        self.moments = f("moments", [P, NT * 6])
        self.std = f("std", [P, NT])
        self.rstd = f("rstd", [P, NT])
        self.ident = f("ident", [P, P])
        self.zero = f("zero", [P, 2 * D], BF16)
        self.eps_ln = f("eps_ln", [P, 1])
        self.eps_var = f("eps_var", [P, 1])
        self.sems = []
        self.passes = nc.alloc_semaphore("passes")
        self.slots_cleared = nc.alloc_semaphore("slots_cleared")

    def sem(self, name):
        self.sems.append(self.nc.alloc_semaphore(name))
        return self.sems[-1]

    def renew_semaphores(self):
        self.nc.clear_and_free_semaphores(self.sems)
        self.sems = []
        self.nc.all_engine_barrier()

    def hold(self, eng):
        eng.sem_inc(self.passes, 1)



class Turn:

    def __init__(self, turn, k, per):
        self.turn, self.k, self.per = turn, k, per
        self.t = turn * per + k
        self.b = k % 2
        self.half = turn * (per // 2) + k // 2

    def at(self, d):
        q = self.k + d
        return Turn(self.turn + q // self.per, q % self.per, self.per)


def tile(t, per=2):
    return Turn(t // per, t % per, per)


def wait(eng, sem, count):
    if not isinstance(count, int) or count > 0:
        eng.wait_ge(sem, count)


def over(eng, first, last, step, per=2, peel=None):
    lo = max(peel or max(per, 4), first + -first % per)
    hi = max(lo, last - last % per)
    for t in range(first, min(lo, last)):
        step(tile(t, per))
    if hi > lo:
        with eng.Fori(lo // per, hi // per) as i:
            for k in range(per):
                step(Turn(i, k, per))
    for t in range(max(hi, first), last):
        step(tile(t, per))


def has(a, d):
    return not isinstance(a.t, int) or 0 <= a.t + d < NT


def passes(eng, step):
    over(eng, 0, NT - 1, step)
    for p in range(NT - 1, NT + 2):
        step(tile(p))


def stage_statistics(K, stats):
    nc, ins = K.nc, K.ins
    XB = 4
    with ExitStack() as ctx:
        sb = lambda name, shape, dt=F32: ctx.enter_context(nc.sbuf_tensor(name, shape, dt))
        x = sb("x", [P, XB, BLK * D])
        diag = sb("diag", [P, XB, BLK * P])
        wproj = sb("wproj", [P, D])
        bproj = sb("bproj", [P, 1])
        prod = sb("prod", [P, BLK, D])
        logit = sb("logit", [P, 2, BLK])
        logitb = sb("logitb", [P, 2, BLK])
        nmax = sb("nmax", [P, 2])
        expw = sb("expw", [P, 2, BLK])
        esum = sb("esum", [P, 2])
        rsum = sb("rsum", [P, 2])
        w = sb("w", [P, 2, BLK])
        ps_mean = [ctx.enter_context(nc.psum_tensor(f"ps_mean{b}", [P, 512], F32)) for b in range(2)]
        ps_var = [ctx.enter_context(nc.psum_tensor(f"ps_var{b}", [P, 512], F32)) for b in range(2)]

        const_loaded = K.sem("t_const_loaded")
        ident_steps = K.sem("t_ident_steps")
        x_loaded = [K.sem(f"t_x_loaded{b}") for b in range(XB)]
        nmax_ready = K.sem("t_nmax_ready")
        exp_ready = K.sem("t_exp_ready")
        w_ready = K.sem("t_w_ready")
        max_ready = K.sem("t_max_ready")
        diag_ready = K.sem("t_diag_ready")
        mean_ready = K.sem("t_mean_ready")
        diff_ready = K.sem("t_diff_ready")
        square_ready = K.sem("t_square_ready")
        var_ready = K.sem("t_var_ready")
        var_copied = K.sem("t_var_copied")
        steps = K.sem("t_vector_steps")
        block = ctx.enter_context(nc.Block())

        @block.sync
        def _(sp):
            sp.dma_start(wproj[:, :], ins["w_proj"].partition_broadcast(P)).then_inc(const_loaded, 16)
            sp.dma_start(bproj[:, :], ins["b_proj"].partition_broadcast(P)).then_inc(const_loaded, 16)

            def load(a):
                wait(sp, var_ready, a.t - XB + 1)
                sp.dma_start(x[:, a.k, :], ins["x"][ds(a.t * P, P), :]).then_inc(x_loaded[a.k], 16)
            over(sp, 0, NT, load, per=XB)

        @block.gpsimd
        def _(pool):
            pool.memset(K.zero[:, :], 0.0)
            pool.memset(K.eps_ln[:, :], LN_EPS)
            pool.memset(K.eps_var[:, :], VAR_EPS)
            pool.memset(K.ident[:, :], 0.0).then_inc(ident_steps, 1)
            pool.wait_ge(ident_steps, 1)
            pool.affine_select(out=K.ident[:, :], in_=K.ident[:, :], compare_op=ALU.not_equal, fill=1.0,
                               base=0, pattern=[[-1, P]], channel_multiplier=1).then_inc(ident_steps, 1)
            pool.wait_ge(ident_steps, 2)

            def spread(a):
                pool.wait_ge(w_ready, a.t + 1)
                wait(pool, var_ready, a.t - XB + 1)
                pool.tensor_tensor(out=diag[:, a.k, :].rearrange("p (k m) -> p k m", k=BLK),
                                   in0=K.ident[:, :].rearrange("p (a m) -> p a m", a=1).broadcast_to([P, BLK, P]),
                                   in1=w[:, a.b, :].rearrange("p (k a) -> p k a", a=1).broadcast_to([P, BLK, P]),
                                   op=ALU.mult).then_inc(diag_ready, 1)
            over(pool, 0, NT, spread, per=XB)

        @block.vector
        def _(dve):
            chain = Chain(dve, steps)
            dve.wait_ge(const_loaded, 32)

            def maximum(a, half):
                W = D // 2
                dve.tensor_reduce(out=stats[:, ds(a.t * 3 * D + 2 * D + half * W, W)],
                                  in_=x[:, a.k, :].rearrange("p (k d) -> p d k", k=BLK)[:, half * W:(half + 1) * W, :],
                                  axis=AX, op=ALU.max).then_inc(max_ready, 1)

            def head(a):
                chain.start(a.t * 3)
                dve.wait_ge(x_loaded[a.k], a.turn * 16 + 16)
                for k in range(BLK):
                    last = dve.tensor_tensor_reduce(out=prod[:, k, :], in0=x[:, a.k, k * D:(k + 1) * D], in1=wproj[:, :],
                                                    scale=1.0, scalar=0.0, op0=ALU.mult, op1=ALU.add,
                                                    accum_out=logit[:, a.b, k:k + 1])
                chain.done(last)
                chain.done(dve.tensor_scalar(out=logitb[:, a.b, :], in0=logit[:, a.b, :], scalar1=bproj[:, 0:1],
                                             scalar2=None, op0=ALU.add))
                dve.tensor_reduce(out=nmax[:, a.b:a.b + 1], in_=logitb[:, a.b, :], axis=AX, op=ALU.max,
                                  negate=True).then_inc(nmax_ready, 1)
                maximum(a, 0)
                dve.wait_ge(exp_ready, a.t + 1)
                wait(dve, diag_ready, a.t - 1)
                chain.done(dve.reciprocal(rsum[:, a.b:a.b + 1], esum[:, a.b:a.b + 1]))
                dve.tensor_scalar(out=w[:, a.b, :], in0=expw[:, a.b, :], scalar1=rsum[:, a.b:a.b + 1],
                                  scalar2=None, op0=ALU.mult).then_inc(w_ready, 1)
                maximum(a, 1)

            def deviations(a):
                dve.wait_ge(mean_ready, a.t + 1)
                dve.wait_ge(max_ready, a.t * 2 + 2)
                dve.tensor_tensor(out=x[:, a.k, :].rearrange("p (k d) -> p k d", k=BLK),
                                  in0=x[:, a.k, :].rearrange("p (k d) -> p k d", k=BLK),
                                  in1=ps_mean[a.b][:, 0:D].rearrange("p (a d) -> p a d", a=1).broadcast_to([P, BLK, D]),
                                  op=ALU.subtract).then_inc(diff_ready, 1)

            def step(a):
                head(a)
                deviations(a.at(-1))
            head(tile(0, XB))
            over(dve, 1, NT, step, per=XB)
            deviations(tile(NT - 1, XB))

        @block.scalar
        def _(act):
            def weights(a):
                act.wait_ge(nmax_ready, a.t + 1)
                act.activation(expw[:, a.b, :], logitb[:, a.b, :], ACT.Exp, bias=nmax[:, a.b:a.b + 1],
                               accum_out=esum[:, a.b:a.b + 1]).then_inc(exp_ready, 1)

            def squares(a):
                act.wait_ge(diff_ready, a.t + 1)
                act.activation(stats[:, ds(a.t * 3 * D, D)], ps_mean[a.b][:, 0:D], ACT.Copy)
                act.activation(x[:, a.k, :], x[:, a.k, :], ACT.Square).then_inc(square_ready, 1)

            def variance(a):
                act.wait_ge(var_ready, a.t + 1)
                act.activation(stats[:, ds(a.t * 3 * D + D, D)], ps_var[a.b][:, 0:D], ACT.Copy).then_inc(var_copied, 1)

            def step(a):
                weights(a)
                squares(a.at(-1))
                variance(a.at(-2))
            weights(tile(0, XB))
            weights(tile(1, XB))
            squares(tile(0, XB))
            over(act, 2, NT, step, per=XB)
            squares(tile(NT - 1, XB))
            variance(tile(NT - 2, XB))
            variance(tile(NT - 1, XB))

        @block.tensor
        def _(pe):
            def mean(a):
                pe.wait_ge(diag_ready, a.t + 1)
                wait(pe, square_ready, a.t - 1)
                for k in range(BLK):
                    last = pe.matmul(ps_mean[a.b][:, 0:D], diag[:, a.k, k * P:(k + 1) * P], x[:, a.k, k * D:(k + 1) * D],
                                     start=(k == 0), stop=(k == BLK - 1))
                last.then_inc(mean_ready, 1)

            def variance(a):
                pe.wait_ge(square_ready, a.t + 1)
                wait(pe, var_copied, a.t - 1)
                for k in range(BLK):
                    last = pe.matmul(ps_var[a.b][:, 0:D], diag[:, a.k, k * P:(k + 1) * P], x[:, a.k, k * D:(k + 1) * D],
                                     start=(k == 0), stop=(k == BLK - 1))
                last.then_inc(var_ready, 1)

            def step(a):
                mean(a)
                variance(a.at(-1))
            mean(tile(0, XB))
            over(pe, 1, NT, step, per=XB)
            variance(tile(NT - 1, XB))


def stage_projection(K, stats):
    nc, ins = K.nc, K.ins
    SC = 3 * DC
    with ExitStack() as ctx:
        sb = lambda name, shape, dt=F32: ctx.enter_context(nc.sbuf_tensor(name, shape, dt))
        wsp = sb("wsp", [P, SC, D])
        bsp = sb("bsp", [P, D])
        gain, shift, pos = sb("gain", [P, D]), sb("shift", [P, D]), sb("pos", [P, D])
        pre = sb("pre", [P, 2, D])
        mom, mean = sb("mom", [P, 2, 6]), sb("mean", [P, 2, 2])
        dev, rdev = sb("dev", [P, 2]), sb("rdev", [P, 2])
        centred, scaled = sb("centred", [P, 2, D]), sb("scaled", [P, 2, D])
        st = sb("st", [P, 2, 3 * D])
        sT = sb("sT", [P, 2, SC * P])
        ps_t = [ctx.enter_context(nc.psum_tensor(f"ps_t{b}", [P, 1024], F32)) for b in range(2)]
        ps_o = [ctx.enter_context(nc.psum_tensor(f"ps_o{b}", [P, 512], F32)) for b in range(2)]
        w_loaded = K.sem("p_w_loaded")
        st_ready = K.sem("p_st_ready")
        transposed = K.sem("p_transposed")
        sT_ready = K.sem("p_sT_ready")
        out_ready = K.sem("p_out_ready")
        out_read = K.sem("p_out_read")
        shift_ready, mean_ready, dev_ready, centred_ready, scaled_ready, h_ready, steps = (
            K.sem("p_" + n) for n in "shift_ready mean_ready dev_ready centred_ready scaled_ready h_ready steps".split())
        block = ctx.enter_context(nc.Block())

        @block.sync
        def _(sp):
            sp.dma_start(wsp[:, :, :], ins["s_proj_w"].rearrange("(c p) n -> p c n", p=P)).then_inc(w_loaded, 16)
            sp.dma_start(bsp[:, :], ins["s_proj_b"].partition_broadcast(P)).then_inc(w_loaded, 16)
            sp.dma_start(gain[:, :], ins["ln_g"].partition_broadcast(P)).then_inc(w_loaded, 16)
            sp.dma_start(shift[:, :], ins["ln_b"].partition_broadcast(P)).then_inc(w_loaded, 16)
            for j in range(BPT):
                sp.dma_start(pos[j * NPOS:(j + 1) * NPOS, :], ins["pos_emb"][0:NPOS, :]).then_inc(w_loaded, 16)

        LOADS = 16 * (4 + BPT)

        @block.gpsimd
        def _(pool):
            pool.wait_ge(w_loaded, LOADS)
            pool.tensor_tensor(out=shift[:, :], in0=shift[:, :], in1=pos[:, :], op=ALU.add).then_inc(shift_ready, 1)

            def scale(a):
                pool.wait_ge(centred_ready, a.t + 1)
                wait(pool, h_ready, a.t - 1)
                pool.tensor_tensor(out=scaled[:, a.b, :], in0=centred[:, a.b, :], in1=gain[:, :], op=ALU.mult).then_inc(scaled_ready, 1)
            over(pool, 0, NT, scale)

        @block.scalar
        def _(act):
            def stage(a):
                wait(act, transposed, a.t - 1)
                act.activation(st[:, a.b, 0:D], stats[:, ds(a.t * 3 * D, D)], ACT.Copy)
                act.activation(st[:, a.b, D:2 * D], stats[:, ds(a.t * 3 * D + D, D)], ACT.Sqrt, bias=K.eps_var[:, 0:1])
                act.activation(st[:, a.b, 2 * D:3 * D], stats[:, ds(a.t * 3 * D + 2 * D, D)], ACT.Copy).then_inc(st_ready, 1)

            def evacuate(a):
                act.wait_ge(transposed, a.t + 1)
                wait(act, out_ready, a.t - 1)
                act.activation(sT[:, a.b, :], ps_t[a.b][:, 0:SC * P], ACT.Copy).then_inc(sT_ready, 1)

            def root(a):
                act.wait_ge(mean_ready, a.t + 1)
                wait(act, centred_ready, a.t - 1)
                act.activation(dev[:, a.b:a.b + 1], mean[:, a.b, 1:2], ACT.Sqrt, bias=K.eps_ln[:, 0:1]).then_inc(dev_ready, 1)

            def step(p):
                if has(p, 1):
                    stage(p.at(1))
                if has(p, 0):
                    evacuate(p)
                if has(p, -2):
                    root(p.at(-2))
            stage(tile(0))
            passes(act, step)

        @block.tensor
        def _(pe):
            def transposes(a):
                pe.wait_ge(st_ready, a.t + 1)
                wait(pe, sT_ready, a.t - 1)
                for c in range(SC):
                    last = pe.transpose(ps_t[a.b][:, c * P:(c + 1) * P], st[:, a.b, c * P:(c + 1) * P], K.ident[:, :])
                last.then_inc(transposed, 1)

            def project(a):
                pe.wait_ge(sT_ready, a.t + 1)
                wait(pe, out_read, a.t - 1)
                for c in range(SC):
                    last = pe.matmul(ps_o[a.b][:, 0:D], sT[:, a.b, c * P:(c + 1) * P], wsp[:, c, :],
                                     start=(c == 0), stop=(c == SC - 1))
                last.then_inc(out_ready, 1)

            def step(a):
                transposes(a)
                project(a.at(-1))
            pe.wait_ge(w_loaded, LOADS)
            transposes(tile(0))
            over(pe, 1, NT, step)
            project(tile(NT - 1))

        @block.vector
        def _(dve):
            dve.wait_ge(w_loaded, LOADS)

            dve.wait_ge(shift_ready, 1)
            chain, chain2 = Chain(dve, steps), Chain(dve, K.sem("p_steps2"))

            def take(a):
                dve.wait_ge(out_ready, a.t + 1)
                wait(dve, centred_ready, a.t - 1)
                dve.tensor_tensor(out=pre[:, a.b, :], in0=ps_o[a.b][:, 0:D], in1=bsp[:, :], op=ALU.add).then_inc(out_read, 1)
                dve.wait_ge(out_read, a.t + 1)
                K.hold(dve)
                chain.start(a.t)
                chain.done(dve.bn_stats(out=mom[:, a.b, :], in_=pre[:, a.b, :]))
                K.hold(dve)
                dve.bn_aggr(out=mean[:, a.b, :], in_=mom[:, a.b, :]).then_inc(mean_ready, 1)

            def centre(a):
                dve.wait_ge(dev_ready, a.t + 1)
                wait(dve, scaled_ready, a.t - 1)
                chain2.start(a.t)
                chain2.done(dve.reciprocal(rdev[:, a.b:a.b + 1], dev[:, a.b:a.b + 1]))
                dve.tensor_scalar(out=centred[:, a.b, :], in0=pre[:, a.b, :], scalar1=mean[:, a.b, 0:1], scalar2=rdev[:, a.b:a.b + 1],
                                  op0=ALU.subtract, op1=ALU.mult).then_inc(centred_ready, 1)

            def finish(a):
                dve.wait_ge(scaled_ready, a.t + 1)
                dve.tensor_tensor(out=K.h[:, ds(a.t * D, D)], in0=scaled[:, a.b, :], in1=shift[:, :], op=ALU.add).then_inc(h_ready, 1)
                take_moments(K, dve, a, h_ready, a.t + 1)

            take(tile(0))
            take(tile(1))
            centre(tile(0))

            def step(a):
                take(a)
                centre(a.at(-1))
                finish(a.at(-2))
            over(dve, 2, NT, step)
            centre(tile(NT - 1))
            finish(tile(NT - 2))
            finish(tile(NT - 1))


def take_moments(K, dve, a, sem, count):
    dve.wait_ge(sem, count)
    K.hold(dve)
    dve.bn_stats(out=K.moments[:, ds(a.t * 6, 6)], in_=K.h[:, ds(a.t * D, D)])


def prepare_norm(K, dve, sems):
    gathered, std_ready, rstd_ready = sems
    for t in range(NT):
        last = dve.bn_aggr(out=K.mv[:, t, :], in_=K.moments[:, t * 6:t * 6 + 6])
    last.then_inc(gathered, 1)
    dve.wait_ge(std_ready, 1)
    dve.reciprocal(K.rstd[:, :], K.std[:, :]).then_inc(rstd_ready, 1)
    dve.wait_ge(rstd_ready, 1)


def root_norm(K, act, sems):
    gathered, std_ready, _ = sems
    act.wait_ge(gathered, 1)
    act.activation(K.std[:, :], K.mv[:, :, 1], ACT.Sqrt, bias=K.eps_ln[:, 0:1]).then_inc(std_ready, 1)


def norm_sems(K, stage):
    return [K.sem(f"{stage}_{n}") for n in ("gathered", "std_ready", "rstd_ready")]


def normalise(K, dve, a, out):
    return dve.tensor_scalar(out=out, in0=K.h[:, ds(a.t * D, D)], scalar1=K.mv[:, ds(a.t, 1), 0],
                             scalar2=K.rstd[:, ds(a.t, 1)], op0=ALU.subtract, op1=ALU.mult)


def stage_attention0(K):
    nc, ins = K.nc, K.ins
    HC = P // D0
    VW = D0 + 1
    with ExitStack() as ctx:
        sb = lambda name, shape, dt=F32: ctx.enter_context(nc.sbuf_tensor(name, shape, dt))
        wq, wk, wv, wo = (sb("a_" + n, [P, DC, D]) for n in ("wq", "wk", "wv", "wo"))
        bqk = sb("a_bqk", [P, 2 * DC])
        bv, bo = sb("a_bv", [P, D]), sb("a_bo", [P, D])
        same = sb("a_same", [P, 4, P])
        head = sb("a_head", [P, HC])
        xn = sb("a_xn", [P, 2, D])
        xT = sb("a_xT", [P, 2, D])
        qk = sb("a_qk", [P, 2, 4, P])
        low = sb("a_low", [P, 2, 4, P])
        q = sb("a_q", [P, 2, DC, P])
        k = sb("a_k", [P, 2, DC, P])
        kh = sb("a_kh", [P, 2, DC * HC, P])
        v = sb("a_v", [P, 2, H0, VW])
        sc = sb("a_sc", [P, 2, 4, P])
        den = sb("a_den", [P, 2, H0])
        rden = sb("a_rden", [P, 2, H0])
        y = sb("a_y", [P, 2, D])
        yT = sb("a_yT", [P, 2, D])
        ps = lambda name: ctx.enter_context(nc.psum_tensor(name, [P, 512], F32))
        ps_x, ps_qk, ps_v, ps_o, ps_yT, ps_w = (ps("a_ps_" + n) for n in ("x", "qk", "v", "o", "yT", "w"))
        ps_s = [ps(f"a_ps_s{b}") for b in range(2)]
        loaded, masks, ones_set = K.sem("a_loaded"), K.sem("a_masks"), K.sem("a_ones_set")
        norm = norm_sems(K, "a")
        names = ("xn_ready xT_ps xT_ready qk_ps v_ps qk_ready low_in low_ready q_ready k_ready kh_ready v_ready "
                 "s_ps s_ready o_ps o_read y_ready yT_ps yT_ready w_ps h_ready moved steps").split()
        S = {n: K.sem("a_" + n) for n in names}
        block = ctx.enter_context(nc.Block())

        @block.sync
        def _(sp):
            for t, n in ((wq, "a0_wqT"), (wk, "a0_wkT"), (wv, "a0_wvT"), (wo, "a0_woT")):
                sp.dma_start(t[:, :, :], ins[n].rearrange("(c p) n -> p c n", p=P)).then_inc(loaded, 16)
            with nc.allow_non_contiguous_dma(reason="512 biases, once"):
                sp.dma_start(bqk[:, 0:DC], ins["a0_bq"].rearrange("(c p) -> p c", p=P)).then_inc(loaded, 16)
                sp.dma_start(bqk[:, DC:2 * DC], ins["a0_bk"].rearrange("(c p) -> p c", p=P)).then_inc(loaded, 16)
            sp.dma_start(bv[:, :], ins["a0_bv"].partition_broadcast(P)).then_inc(loaded, 16)
            sp.dma_start(bo[:, :], ins["a0_bo"].partition_broadcast(P)).then_inc(loaded, 16)

        @block.gpsimd
        def _(pool):
            batch_mask(pool, same, NPOS, masks, causal=False)
            head_mask(pool, head, HC, D0, masks, 3)
            pool.memset(v[:, :, :, D0:VW], 1.0).then_inc(ones_set, 1)

            def spread(a):
                pool.wait_ge(S["k_ready"], a.t + 1)
                wait(pool, S["s_ps"], (a.t - 1) * 4)
                for c in range(DC):
                    last = pool.tensor_tensor(out=kh[:, a.b, c * HC:(c + 1) * HC, :],
                                              in0=k[:, a.b, c:c + 1, :].broadcast_to([P, HC, P]),
                                              in1=head[:, :].rearrange("p (h a) -> p h a", a=1).broadcast_to([P, HC, P]), op=ALU.mult)
                last.then_inc(S["kh_ready"], 1)
            over(pool, 0, NT, spread)

        @block.scalar
        def _(act):
            root_norm(K, act, norm)

            def take_xT(a):
                act.wait_ge(S["xT_ps"], a.t + 1)
                wait(act, S["v_ps"], a.t - 1)
                act.activation(xT[:, a.b, :], ps_x[:, 0:D], ACT.Copy).then_inc(S["xT_ready"], 1)

            def exps(a):
                act.wait_ge(S["low_in"], a.t + 1)
                act.activation(low[:, a.b, :, :], low[:, a.b, :, :], ACT.Exp).then_inc(S["low_ready"], 1)

            def take_yT(a):
                act.wait_ge(S["yT_ps"], a.t + 1)
                wait(act, S["w_ps"], a.t - 1)
                act.activation(yT[:, a.b, :], ps_yT[:, 0:D], ACT.Copy).then_inc(S["yT_ready"], 1)

            def step(p):
                if has(p, -2):
                    take_yT(p.at(-2))
                if has(p, 0):
                    exps(p)
                if has(p, 1):
                    take_xT(p.at(1))
            take_xT(tile(0))
            passes(act, step)

        @block.tensor
        def _(pe):
            pe.wait_ge(loaded, 128)

            def tokens(a):
                pe.wait_ge(S["xn_ready"], a.t + 1)
                wait(pe, S["xT_ready"], a.t)
                for c in range(DC):
                    last = pe.transpose(ps_x[:, c * P:(c + 1) * P], xn[:, a.b, c * P:(c + 1) * P], K.ident[:, :])
                last.then_inc(S["xT_ps"], 1)

            def project(a):
                pe.wait_ge(S["xT_ready"], a.t + 1)
                wait(pe, S["qk_ready"], a.t)
                for j, wt in enumerate((wq, wk)):
                    for m in range(DC):
                        for c in range(DC):
                            last = pe.matmul(ps_qk[:, (j * DC + m) * P:(j * DC + m + 1) * P], wt[:, c, m * P:(m + 1) * P],
                                             xT[:, a.b, c * P:(c + 1) * P], start=(c == 0), stop=(c == DC - 1))
                last.then_inc(S["qk_ps"], 1)
                wait(pe, S["v_ready"], a.t)
                for c in range(DC):
                    last = pe.matmul(ps_v[:, 0:D], xT[:, a.b, c * P:(c + 1) * P], wv[:, c, :], start=(c == 0), stop=(c == DC - 1))
                last.then_inc(S["v_ps"], 1)

            def scores(a, g):
                n = a.t * 4 + g
                wait(pe, S["s_ready"], n - 1)
                for j in range(4):
                    hd = g * 4 + j
                    last = pe.matmul(ps_s[g % 2][:, j * P:(j + 1) * P], kh[:, a.b, hd, :], q[:, a.b, hd // HC, :], start=True, stop=True)
                last.then_inc(S["s_ps"], 1)

            def values(a, g):
                n = a.t * 4 + g
                pe.wait_ge(S["s_ready"], n + 1)
                if g == 0:
                    wait(pe, S["o_read"], a.t)
                for j in range(4):
                    hd = g * 4 + j
                    last = pe.matmul(ps_o[:, hd * VW:(hd + 1) * VW], sc[:, g % 2, j, :], v[:, a.b, hd, :], start=True, stop=True)
                last.then_inc(S["o_ps"], 1)

            def turned(a):
                pe.wait_ge(S["y_ready"], a.t + 1)
                wait(pe, S["yT_ready"], a.t)
                for c in range(DC):
                    last = pe.transpose(ps_yT[:, c * P:(c + 1) * P], y[:, a.b, c * P:(c + 1) * P], K.ident[:, :])
                last.then_inc(S["yT_ps"], 1)

            def combine(a):
                pe.wait_ge(S["yT_ready"], a.t + 1)
                wait(pe, S["h_ready"], a.t)
                for c in range(DC):
                    last = pe.matmul(ps_w[:, 0:D], yT[:, a.b, c * P:(c + 1) * P], wo[:, c, :], start=(c == 0), stop=(c == DC - 1))
                last.then_inc(S["w_ps"], 1)

            def step(p):
                a = p.at(-1)
                if has(p, 0):
                    project(p)
                if has(p, -1):
                    pe.wait_ge(S["kh_ready"], a.t + 1)
                    pe.wait_ge(S["q_ready"], a.t + 1)
                    pe.wait_ge(S["v_ready"], a.t + 1)
                    scores(a, 0)
                if has(p, -2):
                    turned(p.at(-2))
                if has(p, -1):
                    scores(a, 1)
                    values(a, 0)
                if has(p, -2):
                    combine(p.at(-2))
                if has(p, -1):
                    scores(a, 2)
                    values(a, 1)
                    scores(a, 3)
                    values(a, 2)
                if has(p, 1):
                    tokens(p.at(1))
                if has(p, -1):
                    values(a, 3)
            tokens(tile(0))
            passes(pe, step)

        @block.vector
        def _(dve):
            chain = Chain(dve, S["steps"])
            prepare_norm(K, dve, norm)
            dve.wait_ge(loaded, 128)
            dve.wait_ge(masks, 6)
            dve.wait_ge(ones_set, 1)

            def centre(a):
                wait(dve, S["xT_ps"], a.t - 1)
                normalise(K, dve, a, xn[:, a.b, :]).then_inc(S["xn_ready"], 1)

            def features_in(a):
                dve.wait_ge(S["qk_ps"], a.t + 1)
                wait(dve, S["s_ps"], (a.t - 1) * 4)
                wait(dve, S["kh_ready"], a.t - 1)
                dve.tensor_tensor(out=qk[:, a.b, :, :], in0=ps_qk[:, :].rearrange("p (c m) -> p c m", c=4),
                                  in1=bqk[:, :].rearrange("p (c a) -> p c a", a=1).broadcast_to([P, 4, P]),
                                  op=ALU.add).then_inc(S["qk_ready"], 1)
                dve.wait_ge(S["qk_ready"], a.t + 1)
                dve.tensor_scalar(out=low[:, a.b, :, :], in0=qk[:, a.b, :, :], scalar1=0.0, scalar2=None, op0=ALU.min).then_inc(S["low_in"], 1)
                dve.wait_ge(S["v_ps"], a.t + 1)
                wait(dve, S["o_ps"], (a.t - 1) * 4)
                dve.tensor_tensor(out=v[:, a.b, :, 0:D0], in0=ps_v[:, 0:D].rearrange("p (h e) -> p h e", h=H0),
                                  in1=bv[:, :].rearrange("p (h e) -> p h e", h=H0), op=ALU.add).then_inc(S["v_ready"], 1)

            def features_out(a):
                dve.wait_ge(S["low_ready"], a.t + 1)
                dve.scalar_tensor_tensor(out=k[:, a.b, :, :], in0=qk[:, a.b, 2:4, :], scalar=0.0, in1=low[:, a.b, 2:4, :],
                                         op0=ALU.max, op1=ALU.add).then_inc(S["k_ready"], 1)
                dve.scalar_tensor_tensor(out=q[:, a.b, :, :], in0=qk[:, a.b, 0:2, :], scalar=0.0, in1=low[:, a.b, 0:2, :],
                                         op0=ALU.max, op1=ALU.add).then_inc(S["q_ready"], 1)

            def masked(a, g):
                n = a.t * 4 + g
                dve.wait_ge(S["s_ps"], n + 1)
                wait(dve, S["o_ps"], n - 1)
                dve.tensor_tensor(out=sc[:, g % 2, :, :], in0=ps_s[g % 2][:, :].rearrange("p (j m) -> p j m", j=4),
                                  in1=same[:, :, :], op=ALU.mult).then_inc(S["s_ready"], 1)

            def normed(a):
                chain.start(a.t * 2)
                dve.wait_ge(S["o_ps"], a.t * 4 + 4)
                wait(dve, S["yT_ps"], a.t - 1)
                o = ps_o[:, 0:H0 * VW].rearrange("p (h e) -> p h e", h=H0)
                chain.done(dve.tensor_scalar(out=den[:, a.b, :], in0=o[:, :, D0], scalar1=1e-6, scalar2=None, op0=ALU.add))
                chain.done(dve.reciprocal(rden[:, a.b, :], den[:, a.b, :]))
                dve.tensor_tensor(out=y[:, a.b, :].rearrange("p (h e) -> p h e", h=H0), in0=o[:, :, 0:D0],
                                  in1=rden[:, a.b, :].rearrange("p (h a) -> p h a", a=1).broadcast_to([P, H0, D0]),
                                  op=ALU.mult).then_inc(S["y_ready"], 1)
                dve.wait_ge(S["y_ready"], a.t + 1)
                dve.sem_inc(S["o_read"], 1)

            def residual(a):
                dve.wait_ge(S["w_ps"], a.t + 1)
                hs = K.h[:, ds(a.t * D, D)]
                dve.tensor_tensor(out=hs, in0=ps_w[:, 0:D], in1=hs, op=ALU.add).then_inc(S["h_ready"], 1)
                dve.wait_ge(S["h_ready"], a.t + 1)
                dve.tensor_tensor(out=hs, in0=hs, in1=bo[:, :], op=ALU.add).then_inc(S["moved"], 1)
                take_moments(K, dve, a, S["moved"], a.t + 1)

            def step(p):
                a = p.at(-1)
                if has(p, 1):
                    centre(p.at(1))
                if has(p, 0):
                    features_in(p)
                if has(p, -1):
                    masked(a, 0)
                if has(p, 0):
                    features_out(p)
                if has(p, -1):
                    masked(a, 1)
                if has(p, -2):
                    residual(p.at(-2))
                if has(p, -1):
                    masked(a, 2)
                    masked(a, 3)
                    normed(a)
            centre(tile(0))
            passes(dve, step)


def batch_mask(pool, m, width, sem, causal):
    pool.memset(m[:, :, :], 1.0).then_inc(sem, 1)
    pool.wait_ge(sem, 1)
    v = m[:, :, :].rearrange("p a (g s) -> p a g s", s=width)
    G = P // width
    pool.affine_select(out=v, in_=v, compare_op=ALU.is_ge, fill=0.0, base=0,
                       pattern=[[0, 4], [-width, G], [0, width]], channel_multiplier=1).then_inc(sem, 1)
    pool.wait_ge(sem, 2)
    pool.affine_select(out=v, in_=v, compare_op=ALU.is_ge, fill=0.0, base=0 if causal else width - 1,
                       pattern=[[0, 4], [width, G], [1 if causal else 0, width]], channel_multiplier=-1).then_inc(sem, 1)


def head_mask(pool, m, heads, width, sem, n):
    pool.memset(m[:, :], 1.0).then_inc(sem, 1)
    pool.wait_ge(sem, n + 1)
    pool.affine_select(out=m[:, :], in_=m[:, :], compare_op=ALU.is_ge, fill=0.0, base=0,
                       pattern=[[-width, heads]], channel_multiplier=1).then_inc(sem, 1)
    pool.wait_ge(sem, n + 2)
    pool.affine_select(out=m[:, :], in_=m[:, :], compare_op=ALU.is_ge, fill=0.0, base=width - 1,
                       pattern=[[width, heads]], channel_multiplier=-1).then_inc(sem, 1)


def stage_gate(K, name, experts, route, xT, plan=None, weights=None):
    nc, ins = K.nc, K.ins
    E = experts
    with ExitStack() as ctx:
        sb = lambda n, shape, dt=F32: ctx.enter_context(nc.sbuf_tensor(name + n, shape, dt))
        wg = sb("wg", [P, DC, E])
        bias = sb("bias", [P, E])
        rev = sb("rev", [P, E])
        xn = sb("xn", [P, 2, D])
        xt = sb("xt", [P, 2, D])
        work = {n: sb(n, [P, NT, E]) for n in ("score", "left", "eq", "place", "sel1", "sel2")}
        one = {n: sb(n, [P, NT]) for n in ("top", "last", "sum", "rsum")}
        ps_x = [ctx.enter_context(nc.psum_tensor(f"{name}ps_x{b}", [P, 512], F32)) for b in range(2)]
        ps_g = ctx.enter_context(nc.psum_tensor(name + "ps_g", [P, 512], F32))
        ps_r = ctx.enter_context(nc.psum_tensor(name + "ps_r", [P, 512], F32))
        loaded, rev_set = K.sem(name + "loaded"), K.sem(name + "rev_set")
        norm = norm_sems(K, name)
        S = {n: K.sem(name + n) for n in
             "xn_ready xT_ps xt_ready g_ps kept exp_in exp_ready steps hi_ready lo_ready hiT_ready sel_ready rank_ps".split()}
        if plan:
            plan.allocate(sb)
            plan.sel = work["eq"]
        block = ctx.enter_context(nc.Block())

        @block.sync
        def _(sp):
            with nc.allow_non_contiguous_dma(reason="a gate of 8 columns, once"):
                sp.dma_start(wg[:, :, :], ins[name + "gate"].rearrange("(c p) e -> p c e", p=P)).then_inc(loaded, 16)
            if name + "gate_bias" in ins:
                sp.dma_start(bias[:, :], ins[name + "gate_bias"].partition_broadcast(P)).then_inc(loaded, 16)
            if weights:
                weights.load(sp, E1, 0)

        @block.gpsimd
        def _(pool):
            for e in range(E):
                last = pool.memset(rev[:, e:e + 1], float(E - e))
            last.then_inc(rev_set, 1)
            if plan:
                plan.constants(pool)

            def lows(a):
                pool.wait_ge(S["hiT_ready"], a.t + 1)
                K.hold(pool)
                pool.tensor_tensor(out=xT[:, 1, :, ds(a.t * P, P)], in0=xt[:, a.b, :].rearrange("p (c m) -> p c m", c=DC),
                                   in1=xT[:, 0, :, ds(a.t * P, P)], op=ALU.subtract).then_inc(S["kept"], 1)

            def keep(a):
                pool.wait_ge(S["xt_ready"], a.t + 1)
                K.hold(pool)
                src = xt[:, a.b, :].rearrange("p (c m) -> p c m", c=DC)
                pool.tensor_copy(out=xT[:, :, ds(a.t * P, P)], in_=src).then_inc(S["kept"], 1)
            over(pool, 0, NT, lows if plan else keep)
            if weights:
                weights.take_low(pool, 0, 0, 2, 1)

        @block.scalar
        def _(act):
            root_norm(K, act, norm)

            def take(a):
                act.wait_ge(S["xT_ps"], a.t + 1)
                wait(act, S["g_ps"], a.t - 1)
                wait(act, S["kept"], a.t - 1)
                act.activation(xt[:, a.b, :], ps_x[a.b][:, 0:D], ACT.Copy).then_inc(S["xt_ready"], 1)
                if plan:
                    act.activation(xT[:, 0, :, ds(a.t * P, P)], ps_x[a.b][:, 0:D].rearrange("p (c m) -> p c m", c=DC),
                                   ACT.Copy).then_inc(S["hiT_ready"], 1)
            def high(a):
                act.wait_ge(S["xn_ready"], a.t + 1)
                K.hold(act)
                act.activation(plan.rows[:, ds(a.t * 2 * D, D)], xn[:, a.b, :], ACT.Copy).then_inc(S["hi_ready"], 1)

            def step(a):
                if plan:
                    high(a)
                take(a)
            over(act, 0, NT, step)
            if weights:
                for kc in range(DC):
                    weights.take_high_up(act, 0, 2, 1, kc)
                weights.take_high_down(act, 0, 2)
            act.wait_ge(S["exp_in"], 1)
            act.activation(work["score"][:, :, :], work["score"][:, :, :], ACT.Exp).then_inc(S["exp_ready"], 1)

        @block.tensor
        def _(pe):
            pe.wait_ge(loaded, 16)

            def transposes(a):
                pe.wait_ge(S["xn_ready"], a.t + 1)
                wait(pe, S["hiT_ready" if plan else "xt_ready"], a.t - 1)
                for c in range(DC):
                    last = pe.transpose(ps_x[a.b][:, c * P:(c + 1) * P], xn[:, a.b, c * P:(c + 1) * P], K.ident[:, :])
                last.then_inc(S["xT_ps"], 1)

            def logits(a):
                pe.wait_ge(S["xt_ready"], a.t + 1)
                for c in range(DC):
                    last = pe.matmul(ps_g[:, ds(a.t * E, E)], xt[:, a.b, c * P:(c + 1) * P], wg[:, c, :],
                                     start=(c == 0), stop=(c == DC - 1))
                last.then_inc(S["g_ps"], 1)

            def step(a):
                transposes(a)
                logits(a.at(-1))
            transposes(tile(0))
            over(pe, 1, NT, step)
            logits(tile(NT - 1))
            if plan:
                plan.ranks(pe, ps_r, S)

        @block.vector
        def _(dve):
            chain = Chain(dve, S["steps"])
            prepare_norm(K, dve, norm)
            dve.wait_ge(loaded, 16 * (1 + (name + "gate_bias" in ins)))
            dve.wait_ge(rev_set, 1)

            def centre(a):
                wait(dve, S["xT_ps"], a.t - 1)
                if plan:
                    wait(dve, S["lo_ready"], a.t - 1)
                normalise(K, dve, a, xn[:, a.b, :]).then_inc(S["xn_ready"], 1)

            def low(a):
                dve.wait_ge(S["hi_ready"], a.t + 1)
                K.hold(dve)
                row = a.t * 2 * D
                dve.tensor_tensor(out=plan.rows[:, ds(row + D, D)], in0=xn[:, a.b, :], in1=plan.rows[:, ds(row, D)],
                                  op=ALU.subtract).then_inc(S["lo_ready"], 1)

            def step(a):
                centre(a)
                if plan and has(a, -1):
                    low(a.at(-1))
            over(dve, 0, NT, step)
            if plan:
                low(tile(NT - 1))
            dve.wait_ge(S["g_ps"], NT)
            logit = ps_g[:, 0:NT * E].rearrange("p (t e) -> p t e", t=NT)
            route(dve, chain, logit, bias, rev, work, one, S)
            if plan:
                plan.make(dve, chain, work, ps_r, S)


def per_token(m):
    t, e = NT, E0
    return m[:, :].rearrange("p (t a) -> p t a", a=1).broadcast_to([P, t, e])


def top_two(dve, chain, value, rev, work, one):
    left, eq, place = work["left"], work["eq"], work["place"]
    revs = rev[:, :].rearrange("p (a e) -> p a e", a=1).broadcast_to([P, NT, E0])
    for n, sel in enumerate((work["sel1"], work["sel2"])):
        src = value if n == 0 else left
        chain.done(dve.tensor_reduce(out=one["top"][:, :], in_=src[:, :, :], axis=AX, op=ALU.max))
        chain.done(dve.tensor_tensor(out=eq[:, :, :], in0=src[:, :, :], in1=per_token(one["top"]), op=ALU.is_ge))
        chain.done(dve.tensor_tensor(out=place[:, :, :], in0=eq[:, :, :], in1=revs, op=ALU.mult))
        chain.done(dve.tensor_reduce(out=one["last"][:, :], in_=place[:, :, :], axis=AX, op=ALU.max))
        chain.done(dve.tensor_tensor(out=sel[:, :, :], in0=place[:, :, :], in1=per_token(one["last"]), op=ALU.is_equal))
        if n == 0:
            chain.done(dve.scalar_tensor_tensor(out=left[:, :, :], in0=sel[:, :, :], scalar=-1e30, in1=value[:, :, :],
                                                op0=ALU.mult, op1=ALU.add))
    chain.done(dve.tensor_tensor(out=eq[:, :, :], in0=work["sel1"][:, :, :], in1=work["sel2"][:, :, :], op=ALU.add))
    return eq


def route0(gate):
    def route(dve, chain, logit, bias, rev, work, one, S):
        score, left = work["score"], work["sel2"]
        dve.tensor_scalar(out=score[:, :, :], in0=logit, scalar1=-1.0, scalar2=None, op0=ALU.mult).then_inc(S["exp_in"], 1)
        dve.wait_ge(S["exp_ready"], 1)
        chain.done(dve.tensor_scalar(out=left[:, :, :], in0=score[:, :, :], scalar1=1.0, scalar2=None, op0=ALU.add))
        chain.done(dve.reciprocal(score[:, :, :], left[:, :, :]))
        biased = work["left"]
        chain.done(dve.tensor_tensor(out=biased[:, :, :], in0=score[:, :, :],
                                     in1=bias[:, :].rearrange("p (a e) -> p a e", a=1).broadcast_to([P, NT, E0]), op=ALU.add))
        sel = top_two(dve, chain, biased, rev, work, one)
        dve.tensor_tensor(out=gate[:, :, :].rearrange("p e t -> p t e"), in0=score[:, :, :], in1=sel[:, :, :], op=ALU.mult)
    return route


def route1():
    def route(dve, chain, logit, bias, rev, work, one, S):
        score, prob = work["score"], work["left"]
        chain.done(dve.tensor_reduce(out=one["top"][:, :], in_=logit, axis=AX, op=ALU.max))
        dve.tensor_tensor(out=score[:, :, :], in0=logit, in1=per_token(one["top"]), op=ALU.subtract).then_inc(S["exp_in"], 1)
        dve.wait_ge(S["exp_ready"], 1)
        chain.done(dve.tensor_reduce(out=one["sum"][:, :], in_=score[:, :, :], axis=AX, op=ALU.add))
        chain.done(dve.reciprocal(one["rsum"][:, :], one["sum"][:, :]))
        chain.done(dve.tensor_tensor(out=prob[:, :, :], in0=score[:, :, :], in1=per_token(one["rsum"]), op=ALU.mult))
        chain.done(dve.tensor_copy(out=score[:, :, :], in_=prob[:, :, :]))
        sel = top_two(dve, chain, prob, rev, work, one)
        dve.sem_inc(S["sel_ready"], 1)
        chain.done(dve.tensor_tensor(out=work["place"][:, :, :], in0=score[:, :, :], in1=sel[:, :, :], op=ALU.mult))
        chain.done(dve.tensor_reduce(out=one["sum"][:, :], in_=work["place"][:, :, :], axis=AX, op=ALU.add))
        chain.done(dve.reciprocal(one["rsum"][:, :], one["sum"][:, :]))
        chain.done(dve.tensor_tensor(out=prob[:, :, :], in0=work["place"][:, :, :], in1=per_token(one["rsum"]), op=ALU.mult))
    return route


class Plan:

    def __init__(self, nc, ctx, K):
        sb = lambda n, shape, dt=F32: ctx.enter_context(nc.sbuf_tensor("plan_" + n, shape, dt))
        self.rows = sb("rows", [P, NT * 2 * D], BF16)
        self.slot = sb("slot", [P, 2 * NT], mybir.dt.uint32)
        self.weight = sb("weight", [P, 2 * NT])
        self.expert = sb("expert", [P, NB], mybir.dt.int32)
        self.ready = K.sem("plan_constants")

    def allocate(self, sb):
        self.before = sb("before", [P, P])
        self.ones = sb("ones", [P, P])
        self.index = sb("index", [P, NB])
        self.edge = sb("edge", [P, TOK // SB])
        self.total = sb("total", [P, NT, E1])
        self.run = sb("run", [P, NT + 1, E1])
        self.over = sb("over", [P, E1, TOK // SB])
        self.blocks = sb("blocks", [P, E1])
        self.first = sb("first", [P, E1 + 1])
        self.place = sb("place2", [P, NT, E1])
        self.slotf = sb("slotf", [P, 2, NT])
        self.past = sb("past", [P, NB, E1])
        self.expertf = sb("expertf", [P, NB])

    def constants(self, pool):
        pool.memset(self.ones[:, :], 1.0).then_inc(self.ready, 1)
        pool.wait_ge(self.ready, 1)
        pool.affine_select(out=self.before[:, :], in_=self.ones[:, :], compare_op=ALU.is_gt, fill=0.0, base=0,
                           pattern=[[1, P]], channel_multiplier=-1)
        for j in range(NB):
            pool.memset(self.index[:, j:j + 1], float(j))
        for j in range(TOK // SB):
            last = pool.memset(self.edge[:, j:j + 1], float(j * SB))
        last.then_inc(self.ready, 1)

    def ranks(self, pe, ps_r, S):
        pe.wait_ge(self.ready, 2)
        pe.wait_ge(S["sel_ready"], 1)
        sel = self.sel[:, :, :].rearrange("p t e -> p (t e)")
        pe.matmul(ps_r[:, 0:NT * E1], self.before[:, :], sel, start=True, stop=True)
        pe.matmul(ps_r[:, NT * E1:2 * NT * E1], self.ones[:, :], sel, start=True, stop=True).then_inc(S["rank_ps"], 1)

    def make(self, dve, chain, work, ps_r, S):
        dve.wait_ge(S["rank_ps"], 1)
        dve.wait_ge(self.ready, 2)
        rank = ps_r[:, 0:NT * E1].rearrange("p (t e) -> p t e", t=NT)
        chain.done(dve.tensor_copy(out=self.total[:, :, :], in_=ps_r[:, NT * E1:2 * NT * E1].rearrange("p (t e) -> p t e", t=NT)))
        chain.done(dve.memset(self.run[:, 0, :], 0.0))
        for t in range(NT):
            chain.done(dve.tensor_tensor(out=self.run[:, t + 1, :], in0=self.run[:, t, :], in1=self.total[:, t, :], op=ALU.add))
        J = TOK // SB
        chain.done(dve.tensor_tensor(out=self.over[:, :, :], in0=self.run[:, NT, :].rearrange("p (e a) -> p e a", a=1).broadcast_to([P, E1, J]),
                                     in1=self.edge[:, :].rearrange("p (a j) -> p a j", a=1).broadcast_to([P, E1, J]), op=ALU.is_gt))
        chain.done(dve.tensor_reduce(out=self.blocks[:, :], in_=self.over[:, :, :], axis=AX, op=ALU.add))
        chain.done(dve.memset(self.first[:, 0:1], 0.0))
        for e in range(E1):
            chain.done(dve.tensor_tensor(out=self.first[:, e + 1:e + 2], in0=self.first[:, e:e + 1], in1=self.blocks[:, e:e + 1], op=ALU.add))
        firsts = self.first[:, 0:E1].rearrange("p (a e) -> p a e", a=1).broadcast_to([P, NT, E1])
        chain.done(dve.scalar_tensor_tensor(out=self.place[:, :, :], in0=firsts, scalar=float(SB), in1=self.run[:, 0:NT, :],
                                            op0=ALU.mult, op1=ALU.add))
        chain.done(dve.tensor_tensor(out=self.place[:, :, :], in0=rank, in1=self.place[:, :, :], op=ALU.add))
        for k, sel in enumerate((work["sel1"], work["sel2"])):
            chain.done(dve.tensor_tensor(out=work["place"][:, :, :], in0=sel[:, :, :], in1=self.place[:, :, :], op=ALU.mult))
            chain.done(dve.tensor_reduce(out=self.slotf[:, k, :], in_=work["place"][:, :, :], axis=AX, op=ALU.add))
            chain.done(dve.tensor_tensor(out=work["place"][:, :, :], in0=sel[:, :, :], in1=work["left"][:, :, :], op=ALU.mult))
            chain.done(dve.tensor_reduce(out=self.weight[:, k * NT:(k + 1) * NT], in_=work["place"][:, :, :], axis=AX, op=ALU.add))
        dve.tensor_copy(out=self.slot[:, :], in_=self.slotf[:, :, :].rearrange("p k t -> p (k t)"))
        chain.done(dve.tensor_tensor(out=self.past[:, :, :], in0=self.index[:, :].rearrange("p (n a) -> p n a", a=1).broadcast_to([P, NB, E1]),
                                     in1=self.first[:, 1:E1 + 1].rearrange("p (a e) -> p a e", a=1).broadcast_to([P, NB, E1]), op=ALU.is_ge))
        chain.done(dve.tensor_reduce(out=self.expertf[:, :], in_=self.past[:, :, :], axis=AX, op=ALU.add))
        dve.tensor_scalar(out=self.expert[:, :], in0=self.expertf[:, :], scalar1=float(E1 - 1), scalar2=None, op0=ALU.min)


class ExpertWeights:
    UP, DOWN = W1, W1 + HF1 * D
    WORDS = W1 + HF1 * D + D

    def __init__(self, nc, ctx, K):
        self.ins = K.ins
        self.f = ctx.enter_context(nc.sbuf_tensor("w1_f", [P, 2, self.WORDS], F32))
        self.b = ctx.enter_context(nc.sbuf_tensor("w1_b", [P, 3, 2, self.WORDS], BF16))
        self.loaded = [K.sem(f"w1_loaded{s}") for s in range(2)]
        self.high_up, self.high_down, self.low_up, self.low_down = (K.sem("w1_" + n) for n in ("high_up", "high_down", "low_up", "low_down"))
        self.hold = K.hold

    def load(self, eng, expert, s):
        f, up, down, words = self.f, self.UP, self.DOWN, self.WORDS
        eng.dma_start(f[:, s, 0:up], self.ins["f1_up"][ds(expert * P, P), :]).then_inc(self.loaded[s], 16)
        eng.dma_start(f[:, s, up:down], self.ins["f1_down"][ds(expert * P, P), :]).then_inc(self.loaded[s], 16)
        eng.dma_start(f[0:HT1, s, down:words], self.ins["f1_rest"][ds(expert * HT1, HT1), :]).then_inc(self.loaded[s], 16)

    def take_high_up(self, act, s, slot, rounds, kc):
        act.wait_ge(self.loaded[s], rounds * 48)
        w0, w1 = kc * 2 * HID1, (kc + 1) * 2 * HID1
        ins = act.activation(self.b[:, slot, 0, w0:w1], self.f[:, s, w0:w1], ACT.Copy)
        if kc == DC - 1:
            ins.then_inc(self.high_up, 1)

    def take_high_down(self, act, s, slot):
        f, b, up, down, words = self.f, self.b, self.UP, self.DOWN, self.WORDS
        act.activation(b[:, slot, 0, up:down], f[:, s, up:down], ACT.Copy)
        act.activation(b[0:HT1, slot, 0, down:words], f[0:HT1, s, down:words], ACT.Copy).then_inc(self.high_down, 1)

    def take_low(self, pool, use, s, slot, rounds):
        f, b, up, down, words = self.f, self.b, self.UP, self.DOWN, self.WORDS
        pool.wait_ge(self.loaded[s], rounds * 48)
        pool.wait_ge(self.high_up, use + 1)
        self.hold(pool)
        pool.tensor_tensor(out=b[:, slot, 1, 0:up], in0=f[:, s, 0:up], in1=b[:, slot, 0, 0:up], op=ALU.subtract).then_inc(self.low_up, 1)
        pool.wait_ge(self.high_down, use + 1)
        self.hold(pool)
        pool.tensor_tensor(out=b[:, slot, 1, up:down], in0=f[:, s, up:down], in1=b[:, slot, 0, up:down], op=ALU.subtract)
        pool.tensor_tensor(out=b[0:HT1, slot, 1, down:words], in0=f[0:HT1, s, down:words], in1=b[0:HT1, slot, 0, down:words],
                           op=ALU.subtract).then_inc(self.low_down, 1)


def stage_experts0(K, xT, gate):
    nc, ins = K.nc, K.ins
    HB = chunks(HID0)
    NH = len(HB)
    NO = TPG // 2
    with ExitStack() as ctx:
        sb = lambda n, shape, dt=F32: ctx.enter_context(nc.sbuf_tensor("e_" + n, shape, dt))
        wu_f, wd_f = sb("wu_f", [P, 2, DC, HID0]), sb("wd_f", [P, 2, NH, D])
        wu, wd = sb("wu", [P, 2, DC, HID0], BF16), sb("wd", [P, 2, NH, D], BF16)
        gT = sb("gT", [P, P])
        grow = sb("grow", [P, 2, TOK])
        xe = sb("xe", [P, 2, DC, GT], BF16)
        pos = sb("pos", [P, 4, GT], BF16)
        hid = sb("hid", [P, 2, NH, GT], BF16)
        rnd = sb("rnd", [P, 4, 2 * D], BF16)
        ps = lambda n: ctx.enter_context(nc.psum_tensor("e_" + n, [P, 512], F32))
        ps_u = [ps(f"u{b}") for b in range(4)]
        ps_d = [ps(f"d{b}") for b in range(4)]
        gates = nc.dram_tensor("gates", (E0, TOK), F32).ap()
        loaded = [K.sem(f"e_loaded{b}") for b in range(2)]
        grow_loaded = [K.sem(f"e_grow_loaded{b}") for b in range(2)]
        S = {n: K.sem("e_" + n) for n in
             "gT_ps gT_ready gates_stored cast_up cast xe_ready up_ps relu_ready hid_ready down_ps rnd_ready added".split()}
        block = ctx.enter_context(nc.Block())

        def units(eng, step):
            over(eng, 0, E0 * NG, step, per=2 * NG)

        @block.sync
        def _(sp):
            sp.wait_ge(S["gT_ready"], 1)
            sp.dma_start(gates.rearrange("e (t m) -> (e t) m", t=NT), gT[:, :]).then_inc(S["gates_stored"], 16)
            sp.wait_ge(S["gates_stored"], 16)

            def load(e):
                wait(sp, S["xe_ready"], (e.t - 1) * NG)
                sp.dma_start(grow[:, e.b, :], gates[ds(e.t, 1), :].rearrange("a m -> (a m)").partition_broadcast(P)).then_inc(grow_loaded[e.b], 16)
                wait(sp, S["cast"], e.t - 1)
                last = HB[-1][1]
                for dst, src in ((wu_f[:, e.b, :, :], ins["f0_up"][ds(e.t * D, D), :].rearrange("(c p) n -> p c n", p=P)),
                                 (wd_f[:, e.b, 0:NH - 1, :], ins["f0_down"][ds(e.t * HID0, (NH - 1) * P), :].rearrange("(c p) n -> p c n", p=P)),
                                 (wd_f[0:last, e.b, NH - 1, :], ins["f0_down"][ds(e.t * HID0 + (NH - 1) * P, last), :])):
                    sp.dma_start(dst, src).then_inc(loaded[e.b], 16)
            over(sp, 0, E0, load)

        @block.gpsimd
        def _(pool):
            def cast(eb, rounds, units_before):
                pool.wait_ge(loaded[eb], rounds * 48)
                wait(pool, S["down_ps"], units_before * NO)
                K.hold(pool)
                last = HB[-1][1]
                pool.tensor_copy(out=wu[:, eb, :, :], in_=wu_f[:, eb, :, :]).then_inc(S["cast_up"], 1)
                pool.tensor_copy(out=wd[:, eb, 0:NH - 1, :], in_=wd_f[:, eb, 0:NH - 1, :])
                pool.tensor_copy(out=wd[0:last, eb, NH - 1, :], in_=wd_f[0:last, eb, NH - 1, :]).then_inc(S["cast"], 1)

            def step(n):
                eb, g = n.k // NG, n.k % NG
                if not (isinstance(n.t, int) and n.t == 0):
                    add(n.at(-1))
                if g == 2 and not (isinstance(n.t, int) and n.t == E0 * NG - 2):
                    cast(1 - eb, n.turn + 1 + eb, n.t - 2)

            def add(n):
                g = n.k % NG
                for j in range(NO):
                    q, t = n.t * NO + j, g * TPG + 2 * j
                    pool.wait_ge(S["rnd_ready"], q + 1)
                    wait(pool, S["added"], q - NG * NO + 1)
                    hs = K.h[:, t * D:(t + 2) * D]
                    pool.tensor_tensor(out=hs, in0=hs, in1=rnd[:, (n.k * NO + j) % 4, :], op=ALU.add).then_inc(S["added"], 1)
            cast(0, 1, 0)
            over(pool, 0, (E0 - 2) * NG, step, per=2 * NG)
            for n in range((E0 - 2) * NG, E0 * NG):
                step(tile(n, 2 * NG))
            add(tile(E0 * NG - 1, 2 * NG))

        @block.tensor
        def _(pe):
            pe.transpose(ps_d[0][:, 0:P], gate[:, :, :].rearrange("p e t -> p (e t)"), K.ident[:, :]).then_inc(S["gT_ps"], 1)

            def up(n):
                eb, g = n.k // NG, n.k % NG
                if g == 0:
                    pe.wait_ge(S["cast_up"], n.turn * 2 + eb + 1)
                pe.wait_ge(S["xe_ready"], n.t + 1)
                for c, (m, w) in enumerate(HB):
                    q = n.t * NH + c
                    wait(pe, S["relu_ready"], q - 3)
                    for kc in range(DC):
                        last = pe.matmul(ps_u[(n.k * NH + c) % 4][0:w, :], wu[:, eb, kc, m * P:m * P + w], xe[:, n.b, kc, :],
                                         start=(kc == 0), stop=(kc == DC - 1))
                    last.then_inc(S["up_ps"], 1)

            def down(n):
                eb, g = n.k // NG, n.k % NG
                if g == 0:
                    pe.wait_ge(S["cast"], n.turn * 2 + eb + 1)
                pe.wait_ge(S["hid_ready"], n.t * NH + NH)
                for j in range(NO):
                    wait(pe, S["rnd_ready"], n.t * NO + j - 3)
                    for i in range(2):
                        for c, (m, w) in enumerate(HB):
                            last = pe.matmul(ps_d[(n.k * NO + j) % 4][:, i * D:(i + 1) * D],
                                             hid[0:w, n.b, c, (2 * j + i) * P:(2 * j + i + 1) * P], wd[0:w, eb, c, :],
                                             start=(c == 0), stop=(c == NH - 1))
                    last.then_inc(S["down_ps"], 1)

            def step(n):
                up(n)
                if not (isinstance(n.t, int) and n.t == 0):
                    down(n.at(-1))
            units(pe, step)
            down(tile(E0 * NG - 1, 2 * NG))

        @block.scalar
        def _(act):
            act.wait_ge(S["gT_ps"], 1)
            act.activation(gT[:, :], ps_d[0][:, 0:P], ACT.Copy).then_inc(S["gT_ready"], 1)

            def relus(n):
                for c, (m, w) in enumerate(HB):
                    q, slot = n.t * NH + c, (n.k * NH + c) % 4
                    act.wait_ge(S["up_ps"], q + 1)
                    wait(act, S["hid_ready"], q - 3)
                    act.activation(pos[0:w, slot, :], ps_u[slot][0:w, :], ACT.Relu).then_inc(S["relu_ready"], 1)

            def rounds(n):
                for j in range(NO):
                    q, slot = n.t * NO + j, (n.k * NO + j) % 4
                    act.wait_ge(S["down_ps"], q + 1)
                    wait(act, S["added"], q - 3)
                    act.activation(rnd[:, slot, :], ps_d[slot][:, :], ACT.Copy).then_inc(S["rnd_ready"], 1)

            def step(n):
                relus(n)
                if not (isinstance(n.t, int) and n.t == 0):
                    rounds(n.at(-1))
            units(act, step)
            rounds(tile(E0 * NG - 1, 2 * NG))

        @block.vector
        def _(dve):
            def scale(n):
                eb, g = n.k // NG, n.k % NG
                if g == 0:
                    dve.wait_ge(grow_loaded[eb], n.turn * 16 + 16)
                wait(dve, S["up_ps"], (n.t - 1) * NH)
                dve.tensor_tensor(out=xe[:, n.b, :, :], in0=xT[:, :, g * GT:(g + 1) * GT],
                                  in1=grow[:, eb:eb + 1, g * GT:(g + 1) * GT].broadcast_to([P, DC, GT]),
                                  op=ALU.mult).then_inc(S["xe_ready"], 1)

            def square(n):
                for c, (m, w) in enumerate(HB):
                    q, slot = n.t * NH + c, (n.k * NH + c) % 4
                    dve.wait_ge(S["relu_ready"], q + 1)
                    if c == 0:
                        wait(dve, S["down_ps"], (n.t - 1) * NO)
                    dve.tensor_tensor(out=hid[0:w, n.b, c, :], in0=pos[0:w, slot, :], in1=pos[0:w, slot, :],
                                      op=ALU.mult).then_inc(S["hid_ready"], 1)

            def step(n):
                scale(n)
                if not (isinstance(n.t, int) and n.t == 0):
                    square(n.at(-1))
            units(dve, step)
            square(tile(E0 * NG - 1, 2 * NG))


def stage_shared0(K, xT):
    nc, ins = K.nc, K.ins
    HB = chunks(HID0)
    NH = len(HB)
    with ExitStack() as ctx:
        sb = lambda n, shape, dt=F32: ctx.enter_context(nc.sbuf_tensor("s_" + n, shape, dt))
        wu, wd = sb("wu", [P, DC, HID0]), sb("wd", [P, NH, D])
        pos = sb("pos", [P, 4, GT])
        hid = sb("hid", [P, 2, NH, GT])
        ps = lambda n: ctx.enter_context(nc.psum_tensor("s_" + n, [P, 512], F32))
        ps_u = [ps(f"u{b}") for b in range(4)]
        ps_d = [ps(f"d{b}") for b in range(TPG)]
        S = {n: K.sem("s_" + n) for n in "loaded up_ps relu_ready hid_ready down_ps added".split()}
        block = ctx.enter_context(nc.Block())

        @block.sync
        def _(sp):
            last = HB[-1][1]
            sp.dma_start(wu[:, :, :], ins["f0_shared_up"].rearrange("(c p) n -> p c n", p=P)).then_inc(S["loaded"], 16)
            sp.dma_start(wd[:, 0:NH - 1, :], ins["f0_shared_down"][0:(NH - 1) * P, :].rearrange("(c p) n -> p c n", p=P)).then_inc(S["loaded"], 16)
            sp.dma_start(wd[0:last, NH - 1, :], ins["f0_shared_down"][(NH - 1) * P:HID0, :]).then_inc(S["loaded"], 16)

        @block.tensor
        def _(pe):
            pe.wait_ge(S["loaded"], 48)

            def up(g):
                for c, (m, w) in enumerate(HB):
                    q = g * NH + c
                    wait(pe, S["relu_ready"], q - 3)
                    for kc in range(DC):
                        last = pe.matmul(ps_u[q % 4][0:w, :], wu[:, kc, m * P:m * P + w], xT[:, kc, g * GT:(g + 1) * GT],
                                         start=(kc == 0), stop=(kc == DC - 1))
                    last.then_inc(S["up_ps"], 1)

            def down(g):
                pe.wait_ge(S["hid_ready"], g * NH + NH)
                for j in range(TPG):
                    wait(pe, S["added"], g * TPG + j - 3)
                    for c, (m, w) in enumerate(HB):
                        last = pe.matmul(ps_d[j][:, 0:D], hid[0:w, g % 2, c, j * P:(j + 1) * P], wd[0:w, c, :],
                                         start=(c == 0), stop=(c == NH - 1))
                    last.then_inc(S["down_ps"], 1)
            up(0)
            for g in range(1, NG):
                up(g)
                down(g - 1)
            down(NG - 1)

        @block.scalar
        def _(act):
            for g in range(NG):
                for c, (m, w) in enumerate(HB):
                    q = g * NH + c
                    act.wait_ge(S["up_ps"], q + 1)
                    wait(act, S["hid_ready"], q - 3)
                    act.activation(pos[0:w, q % 4, :], ps_u[q % 4][0:w, :], ACT.Relu).then_inc(S["relu_ready"], 1)

        @block.vector
        def _(dve):
            def square(g):
                for c, (m, w) in enumerate(HB):
                    q = g * NH + c
                    dve.wait_ge(S["relu_ready"], q + 1)
                    if c == 0:
                        wait(dve, S["down_ps"], (g - 1) * TPG)
                    dve.tensor_tensor(out=hid[0:w, g % 2, c, :], in0=pos[0:w, q % 4, :], in1=pos[0:w, q % 4, :],
                                      op=ALU.mult).then_inc(S["hid_ready"], 1)

            def add(g):
                for j in range(TPG):
                    t = g * TPG + j
                    dve.wait_ge(S["down_ps"], t + 1)
                    hs = K.h[:, t * D:(t + 1) * D]
                    dve.tensor_tensor(out=hs, in0=ps_d[j][:, 0:D], in1=hs, op=ALU.add).then_inc(S["added"], 1)
                    dve.wait_ge(S["added"], t + 1)
                    dve.bn_stats(out=K.moments[:, t * 6:t * 6 + 6], in_=hs)
            square(0)
            for g in range(1, NG):
                square(g)
                add(g - 1)
            add(NG - 1)


def stage_fused_weights(K, wf):
    nc, ins = K.nc, K.ins
    with ExitStack() as ctx:
        sb = lambda n, shape, dt=F32: ctx.enter_context(nc.sbuf_tensor("w_" + n, shape, dt))
        wT = sb("wT", [D1, 2, H1, D])
        kk = sb("kk", [D1, 2, H1, F1])
        ps = [ctx.enter_context(nc.psum_tensor(f"w_ps{b}", [P, 512], F32)) for b in range(2)]
        loaded, ps_ready, read = K.sem("w_loaded"), K.sem("w_ps_ready"), K.sem("w_read")
        block = ctx.enter_context(nc.Block())
        HB = 512 // F1
        banks = [(j, c, hb) for j in range(2) for c in range(DC) for hb in range(H1 // HB)]

        @block.sync
        def _(sp):
            for j, n in enumerate("qk"):
                sp.dma_start(wT[:, j, :, :], ins[f"a1_w{n}T"].rearrange("(h p) d -> p h d", p=D1)).then_inc(loaded, 16)
                sp.dma_start(kk[:, j, :, :], ins[f"a1_k{n}"].rearrange("h p f -> p h f")).then_inc(loaded, 16)

        @block.tensor
        def _(pe):
            pe.wait_ge(loaded, 64)
            for n, (j, c, hb) in enumerate(banks):
                wait(pe, read, n - 1)
                for i in range(HB):
                    hd = hb * HB + i
                    last = pe.matmul(ps[n % 2][:, i * F1:(i + 1) * F1], wT[:, j, hd, c * P:(c + 1) * P], kk[:, j, hd, :],
                                     start=True, stop=True)
                last.then_inc(ps_ready, 1)

        @block.scalar
        def _(act):
            for n, (j, c, hb) in enumerate(banks):
                act.wait_ge(ps_ready, n + 1)
                act.activation(wf[:, j, c, hb * 512:(hb + 1) * 512], ps[n % 2][:, :], ACT.Copy).then_inc(read, 1)


def stage_attention1(K, wf, slots):
    nc, ins = K.nc, K.ins
    W = H1 * D1
    VW = D1 + 1
    FT = 2 * F1
    G, HG = 4, 4
    YC = W // P
    with ExitStack() as ctx:
        sb = lambda n, shape, dt=F32: ctx.enter_context(nc.sbuf_tensor("b_" + n, shape, dt))
        wv, wo = sb("wv", [P, DC, W]), sb("wo", [P, YC, D])
        causal = sb("causal", [P, 4, P])
        xn, xT = sb("xn", [P, 2, D]), sb("xT", [P, 2, D])
        feat = sb("feat", [P, 4, H1, 2, F1])
        ext = sb("ext", [P, 4, 2, H1])
        fsum = sb("fsum", [P, 4, H1 * 2])
        frec = sb("frec", [P, 4, H1 * 2])
        v = sb("v", [P, 2, H1, VW])
        fT = sb("fT", [P, 2, 2, HG, P])
        sc = sb("sc", [P, 2, HG, P])
        den, rden = sb("den", [P, 2, HG]), sb("rden", [P, 2, HG])
        y, yT = sb("y", [P, 2, W]), sb("yT", [P, 2, W])
        ps = lambda n: ctx.enter_context(nc.psum_tensor("b_ps_" + n, [P, 512], F32))
        ps_f = [ctx.enter_context(nc.psum_tensor(f"b_ps_f{b}", [P, 1024], F32)) for b in range(2)]
        ps_t = [ps(f"t{b}") for b in range(2)]
        ps_s, ps_o = ps("s"), ps("o")
        loaded, mask, ones_set = K.sem("b_loaded"), K.sem("b_mask"), K.sem("b_ones_set")
        norm = norm_sems(K, "b")
        names = ("xn_ready f_ps f_read ext_ready shift_ready exp_ready rec_ready mul_ready feat_ready v_ready "
                 "t_ps t_read s_ps s_ready o_ps o_read y_ready w_ps h_ready steps").split()
        S = {n: K.sem("b_" + n) for n in names}
        block = ctx.enter_context(nc.Block())
        @block.sync
        def _(sp):
            sp.dma_start(wv[:, :, :], ins["a1_wv"].rearrange("(c p) n -> p c n", p=P)).then_inc(loaded, 16)
            sp.dma_start(wo[:, :, :], ins["a1_wo"].rearrange("(c p) n -> p c n", p=P)).then_inc(loaded, 16)
            sp.dma_start(slots.rearrange("(n p) m -> p n m", p=P),
                         K.zero[:, :].rearrange("p (a m) -> p a m", a=1).broadcast_to([P, NB * SB // P, 2 * D])).then_inc(K.slots_cleared, 16)

        THROUGH = [("f00", -1), ("f01", -1), ("y0", -2), ("y1", -2), ("f10", -1), ("f11", -1),
                   ("f20", -1), ("f21", -1), ("f30", -1), ("f31", -1), ("x", 1)]

        def use(a, name):
            slot = [n for n, d in THROUGH].index(name)
            count = lambda p: 1 + sum(0 <= q + d < NT for q in range(p + 1) for d in [d for n, d in THROUGH][:slot if q == p else None])
            first = 1
            if isinstance(a.t, int):
                n = count(a.t) + first
                return n, (n - 1) % 2
            rest = count(4) + first - 4 * len(THROUGH)
            return a.t * len(THROUGH) + rest, (a.k * len(THROUGH) + rest - 1) % 2

        @block.gpsimd
        def _(pool):
            batch_mask(pool, causal, NPOS, mask, causal=True)
            pool.memset(v[:, :, :, D1:VW], 1.0).then_inc(ones_set, 1)

            def scale(a):
                for j in range(2):
                    s = a.b * 2 + j
                    pool.wait_ge(S["rec_ready"], a.t * 2 + j + 1)
                    f = feat[:, s, :, :, :].rearrange("p h s f -> p (h s) f")
                    pool.tensor_tensor(out=f, in0=f, in1=frec[:, s, :].rearrange("p (h a) -> p h a", a=1).broadcast_to([P, 2 * H1, F1]),
                                       op=ALU.mult).then_inc(S["mul_ready"], 1)
            over(pool, 0, NT, scale)

        @block.scalar
        def _(act):
            root_norm(K, act, norm)

            def tokens(a, n, b):
                act.wait_ge(S["t_ps"], n)
                wait(act, S["f_ps"], (a.t - 1) * 3)
                act.activation(xT[:, a.b, :], ps_t[b][:, 0:D], ACT.Copy).then_inc(S["t_read"], 1)

            def exponential(a, j):
                act.wait_ge(S["shift_ready"], a.t * 2 + j + 1)
                act.activation(feat[:, a.b * 2 + j, :, :, :], feat[:, a.b * 2 + j, :, :, :], ACT.Exp).then_inc(S["exp_ready"], 1)

            def values(a):
                act.wait_ge(S["f_ps"], a.t * 3 + 3)
                wait(act, S["o_ps"], (a.t - 1) * G)
                act.activation(v[:, a.b, :, 0:D1], ps_f[(a.k * 3 + 2) % 2][:, :].rearrange("p (h e) -> p h e", h=H1),
                               ACT.Copy).then_inc(S["v_ready"], 1)

            def features(p, g):
                a = p.at(-1)
                for j in range(2):
                    n, b = use(p, f"f{g}{j}")
                    act.wait_ge(S["t_ps"], n)
                    wait(act, S["s_ps"], a.t * G + g - 1)
                    act.activation(fT[:, g % 2, j, :, :], ps_t[b][:, :].rearrange("p (h m) -> p h m", h=HG),
                                   ACT.Copy).then_inc(S["t_read"], 1)

            def outputs(p):
                a = p.at(-2)
                for j in range(2):
                    n, b = use(p, f"y{j}")
                    act.wait_ge(S["t_ps"], n)
                    wait(act, S["w_ps"], a.t - 1)
                    act.activation(yT[:, a.b, j * 512:(j + 1) * 512], ps_t[b][:, :], ACT.Copy).then_inc(S["t_read"], 1)

            def step(p):
                now, before, done = has(p, 0), has(p, -1), has(p, -2)
                if before:
                    features(p, 0)
                if now:
                    exponential(p, 0)
                if done:
                    outputs(p)
                if before:
                    features(p, 1)
                if now:
                    exponential(p, 1)
                    values(p)
                if before:
                    features(p, 2)
                    features(p, 3)
                if has(p, 1):
                    tokens(p.at(1), *use(p, "x"))
            tokens(tile(0), 1, 0)
            passes(act, step)

        @block.tensor
        def _(pe):
            pe.wait_ge(loaded, 32)

            def free_t(count):
                wait(pe, S["t_read"], count - 2)

            def tokens(a, n, b):
                pe.wait_ge(S["xn_ready"], a.t + 1)
                free_t(n)
                for c in range(DC):
                    last = pe.transpose(ps_t[b][:, c * P:(c + 1) * P], xn[:, a.b, c * P:(c + 1) * P], K.ident[:, :])
                last.then_inc(S["t_ps"], 1)

            def project(a, j):
                if j == 2:
                    pe.wait_ge(S["f_read"], a.t * 2 + 1)
                elif j == 0:
                    wait(pe, S["f_read"], a.t * 2)
                else:
                    wait(pe, S["v_ready"], a.t)
                out = ps_f[(a.k * 3 + j) % 2]
                for half in range(2):
                    for c in range(DC):
                        rhs = wv[:, c, half * 512:(half + 1) * 512] if j == 2 else wf[:, j, c, half * 512:(half + 1) * 512]
                        last = pe.matmul(out[:, half * 512:(half + 1) * 512], xT[:, a.b, c * P:(c + 1) * P], rhs,
                                         start=(c == 0), stop=(c == DC - 1))
                last.then_inc(S["f_ps"], 1)

            def features(p, g):
                a = p.at(-1)
                for j in range(2):
                    n, b = use(p, f"f{g}{j}")
                    free_t(n)
                    for i in range(HG):
                        last = pe.transpose(ps_t[b][:, i * P:(i + 1) * P],
                                            feat[:, a.b * 2 + j, g * HG + i, :, :].rearrange("p s f -> p (s f)"), K.ident[:, :])
                    last.then_inc(S["t_ps"], 1)

            def scores(p, g):
                a = p.at(-1)
                pe.wait_ge(S["t_read"], use(p, f"f{g}1")[0])
                wait(pe, S["s_ready"], a.t * G + g)
                for i in range(HG):
                    last = pe.matmul(ps_s[:, i * P:(i + 1) * P], fT[:, g % 2, 1, i, :], fT[:, g % 2, 0, i, :], start=True, stop=True)
                last.then_inc(S["s_ps"], 1)

            def values(a, g):
                pe.wait_ge(S["s_ready"], a.t * G + g + 1)
                wait(pe, S["o_read"], a.t * G + g)
                if g == 0:
                    wait(pe, S["h_ready"], a.t)
                for i in range(HG):
                    last = pe.matmul(ps_o[:, i * VW:(i + 1) * VW], sc[:, g % 2, i, :], v[:, a.b, g * HG + i, :], start=True, stop=True)
                last.then_inc(S["o_ps"], 1)

            def outputs(p):
                a = p.at(-2)
                pe.wait_ge(S["y_ready"], a.t * G + G)
                for j in range(2):
                    n, b = use(p, f"y{j}")
                    free_t(n)
                    for i in range(4):
                        last = pe.transpose(ps_t[b][:, i * P:(i + 1) * P], y[:, a.b, (j * 4 + i) * P:(j * 4 + i + 1) * P], K.ident[:, :])
                    last.then_inc(S["t_ps"], 1)

            def combine(p):
                a = p.at(-2)
                pe.wait_ge(S["t_read"], use(p, "y1")[0])
                pe.wait_ge(S["o_read"], a.t * G + G)
                for c in range(YC):
                    last = pe.matmul(ps_o[:, 0:D], yT[:, a.b, c * P:(c + 1) * P], wo[:, c, :], start=(c == 0), stop=(c == YC - 1))
                last.then_inc(S["w_ps"], 1)

            def step(p):
                now, before, done = has(p, 0), has(p, -1), has(p, -2)
                a = p.at(-1)
                if now:
                    n = use(p.at(-1), "x")[0] if not isinstance(p.t, int) or p.t > 0 else 1
                    pe.wait_ge(S["t_read"], n)
                    project(p, 0)
                if done:
                    values(p.at(-2), G - 1)
                if before:
                    pe.wait_ge(S["feat_ready"], a.t * 2 + 2)
                    features(p, 0)
                    scores(p, 0)
                if now:
                    project(p, 1)
                if done:
                    outputs(p)
                if before:
                    features(p, 1)
                    scores(p, 1)
                if done:
                    combine(p)
                if now:
                    project(p, 2)
                if before:
                    pe.wait_ge(S["v_ready"], a.t + 1)
                    values(a, 0)
                    features(p, 2)
                    scores(p, 2)
                    values(a, 1)
                    features(p, 3)
                    scores(p, 3)
                    values(a, 2)
                if has(p, 1):
                    tokens(p.at(1), *use(p, "x"))
            tokens(tile(0), 1, 0)
            passes(pe, step)

        @block.vector
        def _(dve):
            chain = Chain(dve, S["steps"])
            chain2 = Chain(dve, K.sem("b_steps2"))
            prepare_norm(K, dve, norm)
            dve.wait_ge(mask, 3)
            dve.wait_ge(ones_set, 1)

            def tokens(a):
                wait(dve, S["f_ps"], (a.t - 1) * 3)
                normalise(K, dve, a, xn[:, a.b, :]).then_inc(S["xn_ready"], 1)

            def shifted(a, j):
                s, n = a.b * 2 + j, a.t * 2 + j
                f = ps_f[(a.k * 3 + j) % 2][:, :].rearrange("p (h f) -> p h f", h=H1)
                bc = lambda m: ext[:, s, m, :].rearrange("p (h a) -> p h a", a=1).broadcast_to([P, H1, F1])
                dve.wait_ge(S["f_ps"], a.t * 3 + j + 1)
                dve.tensor_reduce(out=ext[:, s, 0, :], in_=f, axis=AX, op=ALU.max)
                dve.tensor_reduce(out=ext[:, s, 1, :], in_=f, axis=AX, op=ALU.min).then_inc(S["ext_ready"], 1)
                dve.wait_ge(S["ext_ready"], n + 1)
                wait(dve, S["s_ps"], (a.t - 1) * G)
                dve.tensor_tensor(out=feat[:, s, :, 0, :], in0=f, in1=bc(0), op=ALU.subtract)
                dve.tensor_tensor(out=feat[:, s, :, 1, :], in0=bc(1), in1=f, op=ALU.subtract).then_inc(S["shift_ready"], 1)
                dve.wait_ge(S["shift_ready"], n + 1)
                dve.sem_inc(S["f_read"], 1)

            def summed(a, j):
                s, n = a.b * 2 + j, a.t * 2 + j
                dve.wait_ge(S["exp_ready"], n + 1)
                chain.start(n)
                chain.done(dve.tensor_reduce(out=fsum[:, s, :], in_=feat[:, s, :, :, :].rearrange("p h s f -> p (h s) f"), axis=AX, op=ALU.add))
                dve.reciprocal(frec[:, s, :], fsum[:, s, :]).then_inc(S["rec_ready"], 1)

            def bounded(a, j):
                dve.wait_ge(S["mul_ready"], a.t * 2 + j + 1)
                f = feat[:, a.b * 2 + j, :, :, :]
                dve.tensor_scalar(out=f, in0=f, scalar1=FEAT_EPS, scalar2=None, op0=ALU.max).then_inc(S["feat_ready"], 1)

            def masked(a, g):
                n = a.t * G + g
                dve.wait_ge(S["s_ps"], n + 1)
                wait(dve, S["o_ps"], n - 1)
                dve.tensor_tensor(out=sc[:, g % 2, :, :], in0=ps_s[:, :].rearrange("p (h m) -> p h m", h=HG), in1=causal[:, :, :],
                                  op=ALU.mult).then_inc(S["s_ready"], 1)

            def normed(a, g):
                n = a.t * G + g
                dve.wait_ge(S["o_ps"], n + 1)
                if g == 0:
                    wait(dve, S["w_ps"], a.t - 1)
                o = ps_o[:, 0:HG * VW].rearrange("p (h e) -> p h e", h=HG)
                chain2.start(n * 2)
                chain2.done(dve.tensor_scalar(out=den[:, g % 2, :], in0=o[:, :, D1], scalar1=FEAT_EPS, scalar2=None, op0=ALU.add))
                chain2.done(dve.reciprocal(rden[:, g % 2, :], den[:, g % 2, :]))
                dve.tensor_tensor(out=y[:, a.b, g * HG * D1:(g + 1) * HG * D1].rearrange("p (h e) -> p h e", h=HG), in0=o[:, :, 0:D1],
                                  in1=rden[:, g % 2, :].rearrange("p (h a) -> p h a", a=1).broadcast_to([P, HG, D1]),
                                  op=ALU.mult).then_inc(S["y_ready"], 1)
                dve.wait_ge(S["y_ready"], n + 1)
                dve.sem_inc(S["o_read"], 1)

            def combined(a):
                dve.wait_ge(S["w_ps"], a.t + 1)
                hs = K.h[:, ds(a.t * D, D)]
                dve.tensor_tensor(out=hs, in0=ps_o[:, 0:D], in1=hs, op=ALU.add).then_inc(S["h_ready"], 1)
                take_moments(K, dve, a, S["h_ready"], a.t + 1)

            def step(p):
                now, before, done = has(p, 0), has(p, -1), has(p, -2)
                a = p.at(-1)
                if has(p, 1):
                    tokens(p.at(1))
                if now:
                    shifted(p, 0)
                if done:
                    normed(p.at(-2), G - 1)
                if before:
                    masked(a, 0)
                if now:
                    shifted(p, 1)
                if before:
                    masked(a, 1)
                if now:
                    summed(p, 0)
                if done:
                    combined(p.at(-2))
                if now:
                    summed(p, 1)
                if before:
                    normed(a, 0)
                    masked(a, 2)
                if now:
                    bounded(p, 0)
                if before:
                    normed(a, 1)
                    masked(a, 3)
                    normed(a, 2)
                if now:
                    bounded(p, 1)
            tokens(tile(0))
            passes(dve, step)


def stage_experts1(K, xT, plan, slots, weights):
    nc, ins = K.nc, K.ins
    U = TOK // SB
    HU = U // 2
    N = U + NB
    assert HU % 2 == 0
    NH = HF1 + 1
    TU = SB // P
    FB = 4
    wb = weights.b
    DOWN = weights.DOWN
    with ExitStack() as ctx:
        sb = lambda n, shape, dt=F32: ctx.enter_context(nc.sbuf_tensor("g_" + n, shape, dt))
        xr = sb("xr", [P, 2, TU, 2 * D], BF16)
        xg = sb("xg", [P, 2, 2, DC, SB], BF16)
        silu = sb("silu", [P, 2, SB])
        hf = sb("hf", [P, 2, NH, SB])
        hb = sb("hb", [P, 2, 2, NH, SB], BF16)
        y = sb("y", [P, 2, TU * D])
        fetched = sb("fetched", [P, FB, 2, D])
        ps = lambda n, dt=F32: ctx.enter_context(nc.psum_tensor("g_" + n, [P, 2048 // mybir.dt.size(dt)], dt))
        ps_u = [ps(f"u{b}") for b in range(4)]
        ps_d = [ps(f"d{b}") for b in range(2)]
        ps_t = [ps(f"t{b}", BF16) for b in range(2)]
        outs = nc.dram_tensor("expert_outputs", (NB * SB, D), F32).ap()
        identb = sb("identb", [P, P], BF16)
        stored = K.sem("g_stored")
        xr_loaded = [K.sem(f"g_xr_loaded{b}") for b in range(2)]
        got = [K.sem(f"g_got{b}") for b in range(FB)]
        y_stored = [K.sem(f"g_y_stored{b}") for b in range(2)]
        S = {n: K.sem("g_" + n) for n in
             ("identb_ready sent t_ps xg_ready up_ps silu_ready hf_ready hb_high hb_low down_ps "
              "y_ready combined1 combined").split()}
        block = ctx.enter_context(nc.Block())

        def base_unit(n):
            return n if n < HU else n - NB

        def blocks(eng, step):
            over(eng, HU, HU + NB, step, peel=HU + 4)

        @block.sync
        def _(sp):
            def fetch(n):
                b = n.t - HU
                expert = sp.value_load(plan.expert[0:1, ds(b, 1)], min_val=0, max_val=E1 - 1)
                use = b + 1
                wait(sp, weights.low_down, use - 1)
                wait(sp, weights.high_down, use - 1)
                weights.load(sp, expert, 1 - n.b)
                if isinstance(n.t, int) and n.t == HU:
                    sp.wait_ge(S["sent"], 16 * 2 * NT)
                wait(sp, S["t_ps"], b - 1)
                sp.dma_start(xr[:, n.b, :, :], slots[ds(b * SB, SB), :].rearrange("(p a) m -> p a m", a=TU)).then_inc(xr_loaded[n.b], 16)
            blocks(sp, fetch)
            for q in range(NT // 4):
                sp.wait_ge(S["combined"], q * 4 + 4)
                sp.dma_start(K.out[q * 4 * P:(q + 1) * 4 * P, :].rearrange("(t p) d -> p t d", p=P),
                             K.h[:, q * 4 * D:(q + 1) * 4 * D].rearrange("p (t d) -> p t d", t=4)).then_inc(stored, 16)
            sp.wait_ge(stored, 16 * (NT // 4))

        @block.gpsimd
        def _(pool):
            pool.wait_ge(K.slots_cleared, 16)
            for k in range(2):
                for t in range(NT):
                    pool.indirect_dma_start(out=slots[:, :], out_offset=bass.IndirectOffsetOnAxis(ap=plan.slot[:, k * NT + t:k * NT + t + 1], axis=0),
                                            in_=plan.rows[:, t * 2 * D:(t + 1) * 2 * D], in_offset=None).then_inc(S["sent"], 16)

            def step(n):
                b = n.t - HU
                weights.take_low(pool, b + 1, 1 - n.b, n.b, n.half - HU // 2 + 1 + n.b)
            blocks(pool, step)
            for b in range(2):
                pool.wait_ge(y_stored[b], 16 * ((NB + 1 - b) // 2))
            for t in range(NT):
                wait(pool, S["combined"], t - FB + 1)
                for k in range(2):
                    pool.indirect_dma_start(out=fetched[:, t % FB, k, :], out_offset=None, in_=outs[:, :],
                                            in_offset=bass.IndirectOffsetOnAxis(ap=plan.slot[:, k * NT + t:k * NT + t + 1], axis=0))\
                        .then_inc(got[t % FB], 16)

        @block.tensor
        def _(pe):
            def transposes(n):
                b = n.t - HU
                pe.wait_ge(xr_loaded[n.b], (n.half - HU // 2) * 16 + 16)
                wait(pe, S["xg_ready"], b - 1)
                for hl in range(2):
                    for c in range(DC):
                        for a in range(TU):
                            i = (hl * DC + c) * TU + a
                            last = pe.transpose(ps_t[n.b][:, i * P:(i + 1) * P],
                                                xr[:, n.b, a, hl * D + c * P:hl * D + (c + 1) * P], identb[:, :])
                last.then_inc(S["t_ps"], 1)

            def up(n, x, slot):
                for c in range(NH):
                    q, bank = n.t * NH + c, (n.k * NH + c) % 4
                    wait(pe, S["hf_ready"], q - 3)
                    for half in range(2 if c < HF1 else 1):
                        col = (half * HF1 + c) * P if c < HF1 else 2 * HF1 * P
                        parts = [(wh, xh, kc) for wh, xh in ((0, 0), (1, 0), (0, 1)) for kc in range(DC)]
                        for i, (wh, xh, kc) in enumerate(parts):
                            w0 = kc * 2 * HID1 + col
                            last = pe.matmul(ps_u[bank][:, half * SB:(half + 1) * SB], wb[:, slot, wh, w0:w0 + P], x(xh, kc),
                                             start=(i == 0), stop=(i == len(parts) - 1))
                    last.then_inc(S["up_ps"], 1)

            def down(n, slot):
                if not isinstance(n.t, int) or HU <= n.t < HU + NB:
                    pe.wait_ge(weights.low_down, n.t - HU + 2)
                pe.wait_ge(S["hb_high"], n.t + 1)
                pe.wait_ge(S["hb_low"], n.t + 1)
                wait(pe, S["y_ready"], n.t - 1)
                for a in range(TU):
                    parts = [(hh, wh, c) for hh, wh in ((0, 0), (1, 0), (0, 1)) for c in range(NH)]
                    for i, (hh, wh, c) in enumerate(parts):
                        w, w0 = (P, W1 + c * D) if c < HF1 else (HT1, DOWN)
                        last = pe.matmul(ps_d[n.b][:, a * D:(a + 1) * D], hb[0:w, n.b, hh, c, a * P:(a + 1) * P],
                                         wb[0:w, slot, wh, w0:w0 + D], start=(i == 0), stop=(i == len(parts) - 1))
                last.then_inc(S["down_ps"], 1)

            def up_base(n):
                u = base_unit(n.t)
                up(n, lambda hl, kc: xT[:, hl, kc, u * SB:(u + 1) * SB], 2)

            def up_block(n):
                b = n.t - HU
                pe.wait_ge(weights.low_up, b + 2)
                pe.wait_ge(S["xg_ready"], b + 1)
                up(n, lambda hl, kc: xg[:, n.b, hl, kc, :], n.b)

            pe.wait_ge(S["identb_ready"], 1)
            pe.wait_ge(weights.low_up, 1)
            pe.wait_ge(weights.low_down, 1)
            up_base(tile(0))
            for n in range(1, HU):
                up_base(tile(n))
                down(tile(n - 1), 2)
            transposes(tile(HU))
            up_block(tile(HU))
            transposes(tile(HU + 1))
            down(tile(HU - 1), 2)

            def step(n):
                up_block(n)
                transposes(n.at(1))
                down(n.at(-1), 1 - n.b)
            over(pe, HU + 1, HU + NB - 1, step, peel=HU + 4)
            last = tile(HU + NB - 1)
            up_block(last)
            down(last.at(-1), 1 - last.b)
            for n in range(HU + NB, N):
                up_base(tile(n))
                down(tile(n - 1), last.b if n == HU + NB else 2)
            down(tile(N - 1), 2)

        @block.scalar
        def _(act):
            act.activation(identb[:, :], K.ident[:, :], ACT.Copy).then_inc(S["identb_ready"], 1)

            def prepare_up(n, kc):
                wait(act, S["up_ps"], (n.t - 1) * NH)
                weights.take_high_up(act, 1 - n.b, n.b, n.half - HU // 2 + 1 + n.b, kc)

            def prepare_tokens(n):
                b = n.t - HU
                act.wait_ge(S["t_ps"], b + 1)
                wait(act, S["up_ps"], (n.t - 1) * NH)
                act.activation(xg[:, n.b, :, :, :].rearrange("p h c m -> p (h c m)"), ps_t[n.b][:, :], ACT.Copy).then_inc(S["xg_ready"], 1)

            def prepare_down(n):
                wait(act, S["down_ps"], n.t - 1)
                weights.take_high_down(act, 1 - n.b, n.b)

            def silus(n, between=None):
                for c in range(NH):
                    w = P if c < HF1 else HT1
                    q, bank = n.t * NH + c, (n.k * NH + c) % 4
                    act.wait_ge(S["up_ps"], q + 1)
                    wait(act, S["hf_ready"], q - 1)
                    act.activation(silu[0:w, c % 2, :], ps_u[bank][0:w, 0:SB], ACT.Silu).then_inc(S["silu_ready"], 1)
                    if between and c % 2 == 1 and c // 2 < DC:
                        between(c // 2)

            def highs(n):
                act.wait_ge(S["hf_ready"], n.t * NH + NH)
                wait(act, S["down_ps"], n.t - 1)
                act.activation(hb[:, n.b, 0, 0:HF1, :], hf[:, n.b, 0:HF1, :], ACT.Copy)
                act.activation(hb[0:HT1, n.b, 0, HF1, :], hf[0:HT1, n.b, HF1, :], ACT.Copy).then_inc(S["hb_high"], 1)

            def store(n):
                b = n.t - HU
                act.wait_ge(S["y_ready"], n.t + 1)
                act.dma_start(outs[ds(b * SB, SB), :].rearrange("(p a) m -> p (a m)", a=TU), y[:, n.b, :]).then_inc(y_stored[n.b], 16)

            for n in range(HU - 1):
                silus(tile(n))
                highs(tile(n))

            def step(n):
                if not isinstance(n.t, int) or n.t >= HU + 2:
                    store(n.at(-2))
                silus(n, lambda kc: prepare_up(n.at(1), kc))
                prepare_tokens(n.at(1))
                highs(n)
                prepare_down(n.at(1))
            over(act, HU - 1, HU + NB - 1, step, peel=HU + 4)
            for n in range(HU + NB - 1, N):
                if n < HU + NB + 2:
                    store(tile(n - 2))
                silus(tile(n))
                highs(tile(n))

        @block.vector
        def _(dve):
            def gated(n):
                for c in range(NH):
                    w = P if c < HF1 else HT1
                    q, bank = n.t * NH + c, (n.k * NH + c) % 4
                    dve.wait_ge(S["silu_ready"], q + 1)
                    if c == 0:
                        wait(dve, S["hb_high"], n.t - 1)
                        wait(dve, S["hb_low"], n.t - 1)
                    other = ps_u[bank][:, SB:2 * SB] if c < HF1 else ps_u[bank][HT1:2 * HT1, 0:SB]
                    dve.tensor_tensor(out=hf[0:w, n.b, c, :], in0=silu[0:w, c % 2, :], in1=other, op=ALU.mult).then_inc(S["hf_ready"], 1)

            def lows(n):
                dve.wait_ge(S["hb_high"], n.t + 1)
                dve.tensor_tensor(out=hb[:, n.b, 1, 0:HF1, :], in0=hf[:, n.b, 0:HF1, :], in1=hb[:, n.b, 0, 0:HF1, :], op=ALU.subtract)
                dve.tensor_tensor(out=hb[0:HT1, n.b, 1, HF1, :], in0=hf[0:HT1, n.b, HF1, :], in1=hb[0:HT1, n.b, 0, HF1, :],
                                  op=ALU.subtract).then_inc(S["hb_low"], 1)

            def take_block(n):
                dve.wait_ge(S["down_ps"], n.t + 1)
                wait(dve, y_stored[n.b], (n.half - HU // 2) * 16)
                dve.tensor_scalar(out=y[:, n.b, :], in0=ps_d[n.b][:, :], scalar1=1.0, scalar2=None, op0=ALU.mult).then_inc(S["y_ready"], 1)

            def take_base(n):
                u = base_unit(n.t)
                dve.wait_ge(S["down_ps"], n.t + 1)
                hs = K.h[:, u * TU * D:(u + 1) * TU * D]
                dve.tensor_tensor(out=hs, in0=ps_d[n.b][:, :], in1=hs, op=ALU.add).then_inc(S["y_ready"], 1)

            def combine(t):
                dve.wait_ge(got[t % FB], (t // FB + 1) * 32)
                u = t // TU
                dve.wait_ge(S["y_ready"], (u if u < HU else u + NB) + 1)
                hs = K.h[:, t * D:(t + 1) * D]
                for k in range(2):
                    wgt = plan.weight[:, k * NT + t:k * NT + t + 1]
                    dve.scalar_tensor_tensor(out=hs, in0=fetched[:, t % FB, k, :], scalar=wgt, in1=hs, op0=ALU.mult, op1=ALU.add)\
                       .then_inc(S["combined1" if k == 0 else "combined"], 1)
                    if k == 0:
                        dve.wait_ge(S["combined1"], t + 1)

            gated(tile(0))
            lows(tile(0))
            for n in range(1, HU):
                gated(tile(n))
                lows(tile(n))
                take_base(tile(n - 1))
            gated(tile(HU))
            lows(tile(HU))
            take_base(tile(HU - 1))

            def step(n):
                gated(n)
                lows(n)
                take_block(n.at(-1))
            over(dve, HU + 1, HU + NB, step, peel=HU + 4)
            for n in range(HU + NB, N):
                gated(tile(n))
                lows(tile(n))
                (take_block if n == HU + NB else take_base)(tile(n - 1))
                if n > HU + NB:
                    for t in range((n - HU - NB - 1) * NT // HU, (n - HU - NB) * NT // HU):
                        combine(t)
            take_base(tile(N - 1))
            for t in range((HU - 1) * NT // HU, NT):
                combine(t)


def build(nc, ins, out):
    with ExitStack() as ctx:
        K = Core(nc, ctx, ins, out)
        slots = nc.dram_tensor("slots", (NB * SB, 2 * D), BF16).ap()
        with nc.sbuf_tensor("stats", [P, NT * 3 * D], F32) as stats:
            stage_statistics(K, stats)
            stage_projection(K, stats)
        stage_attention0(K)
        with nc.sbuf_tensor("xT", [P, DC, TOK], F32) as xT, nc.sbuf_tensor("gate", [P, E0, NT], F32) as gate:
            stage_gate(K, "f0_", E0, route0(gate), xT)
            stage_experts0(K, xT, gate)
            stage_shared0(K, xT)
        with nc.sbuf_tensor("wf", [P, 2, DC, H1 * F1], F32) as wf:
            stage_fused_weights(K, wf)
            stage_attention1(K, wf, slots)
        K.renew_semaphores()
        with nc.sbuf_tensor("xT1", [P, 2, DC, TOK], BF16) as xT, ExitStack() as moe:
            plan = Plan(nc, moe, K)
            weights = ExpertWeights(nc, moe, K)
            stage_gate(K, "f1_", E1, route1(), xT, plan, weights)
            stage_experts1(K, xT, plan, slots, weights)


def arranged(i):
    import numpy as np

    up = np.concatenate([i["L1_ffn_exp_wgu"], i["L1_ffn_base_wgu"][None]])
    down = np.concatenate([i["L1_ffn_exp_wd"], i["L1_ffn_base_wd"][None]])
    whole = HF1 * P
    up = np.concatenate([up[..., :whole], up[..., HID1:HID1 + whole], up[..., whole:HID1], up[..., HID1 + whole:]], axis=-1)
    return {
        "x": i["x"].reshape(TOK, BLK * D),
        "w_proj": i["L0_tok_w_proj_w"].reshape(D),
        "b_proj": i["L0_tok_w_proj_b"],
        "s_proj_w": i["L0_tok_s_proj_w"],
        "s_proj_b": i["L0_tok_s_proj_b"],
        "ln_g": i["L0_tok_ln_g"],
        "ln_b": i["L0_tok_ln_b"],
        "pos_emb": i["L0_tok_pos_emb"],
        **{f"a0_w{n}T": i[f"L0_attn_W{n}"].T for n in "qkvo"},
        **{f"a0_b{n}": i[f"L0_attn_b{n}"] for n in "qkvo"},
        "a1_wqT": i["L1_attn_Wq"].T,
        "a1_wkT": i["L1_attn_Wk"].T,
        "a1_kq": i["L1_attn_Kq"],
        "a1_kk": i["L1_attn_Kk"],
        "a1_wv": i["L1_attn_Wv"],
        "a1_wo": i["L1_attn_Wo"],
        "f1_gate": i["L1_ffn_gate_w"],
        "f1_up": up.reshape(E1 + 1, DC, P, 2 * HID1).transpose(0, 2, 1, 3).reshape((E1 + 1) * P, W1),
        "f1_down": down[:, :whole].reshape(E1 + 1, HF1, P, D).transpose(0, 2, 1, 3).reshape((E1 + 1) * P, HF1 * D),
        "f1_rest": down[:, whole:].reshape((E1 + 1) * HT1, D),
        "f0_gate": i["L0_ffn_gate_w"].T,
        "f0_gate_bias": i["L0_ffn_expert_bias"],
        "f0_up": i["L0_ffn_w_up"].transpose(0, 2, 1).reshape(E0 * D, HID0),
        "f0_down": i["L0_ffn_w_down"].transpose(0, 2, 1).reshape(E0 * HID0, D),
        "f0_shared_up": i["L0_ffn_shared_w_up"].T,
        "f0_shared_down": i["L0_ffn_shared_w_down"].T,
    }


def kernel(**inputs):
    import numpy as np
    from concourse import bacc
    from concourse.bass_utils import run_bass_kernel_spmd

    nc = bacc.Bacc("TRN2", target_bir_lowering=False, num_devices=1)
    arrays, args = {}, {}
    for name, a in arranged({k: np.asarray(v) for k, v in inputs.items()}).items():
        a = np.ascontiguousarray(a)
        arrays["in_" + name] = a
        args[name] = nc.dram_tensor("in_" + name, a.shape, mybir.dt.from_np(a.dtype), kind="ExternalInput").ap()
    out = nc.dram_tensor("out_0_dram", (TOK // NPOS, NPOS, D), F32, kind="ExternalOutput").ap()
    build(nc, args, out.rearrange("b s d -> (b s) d"))
    r = run_bass_kernel_spmd(nc, [arrays], core_ids=[0])
    return r.results[0]["out_0_dram"]
```

```python
from contextlib import ExitStack

import concourse.bass as bass
from concourse import mybir

P = 128
F32 = mybir.dt.float32
BF16 = mybir.dt.bfloat16
ALU = mybir.AluOpType
ACT = mybir.ActivationFunctionType
AX = mybir.AxisListType.X
ds = bass.ds

D = 256
DC = D // P
BLK = 16
NPOS = 16
TOK = 2048
NT = TOK // P
BPT = P // NPOS
H0, D0 = 16, 16
H1, D1, F1 = 16, 64, 64
E0, HID0 = 8, 352
E1, HID1 = 8, 704
GT = 512
NG = TOK // GT
TPG = GT // P
SB = 256
NB = (2 * TOK + E1 * (SB - 1)) // SB
W1 = DC * 2 * HID1
HF1 = HID1 // P
HT1 = HID1 - HF1 * P
LN_EPS = 1e-5
VAR_EPS = 1e-8
FEAT_EPS = 1e-12


class Chain:

    def __init__(self, eng, sem):
        self.eng, self.sem, self.base, self.n = eng, sem, 0, 0

    def start(self, base):
        self.base, self.n = base, 0

    def done(self, ins):
        ins.then_inc(self.sem, 1)
        self.n += 1
        self.eng.wait_ge(self.sem, self.base + self.n)


def chunks(n):
    return [(c, min(P, n - c * P)) for c in range((n + P - 1) // P)]


class Core:

    def __init__(self, nc, ctx, ins, out):
        self.nc, self.ins, self.out = nc, ins, out
        self.ctx = ctx
        f = lambda name, shape, dt=F32: ctx.enter_context(nc.sbuf_tensor(name, shape, dt))
        self.h = f("h", [P, NT * D])
        self.mv = f("mv", [P, NT, 2])
        self.moments = f("moments", [P, NT * 6])
        self.std = f("std", [P, NT])
        self.rstd = f("rstd", [P, NT])
        self.ident = f("ident", [P, P])
        self.zero = f("zero", [P, 2 * D], BF16)
        self.eps_ln = f("eps_ln", [P, 1])
        self.eps_var = f("eps_var", [P, 1])
        self.sems = []
        self.passes = nc.alloc_semaphore("passes")
        self.slots_cleared = nc.alloc_semaphore("slots_cleared")

    def sem(self, name):
        self.sems.append(self.nc.alloc_semaphore(name))
        return self.sems[-1]

    def renew_semaphores(self):
        self.nc.clear_and_free_semaphores(self.sems)
        self.sems = []
        self.nc.all_engine_barrier()

    def hold(self, eng):
        eng.sem_inc(self.passes, 1)



class Turn:

    def __init__(self, turn, k, per):
        self.turn, self.k, self.per = turn, k, per
        self.t = turn * per + k
        self.b = k % 2
        self.half = turn * (per // 2) + k // 2

    def at(self, d):
        q = self.k + d
        return Turn(self.turn + q // self.per, q % self.per, self.per)


def tile(t, per=2):
    return Turn(t // per, t % per, per)


def wait(eng, sem, count):
    if not isinstance(count, int) or count > 0:
        eng.wait_ge(sem, count)


def over(eng, first, last, step, per=2, peel=None):
    lo = max(peel or max(per, 4), first + -first % per)
    hi = max(lo, last - last % per)
    for t in range(first, min(lo, last)):
        step(tile(t, per))
    if hi > lo:
        with eng.Fori(lo // per, hi // per) as i:
            for k in range(per):
                step(Turn(i, k, per))
    for t in range(max(hi, first), last):
        step(tile(t, per))


def has(a, d):
    return not isinstance(a.t, int) or 0 <= a.t + d < NT


def passes(eng, step):
    over(eng, 0, NT - 1, step)
    for p in range(NT - 1, NT + 2):
        step(tile(p))


class ProjectionWeights:
    def __init__(self, nc, ctx, K):
        sb = lambda name, shape: ctx.enter_context(nc.sbuf_tensor(name, shape, F32))
        self.wsp, self.bsp = sb("wsp", [P, 3 * DC, D]), sb("bsp", [P, D])
        self.gain, self.shift, self.pos = sb("gain", [P, D]), sb("shift", [P, D]), sb("pos", [P, D])
        self.loaded, self.all = K.sem("p_w_loaded"), 16 * (4 + BPT)

    def load(self, sp, ins):
        sp.dma_start(self.wsp[:, :, :], ins["s_proj_w"].rearrange("(c p) n -> p c n", p=P)).then_inc(self.loaded, 16)
        sp.dma_start(self.bsp[:, :], ins["s_proj_b"].partition_broadcast(P)).then_inc(self.loaded, 16)
        sp.dma_start(self.gain[:, :], ins["ln_g"].partition_broadcast(P)).then_inc(self.loaded, 16)
        sp.dma_start(self.shift[:, :], ins["ln_b"].partition_broadcast(P)).then_inc(self.loaded, 16)
        for j in range(BPT):
            sp.dma_start(self.pos[j * NPOS:(j + 1) * NPOS, :], ins["pos_emb"][0:NPOS, :]).then_inc(self.loaded, 16)


class Attention0Weights:
    def __init__(self, nc, ctx, K):
        sb = lambda name, shape: ctx.enter_context(nc.sbuf_tensor("a_" + name, shape, F32))
        self.wq, self.wk, self.wv, self.wo = (sb(n, [P, DC, D]) for n in ("wq", "wk", "wv", "wo"))
        self.bqk = sb("bqk", [P, 2 * DC])
        self.bv, self.bo = sb("bv", [P, D]), sb("bo", [P, D])
        self.nc, self.loaded, self.all = nc, K.sem("a_loaded"), 16 * 8

    def load(self, sp, ins):
        for t, n in ((self.wq, "a0_wqT"), (self.wk, "a0_wkT"), (self.wv, "a0_wvT"), (self.wo, "a0_woT")):
            sp.dma_start(t[:, :, :], ins[n].rearrange("(c p) n -> p c n", p=P)).then_inc(self.loaded, 16)
        with self.nc.allow_non_contiguous_dma(reason="512 biases, once"):
            sp.dma_start(self.bqk[:, 0:DC], ins["a0_bq"].rearrange("(c p) -> p c", p=P)).then_inc(self.loaded, 16)
            sp.dma_start(self.bqk[:, DC:2 * DC], ins["a0_bk"].rearrange("(c p) -> p c", p=P)).then_inc(self.loaded, 16)
        sp.dma_start(self.bv[:, :], ins["a0_bv"].partition_broadcast(P)).then_inc(self.loaded, 16)
        sp.dma_start(self.bo[:, :], ins["a0_bo"].partition_broadcast(P)).then_inc(self.loaded, 16)


class SharedWeights:
    def __init__(self, nc, ctx, K):
        sb = lambda name, shape: ctx.enter_context(nc.sbuf_tensor("s_" + name, shape, F32))
        self.wu, self.wd = sb("wu", [P, DC, HID0]), sb("wd", [P, len(chunks(HID0)), D])
        self.loaded, self.all = K.sem("s_loaded"), 16 * 3

    def load(self, sp, ins):
        (m, last), wd = chunks(HID0)[-1], self.wd
        sp.dma_start(self.wu[:, :, :], ins["f0_shared_up"].rearrange("(c p) n -> p c n", p=P)).then_inc(self.loaded, 16)
        sp.dma_start(wd[:, 0:m, :], ins["f0_shared_down"][0:m * P, :].rearrange("(c p) n -> p c n", p=P)).then_inc(self.loaded, 16)
        sp.dma_start(wd[0:last, m, :], ins["f0_shared_down"][m * P:HID0, :]).then_inc(self.loaded, 16)


class Experts0Inputs:

    def __init__(self, nc, ctx, K):
        sb = lambda name, shape: ctx.enter_context(nc.sbuf_tensor("e_" + name, shape, F32))
        self.NH = len(chunks(HID0))
        self.wu, self.wd = sb("wu_f", [P, 2, DC, HID0]), sb("wd_f", [P, 2, self.NH, D])
        self.gT = sb("gT", [P, P])
        self.grow = sb("grow", [P, 2, TOK])
        self.gates = nc.dram_tensor("gates", (E0, TOK), F32).ap()
        self.loaded = [K.sem(f"e_loaded{b}") for b in range(2)]
        self.grow_loaded = [K.sem(f"e_grow_loaded{b}") for b in range(2)]
        self.gT_ps, self.gT_ready, self.gates_stored = (K.sem("e_" + n) for n in ("gT_ps", "gT_ready", "gates_stored"))

    def load_weights(self, sp, ins, e):
        m, last = chunks(HID0)[-1]
        for dst, src in ((self.wu[:, e.b, :, :], ins["f0_up"][ds(e.t * D, D), :].rearrange("(c p) n -> p c n", p=P)),
                         (self.wd[:, e.b, 0:m, :], ins["f0_down"][ds(e.t * HID0, m * P), :].rearrange("(c p) n -> p c n", p=P)),
                         (self.wd[0:last, e.b, m, :], ins["f0_down"][ds(e.t * HID0 + m * P, last), :])):
            sp.dma_start(dst, src).then_inc(self.loaded[e.b], 16)

    def load_gates(self, sp, e):
        sp.dma_start(self.grow[:, e.b, :], self.gates[ds(e.t, 1), :].rearrange("a m -> (a m)").partition_broadcast(P)).then_inc(self.grow_loaded[e.b], 16)


class Attention1Weights:
    def __init__(self, nc, ctx, K):
        W = H1 * D1
        sb = lambda name, shape: ctx.enter_context(nc.sbuf_tensor("b_" + name, shape, F32))
        self.wT = sb("wT", [P, 2, H1 // 2, D])
        self.kk = sb("kk", [P, 2, H1 // 2, 2 * F1])
        self.wv, self.wo = sb("wv", [P, DC, W]), sb("wo", [P, W // P, D])
        self.cleared = K.sem("b_cleared")
        self.parts_loaded, self.all_parts = K.sem("b_parts_loaded"), 16 * 6
        self.loaded, self.all = K.sem("b_loaded"), 16 * 2

    def clear(self, pool):
        pool.memset(self.kk[:, :, :, :], 0.0).then_inc(self.cleared, 1)

    def load(self, sp, ins):
        sp.wait_ge(self.cleared, 1)
        for j, n in enumerate("qk"):
            sp.dma_start(self.wT[:, j, :, :], ins[f"a1_w{n}T"].rearrange("(h p) d -> p h d", p=P)).then_inc(self.parts_loaded, 16)
            for o in range(2):
                sp.dma_start(self.kk[o * D1:(o + 1) * D1, j, :, o * F1:(o + 1) * F1],
                             ins[f"a1_k{n}"].rearrange("(h o) p f -> o p h f", o=2)[o]).then_inc(self.parts_loaded, 16)
        sp.dma_start(self.wv[:, :, :], ins["a1_wv"].rearrange("(c p) n -> p c n", p=P)).then_inc(self.loaded, 16)
        sp.dma_start(self.wo[:, :, :], ins["a1_wo"].rearrange("(c p) n -> p c n", p=P)).then_inc(self.loaded, 16)


def stage_statistics(K, stats, later):
    nc, ins = K.nc, K.ins
    XB = 4
    DB = 10
    with ExitStack() as ctx:
        sb = lambda name, shape, dt=F32: ctx.enter_context(nc.sbuf_tensor(name, shape, dt))
        x = sb("x", [P, XB, BLK * D])
        diag = sb("diag", [P, XB, BLK * P])
        wproj = sb("wproj", [P, D])
        bproj = sb("bproj", [P, 1])
        prod = sb("prod", [P, BLK, D])
        logit = sb("logit", [P, 2, BLK])
        logitb = sb("logitb", [P, 2, BLK])
        mean = sb("t_mean", [P, 2, D])
        nmax = sb("nmax", [P, 2])
        expw = sb("expw", [P, 2, BLK])
        esum = sb("esum", [P, 2])
        rsum = sb("rsum", [P, 2])
        w = sb("w", [P, 2, BLK])
        ps_mean = [ctx.enter_context(nc.psum_tensor(f"ps_mean{b}", [P, 512], F32)) for b in range(2)]
        ps_var = [ctx.enter_context(nc.psum_tensor(f"ps_var{b}", [P, 512], F32)) for b in range(2)]

        const_loaded = K.sem("t_const_loaded")
        ident_steps = K.sem("t_ident_steps")
        x_loaded = [K.sem(f"t_x_loaded{b}") for b in range(XB)]
        nmax_ready = K.sem("t_nmax_ready")
        exp_ready = K.sem("t_exp_ready")
        w_ready = K.sem("t_w_ready")
        max_ready = K.sem("t_max_ready")
        diag_ready = K.sem("t_diag_ready")
        mean_ready = K.sem("t_mean_ready")
        mean_copied = K.sem("t_mean_copied")
        diff_ready = K.sem("t_diff_ready")
        diff2_ready = K.sem("t_diff2_ready")
        square_ready = K.sem("t_square_ready")
        var_ready = K.sem("t_var_ready")
        var_copied = K.sem("t_var_copied")
        steps = K.sem("t_vector_steps")
        block = ctx.enter_context(nc.Block())

        @block.sync
        def _(sp):
            sp.dma_start(wproj[:, :], ins["w_proj"].partition_broadcast(P)).then_inc(const_loaded, 16)
            sp.dma_start(bproj[:, :], ins["b_proj"].partition_broadcast(P)).then_inc(const_loaded, 16)

            def load(a):
                wait(sp, var_ready, a.t - XB + 1)
                sp.dma_start(x[:, a.k, :], ins["x"][ds(a.t * P, P), :]).then_inc(x_loaded[a.k], 16)
            over(sp, 0, NT, load, per=XB)
            for weights in later:
                weights.load(sp, ins)

        @block.gpsimd
        def _(pool):
            pool.memset(K.zero[:, :], 0.0)
            pool.memset(K.eps_ln[:, :], LN_EPS)
            pool.memset(K.eps_var[:, :], VAR_EPS)
            pool.memset(K.ident[:, :], 0.0).then_inc(ident_steps, 1)
            pool.wait_ge(ident_steps, 1)
            pool.affine_select(out=K.ident[:, :], in_=K.ident[:, :], compare_op=ALU.not_equal, fill=1.0,
                               base=0, pattern=[[-1, P]], channel_multiplier=1).then_inc(ident_steps, 1)
            pool.wait_ge(ident_steps, 2)

            def spread(a):
                pool.wait_ge(w_ready, a.t + 1)
                wait(pool, var_ready, a.t - XB + 1)
                pool.tensor_tensor(out=diag[:, a.k, :].rearrange("p (k m) -> p k m", k=BLK),
                                   in0=K.ident[:, :].rearrange("p (a m) -> p a m", a=1).broadcast_to([P, BLK, P]),
                                   in1=w[:, a.b, :].rearrange("p (k a) -> p k a", a=1).broadcast_to([P, BLK, P]),
                                   op=ALU.mult).then_inc(diag_ready, 1)

            def deviations(a):
                pool.wait_ge(mean_copied, a.t + 1)
                pool.wait_ge(max_ready, a.t * 2 + 2)
                K.hold(pool)
                rows = x[:, a.k, DB * D:BLK * D].rearrange("p (k d) -> p k d", d=D)
                pool.tensor_tensor(out=rows, in0=rows, in1=mean[:, a.b, :].rearrange("p (a d) -> p a d", a=1).broadcast_to([P, BLK - DB, D]),
                                   op=ALU.subtract).then_inc(diff2_ready, 1)

            def step(a):
                spread(a)
                deviations(a.at(-1))
            spread(tile(0, XB))
            over(pool, 1, NT, step, per=XB)
            deviations(tile(NT - 1, XB))

        @block.vector
        def _(dve):
            chain = Chain(dve, steps)
            dve.wait_ge(const_loaded, 32)

            def maximum(a, half):
                W = D // 2
                dve.tensor_reduce(out=stats[:, ds(a.t * 3 * D + 2 * D + half * W, W)],
                                  in_=x[:, a.k, :].rearrange("p (k d) -> p d k", k=BLK)[:, half * W:(half + 1) * W, :],
                                  axis=AX, op=ALU.max).then_inc(max_ready, 1)

            def head(a):
                chain.start(a.t * 3)
                dve.wait_ge(x_loaded[a.k], a.turn * 16 + 16)
                for k in range(BLK):
                    last = dve.tensor_tensor_reduce(out=prod[:, k, :], in0=x[:, a.k, k * D:(k + 1) * D], in1=wproj[:, :],
                                                    scale=1.0, scalar=0.0, op0=ALU.mult, op1=ALU.add,
                                                    accum_out=logit[:, a.b, k:k + 1])
                chain.done(last)
                chain.done(dve.tensor_scalar(out=logitb[:, a.b, :], in0=logit[:, a.b, :], scalar1=bproj[:, 0:1],
                                             scalar2=None, op0=ALU.add))
                dve.tensor_reduce(out=nmax[:, a.b:a.b + 1], in_=logitb[:, a.b, :], axis=AX, op=ALU.max,
                                  negate=True).then_inc(nmax_ready, 1)
                maximum(a, 0)
                dve.wait_ge(exp_ready, a.t + 1)
                wait(dve, diag_ready, a.t - 1)
                chain.done(dve.reciprocal(rsum[:, a.b:a.b + 1], esum[:, a.b:a.b + 1]))
                dve.tensor_scalar(out=w[:, a.b, :], in0=expw[:, a.b, :], scalar1=rsum[:, a.b:a.b + 1],
                                  scalar2=None, op0=ALU.mult).then_inc(w_ready, 1)
                maximum(a, 1)

            def deviations(a):
                dve.wait_ge(mean_copied, a.t + 1)
                dve.wait_ge(max_ready, a.t * 2 + 2)
                rows = x[:, a.k, 0:DB * D].rearrange("p (k d) -> p k d", d=D)
                dve.tensor_tensor(out=rows, in0=rows, in1=mean[:, a.b, :].rearrange("p (a d) -> p a d", a=1).broadcast_to([P, DB, D]),
                                  op=ALU.subtract).then_inc(diff_ready, 1)

            def step(a):
                head(a)
                deviations(a.at(-1))
            head(tile(0, XB))
            over(dve, 1, NT, step, per=XB)
            deviations(tile(NT - 1, XB))

        @block.scalar
        def _(act):
            def weights(a):
                act.wait_ge(nmax_ready, a.t + 1)
                act.activation(expw[:, a.b, :], logitb[:, a.b, :], ACT.Exp, bias=nmax[:, a.b:a.b + 1],
                               accum_out=esum[:, a.b:a.b + 1]).then_inc(exp_ready, 1)

            def squares(a):
                act.wait_ge(mean_ready, a.t + 1)
                wait(act, diff_ready, a.t - 1)
                wait(act, diff2_ready, a.t - 1)
                act.activation(mean[:, a.b, :], ps_mean[a.b][:, 0:D], ACT.Copy).then_inc(mean_copied, 1)
                act.activation(stats[:, ds(a.t * 3 * D, D)], ps_mean[a.b][:, 0:D], ACT.Copy)
                act.wait_ge(diff_ready, a.t + 1)
                act.wait_ge(diff2_ready, a.t + 1)
                act.activation(x[:, a.k, :], x[:, a.k, :], ACT.Square).then_inc(square_ready, 1)

            def variance(a):
                act.wait_ge(var_ready, a.t + 1)
                act.activation(stats[:, ds(a.t * 3 * D + D, D)], ps_var[a.b][:, 0:D], ACT.Copy).then_inc(var_copied, 1)

            def step(a):
                weights(a)
                squares(a.at(-1))
                variance(a.at(-2))
            weights(tile(0, XB))
            weights(tile(1, XB))
            squares(tile(0, XB))
            over(act, 2, NT, step, per=XB)
            squares(tile(NT - 1, XB))
            variance(tile(NT - 2, XB))
            variance(tile(NT - 1, XB))

        @block.tensor
        def _(pe):
            def mean(a):
                pe.wait_ge(diag_ready, a.t + 1)
                wait(pe, square_ready, a.t - 1)
                for k in range(BLK):
                    last = pe.matmul(ps_mean[a.b][:, 0:D], diag[:, a.k, k * P:(k + 1) * P], x[:, a.k, k * D:(k + 1) * D],
                                     start=(k == 0), stop=(k == BLK - 1))
                last.then_inc(mean_ready, 1)

            def variance(a):
                pe.wait_ge(square_ready, a.t + 1)
                wait(pe, var_copied, a.t - 1)
                for k in range(BLK):
                    last = pe.matmul(ps_var[a.b][:, 0:D], diag[:, a.k, k * P:(k + 1) * P], x[:, a.k, k * D:(k + 1) * D],
                                     start=(k == 0), stop=(k == BLK - 1))
                last.then_inc(var_ready, 1)

            def step(a):
                mean(a)
                variance(a.at(-1))
            mean(tile(0, XB))
            over(pe, 1, NT, step, per=XB)
            variance(tile(NT - 1, XB))


def stage_projection(K, stats, weights):
    nc, ins = K.nc, K.ins
    SC = 3 * DC
    with ExitStack() as ctx:
        sb = lambda name, shape, dt=F32: ctx.enter_context(nc.sbuf_tensor(name, shape, dt))
        wsp, bsp, gain, shift, pos = weights.wsp, weights.bsp, weights.gain, weights.shift, weights.pos
        pre = sb("pre", [P, 2, D])
        mom, mean = sb("mom", [P, 2, 6]), sb("mean", [P, 2, 2])
        dev, rdev = sb("dev", [P, 2]), sb("rdev", [P, 2])
        centred, scaled = sb("centred", [P, 2, D]), sb("scaled", [P, 2, D])
        st = sb("st", [P, 2, 3 * D])
        sT = sb("sT", [P, 2, SC * P])
        ps_t = [ctx.enter_context(nc.psum_tensor(f"ps_t{b}", [P, 1024], F32)) for b in range(2)]
        ps_o = [ctx.enter_context(nc.psum_tensor(f"ps_o{b}", [P, 512], F32)) for b in range(2)]
        w_loaded, LOADS = weights.loaded, weights.all
        st_ready = K.sem("p_st_ready")
        transposed = K.sem("p_transposed")
        sT_ready = K.sem("p_sT_ready")
        out_ready = K.sem("p_out_ready")
        out_read = K.sem("p_out_read")
        shift_ready, mean_ready, dev_ready, centred_ready, scaled_ready, h_ready, steps = (
            K.sem("p_" + n) for n in "shift_ready mean_ready dev_ready centred_ready scaled_ready h_ready steps".split())
        block = ctx.enter_context(nc.Block())

        @block.gpsimd
        def _(pool):
            pool.wait_ge(w_loaded, LOADS)
            pool.tensor_tensor(out=shift[:, :], in0=shift[:, :], in1=pos[:, :], op=ALU.add).then_inc(shift_ready, 1)

            def scale(a):
                pool.wait_ge(centred_ready, a.t + 1)
                wait(pool, h_ready, a.t - 1)
                pool.tensor_tensor(out=scaled[:, a.b, :], in0=centred[:, a.b, :], in1=gain[:, :], op=ALU.mult).then_inc(scaled_ready, 1)
            over(pool, 0, NT, scale)

        @block.scalar
        def _(act):
            def stage(a):
                wait(act, transposed, a.t - 1)
                act.activation(st[:, a.b, 0:D], stats[:, ds(a.t * 3 * D, D)], ACT.Copy)
                act.activation(st[:, a.b, D:2 * D], stats[:, ds(a.t * 3 * D + D, D)], ACT.Sqrt, bias=K.eps_var[:, 0:1])
                act.activation(st[:, a.b, 2 * D:3 * D], stats[:, ds(a.t * 3 * D + 2 * D, D)], ACT.Copy).then_inc(st_ready, 1)

            def evacuate(a):
                act.wait_ge(transposed, a.t + 1)
                wait(act, out_ready, a.t - 1)
                act.activation(sT[:, a.b, :], ps_t[a.b][:, 0:SC * P], ACT.Copy).then_inc(sT_ready, 1)

            def root(a):
                act.wait_ge(mean_ready, a.t + 1)
                wait(act, centred_ready, a.t - 1)
                act.activation(dev[:, a.b:a.b + 1], mean[:, a.b, 1:2], ACT.Sqrt, bias=K.eps_ln[:, 0:1]).then_inc(dev_ready, 1)

            def step(p):
                if has(p, 1):
                    stage(p.at(1))
                if has(p, 0):
                    evacuate(p)
                if has(p, -2):
                    root(p.at(-2))
            stage(tile(0))
            passes(act, step)

        @block.tensor
        def _(pe):
            def transposes(a):
                pe.wait_ge(st_ready, a.t + 1)
                wait(pe, sT_ready, a.t - 1)
                for c in range(SC):
                    last = pe.transpose(ps_t[a.b][:, c * P:(c + 1) * P], st[:, a.b, c * P:(c + 1) * P], K.ident[:, :])
                last.then_inc(transposed, 1)

            def project(a):
                pe.wait_ge(sT_ready, a.t + 1)
                wait(pe, out_read, a.t - 1)
                for c in range(SC):
                    last = pe.matmul(ps_o[a.b][:, 0:D], sT[:, a.b, c * P:(c + 1) * P], wsp[:, c, :],
                                     start=(c == 0), stop=(c == SC - 1))
                last.then_inc(out_ready, 1)

            def step(a):
                transposes(a)
                project(a.at(-1))
            pe.wait_ge(w_loaded, LOADS)
            transposes(tile(0))
            over(pe, 1, NT, step)
            project(tile(NT - 1))

        @block.vector
        def _(dve):
            dve.wait_ge(w_loaded, LOADS)

            dve.wait_ge(shift_ready, 1)
            chain, chain2 = Chain(dve, steps), Chain(dve, K.sem("p_steps2"))

            def take(a):
                dve.wait_ge(out_ready, a.t + 1)
                wait(dve, centred_ready, a.t - 1)
                dve.tensor_tensor(out=pre[:, a.b, :], in0=ps_o[a.b][:, 0:D], in1=bsp[:, :], op=ALU.add).then_inc(out_read, 1)
                dve.wait_ge(out_read, a.t + 1)
                K.hold(dve)
                chain.start(a.t)
                chain.done(dve.bn_stats(out=mom[:, a.b, :], in_=pre[:, a.b, :]))
                K.hold(dve)
                dve.bn_aggr(out=mean[:, a.b, :], in_=mom[:, a.b, :]).then_inc(mean_ready, 1)

            def centre(a):
                dve.wait_ge(dev_ready, a.t + 1)
                wait(dve, scaled_ready, a.t - 1)
                chain2.start(a.t)
                chain2.done(dve.reciprocal(rdev[:, a.b:a.b + 1], dev[:, a.b:a.b + 1]))
                dve.tensor_scalar(out=centred[:, a.b, :], in0=pre[:, a.b, :], scalar1=mean[:, a.b, 0:1], scalar2=rdev[:, a.b:a.b + 1],
                                  op0=ALU.subtract, op1=ALU.mult).then_inc(centred_ready, 1)

            def finish(a):
                dve.wait_ge(scaled_ready, a.t + 1)
                dve.tensor_tensor(out=K.h[:, ds(a.t * D, D)], in0=scaled[:, a.b, :], in1=shift[:, :], op=ALU.add).then_inc(h_ready, 1)
                take_moments(K, dve, a, h_ready, a.t + 1)

            take(tile(0))
            take(tile(1))
            centre(tile(0))

            def step(a):
                take(a)
                centre(a.at(-1))
                finish(a.at(-2))
            over(dve, 2, NT, step)
            centre(tile(NT - 1))
            finish(tile(NT - 2))
            finish(tile(NT - 1))


def take_moments(K, dve, a, sem, count):
    dve.wait_ge(sem, count)
    K.hold(dve)
    dve.bn_stats(out=K.moments[:, ds(a.t * 6, 6)], in_=K.h[:, ds(a.t * D, D)])


def prepare_norm(K, dve, sems):
    gathered, std_ready, rstd_ready = sems
    for t in range(NT):
        last = dve.bn_aggr(out=K.mv[:, t, :], in_=K.moments[:, t * 6:t * 6 + 6])
    last.then_inc(gathered, 1)
    dve.wait_ge(std_ready, 1)
    dve.reciprocal(K.rstd[:, :], K.std[:, :]).then_inc(rstd_ready, 1)
    dve.wait_ge(rstd_ready, 1)


def root_norm(K, act, sems):
    gathered, std_ready, _ = sems
    act.wait_ge(gathered, 1)
    act.activation(K.std[:, :], K.mv[:, :, 1], ACT.Sqrt, bias=K.eps_ln[:, 0:1]).then_inc(std_ready, 1)


def norm_sems(K, stage):
    return [K.sem(f"{stage}_{n}") for n in ("gathered", "std_ready", "rstd_ready")]


def normalise(K, dve, a, out):
    return dve.tensor_scalar(out=out, in0=K.h[:, ds(a.t * D, D)], scalar1=K.mv[:, ds(a.t, 1), 0],
                             scalar2=K.rstd[:, ds(a.t, 1)], op0=ALU.subtract, op1=ALU.mult)


def stage_attention0(K, weights):
    nc, ins = K.nc, K.ins
    HC = P // D0
    VW = D0 + 1
    with ExitStack() as ctx:
        sb = lambda name, shape, dt=F32: ctx.enter_context(nc.sbuf_tensor(name, shape, dt))
        wq, wk, wv, wo = weights.wq, weights.wk, weights.wv, weights.wo
        bqk, bv, bo = weights.bqk, weights.bv, weights.bo
        same = sb("a_same", [P, 4, P])
        head = sb("a_head", [P, HC])
        xn = sb("a_xn", [P, 2, D])
        xT = sb("a_xT", [P, 2, D])
        qk = sb("a_qk", [P, 2, 4, P])
        low = sb("a_low", [P, 2, 4, P])
        q = sb("a_q", [P, 2, DC, P])
        k = sb("a_k", [P, 2, DC, P])
        kh = sb("a_kh", [P, 2, DC * HC, P])
        v = sb("a_v", [P, 2, H0, VW])
        sc = sb("a_sc", [P, 2, 4, P])
        den = sb("a_den", [P, 2, H0])
        rden = sb("a_rden", [P, 2, H0])
        y = sb("a_y", [P, 2, D])
        yT = sb("a_yT", [P, 2, D])
        ps = lambda name: ctx.enter_context(nc.psum_tensor(name, [P, 512], F32))
        ps_x, ps_qk, ps_v, ps_o, ps_yT, ps_w = (ps("a_ps_" + n) for n in ("x", "qk", "v", "o", "yT", "w"))
        ps_s = [ps(f"a_ps_s{b}") for b in range(2)]
        loaded, masks, ones_set = weights.loaded, K.sem("a_masks"), K.sem("a_ones_set")
        norm = norm_sems(K, "a")
        names = ("xn_ready xT_ps xT_ready qk_ps v_ps qk_ready low_in low_ready q_ready k_ready kh_ready v_ready "
                 "s_ps s_ready o_ps o_read y_ready yT_ps yT_ready w_ps h_ready moved steps").split()
        S = {n: K.sem("a_" + n) for n in names}
        block = ctx.enter_context(nc.Block())

        @block.gpsimd
        def _(pool):
            batch_mask(pool, same, NPOS, masks, causal=False)
            head_mask(pool, head, HC, D0, masks, 3)
            pool.memset(v[:, :, :, D0:VW], 1.0).then_inc(ones_set, 1)

            def spread(a):
                pool.wait_ge(S["k_ready"], a.t + 1)
                wait(pool, S["s_ps"], (a.t - 1) * 4)
                for c in range(DC):
                    last = pool.tensor_tensor(out=kh[:, a.b, c * HC:(c + 1) * HC, :],
                                              in0=k[:, a.b, c:c + 1, :].broadcast_to([P, HC, P]),
                                              in1=head[:, :].rearrange("p (h a) -> p h a", a=1).broadcast_to([P, HC, P]), op=ALU.mult)
                last.then_inc(S["kh_ready"], 1)
            over(pool, 0, NT, spread)

        @block.scalar
        def _(act):
            root_norm(K, act, norm)

            def take_xT(a):
                act.wait_ge(S["xT_ps"], a.t + 1)
                wait(act, S["v_ps"], a.t - 1)
                act.activation(xT[:, a.b, :], ps_x[:, 0:D], ACT.Copy).then_inc(S["xT_ready"], 1)

            def exps(a):
                act.wait_ge(S["low_in"], a.t + 1)
                act.activation(low[:, a.b, :, :], low[:, a.b, :, :], ACT.Exp).then_inc(S["low_ready"], 1)

            def take_yT(a):
                act.wait_ge(S["yT_ps"], a.t + 1)
                wait(act, S["w_ps"], a.t - 1)
                act.activation(yT[:, a.b, :], ps_yT[:, 0:D], ACT.Copy).then_inc(S["yT_ready"], 1)

            def step(p):
                if has(p, -2):
                    take_yT(p.at(-2))
                if has(p, 0):
                    exps(p)
                if has(p, 1):
                    take_xT(p.at(1))
            take_xT(tile(0))
            passes(act, step)

        @block.tensor
        def _(pe):
            pe.wait_ge(loaded, weights.all)

            def tokens(a):
                pe.wait_ge(S["xn_ready"], a.t + 1)
                wait(pe, S["xT_ready"], a.t)
                for c in range(DC):
                    last = pe.transpose(ps_x[:, c * P:(c + 1) * P], xn[:, a.b, c * P:(c + 1) * P], K.ident[:, :])
                last.then_inc(S["xT_ps"], 1)

            def project(a):
                pe.wait_ge(S["xT_ready"], a.t + 1)
                wait(pe, S["qk_ready"], a.t)
                for j, wt in enumerate((wq, wk)):
                    for m in range(DC):
                        for c in range(DC):
                            last = pe.matmul(ps_qk[:, (j * DC + m) * P:(j * DC + m + 1) * P], wt[:, c, m * P:(m + 1) * P],
                                             xT[:, a.b, c * P:(c + 1) * P], start=(c == 0), stop=(c == DC - 1))
                last.then_inc(S["qk_ps"], 1)
                wait(pe, S["v_ready"], a.t)
                for c in range(DC):
                    last = pe.matmul(ps_v[:, 0:D], xT[:, a.b, c * P:(c + 1) * P], wv[:, c, :], start=(c == 0), stop=(c == DC - 1))
                last.then_inc(S["v_ps"], 1)

            def scores(a, g):
                n = a.t * 4 + g
                wait(pe, S["s_ready"], n - 1)
                for j in range(4):
                    hd = g * 4 + j
                    last = pe.matmul(ps_s[g % 2][:, j * P:(j + 1) * P], kh[:, a.b, hd, :], q[:, a.b, hd // HC, :], start=True, stop=True)
                last.then_inc(S["s_ps"], 1)

            def values(a, g):
                n = a.t * 4 + g
                pe.wait_ge(S["s_ready"], n + 1)
                if g == 0:
                    wait(pe, S["o_read"], a.t)
                for j in range(4):
                    hd = g * 4 + j
                    last = pe.matmul(ps_o[:, hd * VW:(hd + 1) * VW], sc[:, g % 2, j, :], v[:, a.b, hd, :], start=True, stop=True)
                last.then_inc(S["o_ps"], 1)

            def turned(a):
                pe.wait_ge(S["y_ready"], a.t + 1)
                wait(pe, S["yT_ready"], a.t)
                for c in range(DC):
                    last = pe.transpose(ps_yT[:, c * P:(c + 1) * P], y[:, a.b, c * P:(c + 1) * P], K.ident[:, :])
                last.then_inc(S["yT_ps"], 1)

            def combine(a):
                pe.wait_ge(S["yT_ready"], a.t + 1)
                wait(pe, S["h_ready"], a.t)
                for c in range(DC):
                    last = pe.matmul(ps_w[:, 0:D], yT[:, a.b, c * P:(c + 1) * P], wo[:, c, :], start=(c == 0), stop=(c == DC - 1))
                last.then_inc(S["w_ps"], 1)

            def step(p):
                a = p.at(-1)
                if has(p, 0):
                    project(p)
                if has(p, -1):
                    pe.wait_ge(S["kh_ready"], a.t + 1)
                    pe.wait_ge(S["q_ready"], a.t + 1)
                    pe.wait_ge(S["v_ready"], a.t + 1)
                    scores(a, 0)
                if has(p, -2):
                    turned(p.at(-2))
                if has(p, -1):
                    scores(a, 1)
                    values(a, 0)
                if has(p, -2):
                    combine(p.at(-2))
                if has(p, -1):
                    scores(a, 2)
                    values(a, 1)
                    scores(a, 3)
                    values(a, 2)
                if has(p, 1):
                    tokens(p.at(1))
                if has(p, -1):
                    values(a, 3)
            tokens(tile(0))
            passes(pe, step)

        @block.vector
        def _(dve):
            chain = Chain(dve, S["steps"])
            prepare_norm(K, dve, norm)
            dve.wait_ge(loaded, weights.all)
            dve.wait_ge(masks, 6)
            dve.wait_ge(ones_set, 1)

            def centre(a):
                wait(dve, S["xT_ps"], a.t - 1)
                normalise(K, dve, a, xn[:, a.b, :]).then_inc(S["xn_ready"], 1)

            def features_in(a):
                dve.wait_ge(S["qk_ps"], a.t + 1)
                wait(dve, S["s_ps"], (a.t - 1) * 4)
                wait(dve, S["kh_ready"], a.t - 1)
                dve.tensor_tensor(out=qk[:, a.b, :, :], in0=ps_qk[:, :].rearrange("p (c m) -> p c m", c=4),
                                  in1=bqk[:, :].rearrange("p (c a) -> p c a", a=1).broadcast_to([P, 4, P]),
                                  op=ALU.add).then_inc(S["qk_ready"], 1)
                dve.wait_ge(S["qk_ready"], a.t + 1)
                dve.tensor_scalar(out=low[:, a.b, :, :], in0=qk[:, a.b, :, :], scalar1=0.0, scalar2=None, op0=ALU.min).then_inc(S["low_in"], 1)
                dve.wait_ge(S["v_ps"], a.t + 1)
                wait(dve, S["o_ps"], (a.t - 1) * 4)
                dve.tensor_tensor(out=v[:, a.b, :, 0:D0], in0=ps_v[:, 0:D].rearrange("p (h e) -> p h e", h=H0),
                                  in1=bv[:, :].rearrange("p (h e) -> p h e", h=H0), op=ALU.add).then_inc(S["v_ready"], 1)

            def features_out(a):
                dve.wait_ge(S["low_ready"], a.t + 1)
                dve.scalar_tensor_tensor(out=k[:, a.b, :, :], in0=qk[:, a.b, 2:4, :], scalar=0.0, in1=low[:, a.b, 2:4, :],
                                         op0=ALU.max, op1=ALU.add).then_inc(S["k_ready"], 1)
                dve.scalar_tensor_tensor(out=q[:, a.b, :, :], in0=qk[:, a.b, 0:2, :], scalar=0.0, in1=low[:, a.b, 0:2, :],
                                         op0=ALU.max, op1=ALU.add).then_inc(S["q_ready"], 1)

            def masked(a, g):
                n = a.t * 4 + g
                dve.wait_ge(S["s_ps"], n + 1)
                wait(dve, S["o_ps"], n - 1)
                dve.tensor_tensor(out=sc[:, g % 2, :, :], in0=ps_s[g % 2][:, :].rearrange("p (j m) -> p j m", j=4),
                                  in1=same[:, :, :], op=ALU.mult).then_inc(S["s_ready"], 1)

            def normed(a):
                chain.start(a.t * 2)
                dve.wait_ge(S["o_ps"], a.t * 4 + 4)
                wait(dve, S["yT_ps"], a.t - 1)
                o = ps_o[:, 0:H0 * VW].rearrange("p (h e) -> p h e", h=H0)
                chain.done(dve.tensor_scalar(out=den[:, a.b, :], in0=o[:, :, D0], scalar1=1e-6, scalar2=None, op0=ALU.add))
                chain.done(dve.reciprocal(rden[:, a.b, :], den[:, a.b, :]))
                dve.tensor_tensor(out=y[:, a.b, :].rearrange("p (h e) -> p h e", h=H0), in0=o[:, :, 0:D0],
                                  in1=rden[:, a.b, :].rearrange("p (h a) -> p h a", a=1).broadcast_to([P, H0, D0]),
                                  op=ALU.mult).then_inc(S["y_ready"], 1)
                dve.wait_ge(S["y_ready"], a.t + 1)
                dve.sem_inc(S["o_read"], 1)

            def residual(a):
                dve.wait_ge(S["w_ps"], a.t + 1)
                hs = K.h[:, ds(a.t * D, D)]
                dve.tensor_tensor(out=hs, in0=ps_w[:, 0:D], in1=hs, op=ALU.add).then_inc(S["h_ready"], 1)
                dve.wait_ge(S["h_ready"], a.t + 1)
                dve.tensor_tensor(out=hs, in0=hs, in1=bo[:, :], op=ALU.add).then_inc(S["moved"], 1)
                take_moments(K, dve, a, S["moved"], a.t + 1)

            def step(p):
                a = p.at(-1)
                if has(p, 1):
                    centre(p.at(1))
                if has(p, 0):
                    features_in(p)
                if has(p, -1):
                    masked(a, 0)
                if has(p, 0):
                    features_out(p)
                if has(p, -1):
                    masked(a, 1)
                if has(p, -2):
                    residual(p.at(-2))
                if has(p, -1):
                    masked(a, 2)
                    masked(a, 3)
                    normed(a)
            centre(tile(0))
            passes(dve, step)


def batch_mask(pool, m, width, sem, causal):
    pool.memset(m[:, :, :], 1.0).then_inc(sem, 1)
    pool.wait_ge(sem, 1)
    v = m[:, :, :].rearrange("p a (g s) -> p a g s", s=width)
    G = P // width
    pool.affine_select(out=v, in_=v, compare_op=ALU.is_ge, fill=0.0, base=0,
                       pattern=[[0, 4], [-width, G], [0, width]], channel_multiplier=1).then_inc(sem, 1)
    pool.wait_ge(sem, 2)
    pool.affine_select(out=v, in_=v, compare_op=ALU.is_ge, fill=0.0, base=0 if causal else width - 1,
                       pattern=[[0, 4], [width, G], [1 if causal else 0, width]], channel_multiplier=-1).then_inc(sem, 1)


def head_mask(pool, m, heads, width, sem, n):
    pool.memset(m[:, :], 1.0).then_inc(sem, 1)
    pool.wait_ge(sem, n + 1)
    pool.affine_select(out=m[:, :], in_=m[:, :], compare_op=ALU.is_ge, fill=0.0, base=0,
                       pattern=[[-width, heads]], channel_multiplier=1).then_inc(sem, 1)
    pool.wait_ge(sem, n + 2)
    pool.affine_select(out=m[:, :], in_=m[:, :], compare_op=ALU.is_ge, fill=0.0, base=width - 1,
                       pattern=[[width, heads]], channel_multiplier=-1).then_inc(sem, 1)


def stage_gate(K, name, experts, route, xT, plan=None, weights=None, later=()):
    nc, ins = K.nc, K.ins
    E = experts
    with ExitStack() as ctx:
        sb = lambda n, shape, dt=F32: ctx.enter_context(nc.sbuf_tensor(name + n, shape, dt))
        wg = sb("wg", [P, DC, E])
        bias = sb("bias", [P, E])
        rev = sb("rev", [P, E])
        xn = sb("xn", [P, 2, D])
        xt = sb("xt", [P, 2, D])
        work = {n: sb(n, [P, NT, E]) for n in ("score", "left", "eq", "place", "sel1", "sel2")}
        one = {n: sb(n, [P, NT]) for n in ("top", "last", "sum", "rsum")}
        ps_x = [ctx.enter_context(nc.psum_tensor(f"{name}ps_x{b}", [P, 512], F32)) for b in range(2)]
        ps_g = ctx.enter_context(nc.psum_tensor(name + "ps_g", [P, 512], F32))
        ps_r = ctx.enter_context(nc.psum_tensor(name + "ps_r", [P, 512], F32))
        loaded, rev_set = K.sem(name + "loaded"), K.sem(name + "rev_set")
        norm = norm_sems(K, name)
        S = {n: K.sem(name + n) for n in
             "xn_ready xT_ps xt_ready g_ps kept exp_in exp_ready steps hi_ready lo_ready hiT_ready sel_ready rank_ps".split()}
        if plan:
            plan.allocate(sb)
            plan.sel = work["eq"]
        block = ctx.enter_context(nc.Block())

        @block.sync
        def _(sp):
            with nc.allow_non_contiguous_dma(reason="a gate of 8 columns, once"):
                sp.dma_start(wg[:, :, :], ins[name + "gate"].rearrange("(c p) e -> p c e", p=P)).then_inc(loaded, 16)
            if name + "gate_bias" in ins:
                sp.dma_start(bias[:, :], ins[name + "gate_bias"].partition_broadcast(P)).then_inc(loaded, 16)
            if weights:
                weights.load(sp, E1, 0)
            for w in later:
                w.load(sp, ins)

        @block.gpsimd
        def _(pool):
            for e in range(E):
                last = pool.memset(rev[:, e:e + 1], float(E - e))
            last.then_inc(rev_set, 1)
            if plan:
                plan.constants(pool)

            def lows(a):
                pool.wait_ge(S["hiT_ready"], a.t + 1)
                K.hold(pool)
                pool.tensor_tensor(out=xT[:, 1, :, ds(a.t * P, P)], in0=xt[:, a.b, :].rearrange("p (c m) -> p c m", c=DC),
                                   in1=xT[:, 0, :, ds(a.t * P, P)], op=ALU.subtract).then_inc(S["kept"], 1)

            def keep(a):
                pool.wait_ge(S["xt_ready"], a.t + 1)
                K.hold(pool)
                src = xt[:, a.b, :].rearrange("p (c m) -> p c m", c=DC)
                pool.tensor_copy(out=xT[:, :, ds(a.t * P, P)], in_=src).then_inc(S["kept"], 1)
            over(pool, 0, NT, lows if plan else keep)
            if weights:
                weights.take_low(pool, 0, 0, 2, 1)

        @block.scalar
        def _(act):
            root_norm(K, act, norm)

            def take(a):
                act.wait_ge(S["xT_ps"], a.t + 1)
                wait(act, S["g_ps"], a.t - 1)
                wait(act, S["kept"], a.t - 1)
                act.activation(xt[:, a.b, :], ps_x[a.b][:, 0:D], ACT.Copy).then_inc(S["xt_ready"], 1)
                if plan:
                    act.activation(xT[:, 0, :, ds(a.t * P, P)], ps_x[a.b][:, 0:D].rearrange("p (c m) -> p c m", c=DC),
                                   ACT.Copy).then_inc(S["hiT_ready"], 1)
            def high(a):
                act.wait_ge(S["xn_ready"], a.t + 1)
                K.hold(act)
                act.activation(plan.rows[:, ds(a.t * 2 * D, D)], xn[:, a.b, :], ACT.Copy).then_inc(S["hi_ready"], 1)

            def step(a):
                if plan:
                    high(a)
                take(a)
            over(act, 0, NT, step)
            if weights:
                for kc in range(DC):
                    weights.take_high_up(act, 0, 2, 1, kc)
                weights.take_high_down(act, 0, 2)
            act.wait_ge(S["exp_in"], 1)
            act.activation(work["score"][:, :, :], work["score"][:, :, :], ACT.Exp).then_inc(S["exp_ready"], 1)

        @block.tensor
        def _(pe):
            pe.wait_ge(loaded, 16)

            def transposes(a):
                pe.wait_ge(S["xn_ready"], a.t + 1)
                wait(pe, S["hiT_ready" if plan else "xt_ready"], a.t - 1)
                for c in range(DC):
                    last = pe.transpose(ps_x[a.b][:, c * P:(c + 1) * P], xn[:, a.b, c * P:(c + 1) * P], K.ident[:, :])
                last.then_inc(S["xT_ps"], 1)

            def logits(a):
                pe.wait_ge(S["xt_ready"], a.t + 1)
                for c in range(DC):
                    last = pe.matmul(ps_g[:, ds(a.t * E, E)], xt[:, a.b, c * P:(c + 1) * P], wg[:, c, :],
                                     start=(c == 0), stop=(c == DC - 1))
                last.then_inc(S["g_ps"], 1)

            def step(a):
                transposes(a)
                logits(a.at(-1))
            transposes(tile(0))
            over(pe, 1, NT, step)
            logits(tile(NT - 1))
            if plan:
                plan.ranks(pe, ps_r, S)

        @block.vector
        def _(dve):
            chain = Chain(dve, S["steps"])
            prepare_norm(K, dve, norm)
            dve.wait_ge(loaded, 16 * (1 + (name + "gate_bias" in ins)))
            dve.wait_ge(rev_set, 1)

            def centre(a):
                wait(dve, S["xT_ps"], a.t - 1)
                if plan:
                    wait(dve, S["lo_ready"], a.t - 1)
                normalise(K, dve, a, xn[:, a.b, :]).then_inc(S["xn_ready"], 1)

            def low(a):
                dve.wait_ge(S["hi_ready"], a.t + 1)
                K.hold(dve)
                row = a.t * 2 * D
                dve.tensor_tensor(out=plan.rows[:, ds(row + D, D)], in0=xn[:, a.b, :], in1=plan.rows[:, ds(row, D)],
                                  op=ALU.subtract).then_inc(S["lo_ready"], 1)

            def step(a):
                centre(a)
                if plan and has(a, -1):
                    low(a.at(-1))
            over(dve, 0, NT, step)
            if plan:
                low(tile(NT - 1))
            dve.wait_ge(S["g_ps"], NT)
            logit = ps_g[:, 0:NT * E].rearrange("p (t e) -> p t e", t=NT)
            route(dve, chain, logit, bias, rev, work, one, S)
            if plan:
                plan.make(dve, chain, work, ps_r, S)


def per_token(m):
    t, e = NT, E0
    return m[:, :].rearrange("p (t a) -> p t a", a=1).broadcast_to([P, t, e])


def top_two(dve, chain, value, rev, work, one):
    left, eq, place = work["left"], work["eq"], work["place"]
    revs = rev[:, :].rearrange("p (a e) -> p a e", a=1).broadcast_to([P, NT, E0])
    for n, sel in enumerate((work["sel1"], work["sel2"])):
        src = value if n == 0 else left
        chain.done(dve.tensor_reduce(out=one["top"][:, :], in_=src[:, :, :], axis=AX, op=ALU.max))
        chain.done(dve.tensor_tensor(out=eq[:, :, :], in0=src[:, :, :], in1=per_token(one["top"]), op=ALU.is_ge))
        chain.done(dve.tensor_tensor(out=place[:, :, :], in0=eq[:, :, :], in1=revs, op=ALU.mult))
        chain.done(dve.tensor_reduce(out=one["last"][:, :], in_=place[:, :, :], axis=AX, op=ALU.max))
        chain.done(dve.tensor_tensor(out=sel[:, :, :], in0=place[:, :, :], in1=per_token(one["last"]), op=ALU.is_equal))
        if n == 0:
            chain.done(dve.scalar_tensor_tensor(out=left[:, :, :], in0=sel[:, :, :], scalar=-1e30, in1=value[:, :, :],
                                                op0=ALU.mult, op1=ALU.add))
    chain.done(dve.tensor_tensor(out=eq[:, :, :], in0=work["sel1"][:, :, :], in1=work["sel2"][:, :, :], op=ALU.add))
    return eq


def route0(gate):
    def route(dve, chain, logit, bias, rev, work, one, S):
        score, left = work["score"], work["sel2"]
        dve.tensor_scalar(out=score[:, :, :], in0=logit, scalar1=-1.0, scalar2=None, op0=ALU.mult).then_inc(S["exp_in"], 1)
        dve.wait_ge(S["exp_ready"], 1)
        chain.done(dve.tensor_scalar(out=left[:, :, :], in0=score[:, :, :], scalar1=1.0, scalar2=None, op0=ALU.add))
        chain.done(dve.reciprocal(score[:, :, :], left[:, :, :]))
        biased = work["left"]
        chain.done(dve.tensor_tensor(out=biased[:, :, :], in0=score[:, :, :],
                                     in1=bias[:, :].rearrange("p (a e) -> p a e", a=1).broadcast_to([P, NT, E0]), op=ALU.add))
        sel = top_two(dve, chain, biased, rev, work, one)
        dve.tensor_tensor(out=gate[:, :, :].rearrange("p e t -> p t e"), in0=score[:, :, :], in1=sel[:, :, :], op=ALU.mult)
    return route


def route1():
    def route(dve, chain, logit, bias, rev, work, one, S):
        score, prob = work["score"], work["left"]
        chain.done(dve.tensor_reduce(out=one["top"][:, :], in_=logit, axis=AX, op=ALU.max))
        dve.tensor_tensor(out=score[:, :, :], in0=logit, in1=per_token(one["top"]), op=ALU.subtract).then_inc(S["exp_in"], 1)
        dve.wait_ge(S["exp_ready"], 1)
        chain.done(dve.tensor_reduce(out=one["sum"][:, :], in_=score[:, :, :], axis=AX, op=ALU.add))
        chain.done(dve.reciprocal(one["rsum"][:, :], one["sum"][:, :]))
        chain.done(dve.tensor_tensor(out=prob[:, :, :], in0=score[:, :, :], in1=per_token(one["rsum"]), op=ALU.mult))
        chain.done(dve.tensor_copy(out=score[:, :, :], in_=prob[:, :, :]))
        sel = top_two(dve, chain, prob, rev, work, one)
        dve.sem_inc(S["sel_ready"], 1)
        chain.done(dve.tensor_tensor(out=work["place"][:, :, :], in0=score[:, :, :], in1=sel[:, :, :], op=ALU.mult))
        chain.done(dve.tensor_reduce(out=one["sum"][:, :], in_=work["place"][:, :, :], axis=AX, op=ALU.add))
        chain.done(dve.reciprocal(one["rsum"][:, :], one["sum"][:, :]))
        chain.done(dve.tensor_tensor(out=prob[:, :, :], in0=work["place"][:, :, :], in1=per_token(one["rsum"]), op=ALU.mult))
    return route


class Plan:

    def __init__(self, nc, ctx, K):
        sb = lambda n, shape, dt=F32: ctx.enter_context(nc.sbuf_tensor("plan_" + n, shape, dt))
        self.rows = sb("rows", [P, NT * 2 * D], BF16)
        self.slot = sb("slot", [P, 2 * NT], mybir.dt.uint32)
        self.weight = sb("weight", [P, 2 * NT])
        self.expert = sb("expert", [P, NB], mybir.dt.int32)
        self.ready = K.sem("plan_constants")

    def allocate(self, sb):
        self.before = sb("before", [P, P])
        self.ones = sb("ones", [P, P])
        self.index = sb("index", [P, NB])
        self.edge = sb("edge", [P, TOK // SB])
        self.total = sb("total", [P, NT, E1])
        self.run = sb("run", [P, NT + 1, E1])
        self.over = sb("over", [P, E1, TOK // SB])
        self.blocks = sb("blocks", [P, E1])
        self.first = sb("first", [P, E1 + 1])
        self.place = sb("place2", [P, NT, E1])
        self.slotf = sb("slotf", [P, 2, NT])
        self.past = sb("past", [P, NB, E1])
        self.expertf = sb("expertf", [P, NB])

    def constants(self, pool):
        pool.memset(self.ones[:, :], 1.0).then_inc(self.ready, 1)
        pool.wait_ge(self.ready, 1)
        pool.affine_select(out=self.before[:, :], in_=self.ones[:, :], compare_op=ALU.is_gt, fill=0.0, base=0,
                           pattern=[[1, P]], channel_multiplier=-1)
        for j in range(NB):
            pool.memset(self.index[:, j:j + 1], float(j))
        for j in range(TOK // SB):
            last = pool.memset(self.edge[:, j:j + 1], float(j * SB))
        last.then_inc(self.ready, 1)

    def ranks(self, pe, ps_r, S):
        pe.wait_ge(self.ready, 2)
        pe.wait_ge(S["sel_ready"], 1)
        sel = self.sel[:, :, :].rearrange("p t e -> p (t e)")
        pe.matmul(ps_r[:, 0:NT * E1], self.before[:, :], sel, start=True, stop=True)
        pe.matmul(ps_r[:, NT * E1:2 * NT * E1], self.ones[:, :], sel, start=True, stop=True).then_inc(S["rank_ps"], 1)

    def make(self, dve, chain, work, ps_r, S):
        dve.wait_ge(S["rank_ps"], 1)
        dve.wait_ge(self.ready, 2)
        rank = ps_r[:, 0:NT * E1].rearrange("p (t e) -> p t e", t=NT)
        chain.done(dve.tensor_copy(out=self.total[:, :, :], in_=ps_r[:, NT * E1:2 * NT * E1].rearrange("p (t e) -> p t e", t=NT)))
        chain.done(dve.memset(self.run[:, 0, :], 0.0))
        for t in range(NT):
            chain.done(dve.tensor_tensor(out=self.run[:, t + 1, :], in0=self.run[:, t, :], in1=self.total[:, t, :], op=ALU.add))
        J = TOK // SB
        chain.done(dve.tensor_tensor(out=self.over[:, :, :], in0=self.run[:, NT, :].rearrange("p (e a) -> p e a", a=1).broadcast_to([P, E1, J]),
                                     in1=self.edge[:, :].rearrange("p (a j) -> p a j", a=1).broadcast_to([P, E1, J]), op=ALU.is_gt))
        chain.done(dve.tensor_reduce(out=self.blocks[:, :], in_=self.over[:, :, :], axis=AX, op=ALU.add))
        chain.done(dve.memset(self.first[:, 0:1], 0.0))
        for e in range(E1):
            chain.done(dve.tensor_tensor(out=self.first[:, e + 1:e + 2], in0=self.first[:, e:e + 1], in1=self.blocks[:, e:e + 1], op=ALU.add))
        firsts = self.first[:, 0:E1].rearrange("p (a e) -> p a e", a=1).broadcast_to([P, NT, E1])
        chain.done(dve.scalar_tensor_tensor(out=self.place[:, :, :], in0=firsts, scalar=float(SB), in1=self.run[:, 0:NT, :],
                                            op0=ALU.mult, op1=ALU.add))
        chain.done(dve.tensor_tensor(out=self.place[:, :, :], in0=rank, in1=self.place[:, :, :], op=ALU.add))
        for k, sel in enumerate((work["sel1"], work["sel2"])):
            chain.done(dve.tensor_tensor(out=work["place"][:, :, :], in0=sel[:, :, :], in1=self.place[:, :, :], op=ALU.mult))
            chain.done(dve.tensor_reduce(out=self.slotf[:, k, :], in_=work["place"][:, :, :], axis=AX, op=ALU.add))
            chain.done(dve.tensor_tensor(out=work["place"][:, :, :], in0=sel[:, :, :], in1=work["left"][:, :, :], op=ALU.mult))
            chain.done(dve.tensor_reduce(out=self.weight[:, k * NT:(k + 1) * NT], in_=work["place"][:, :, :], axis=AX, op=ALU.add))
        dve.tensor_copy(out=self.slot[:, :], in_=self.slotf[:, :, :].rearrange("p k t -> p (k t)"))
        chain.done(dve.tensor_tensor(out=self.past[:, :, :], in0=self.index[:, :].rearrange("p (n a) -> p n a", a=1).broadcast_to([P, NB, E1]),
                                     in1=self.first[:, 1:E1 + 1].rearrange("p (a e) -> p a e", a=1).broadcast_to([P, NB, E1]), op=ALU.is_ge))
        chain.done(dve.tensor_reduce(out=self.expertf[:, :], in_=self.past[:, :, :], axis=AX, op=ALU.add))
        dve.tensor_scalar(out=self.expert[:, :], in0=self.expertf[:, :], scalar1=float(E1 - 1), scalar2=None, op0=ALU.min)


class ExpertWeights:
    UP, DOWN = W1, W1 + HF1 * D
    WORDS = W1 + HF1 * D + D

    def __init__(self, nc, ctx, K):
        self.ins = K.ins
        self.f = ctx.enter_context(nc.sbuf_tensor("w1_f", [P, 2, self.WORDS], F32))
        self.b = ctx.enter_context(nc.sbuf_tensor("w1_b", [P, 3, 2, self.WORDS], BF16))
        self.loaded = [K.sem(f"w1_loaded{s}") for s in range(2)]
        self.high_up, self.high_down, self.low_up, self.low_down = (K.sem("w1_" + n) for n in ("high_up", "high_down", "low_up", "low_down"))
        self.hold = K.hold

    def load(self, eng, expert, s):
        f, up, down, words = self.f, self.UP, self.DOWN, self.WORDS
        eng.dma_start(f[:, s, 0:up], self.ins["f1_up"][ds(expert * P, P), :]).then_inc(self.loaded[s], 16)
        eng.dma_start(f[:, s, up:down], self.ins["f1_down"][ds(expert * P, P), :]).then_inc(self.loaded[s], 16)
        eng.dma_start(f[0:HT1, s, down:words], self.ins["f1_rest"][ds(expert * HT1, HT1), :]).then_inc(self.loaded[s], 16)

    def take_high_up(self, act, s, slot, rounds, kc):
        act.wait_ge(self.loaded[s], rounds * 48)
        w0, w1 = kc * 2 * HID1, (kc + 1) * 2 * HID1
        ins = act.activation(self.b[:, slot, 0, w0:w1], self.f[:, s, w0:w1], ACT.Copy)
        if kc == DC - 1:
            ins.then_inc(self.high_up, 1)

    def take_high_down(self, act, s, slot):
        f, b, up, down, words = self.f, self.b, self.UP, self.DOWN, self.WORDS
        act.activation(b[:, slot, 0, up:down], f[:, s, up:down], ACT.Copy)
        act.activation(b[0:HT1, slot, 0, down:words], f[0:HT1, s, down:words], ACT.Copy).then_inc(self.high_down, 1)

    def take_low(self, pool, use, s, slot, rounds):
        f, b, up, down, words = self.f, self.b, self.UP, self.DOWN, self.WORDS
        pool.wait_ge(self.loaded[s], rounds * 48)
        pool.wait_ge(self.high_up, use + 1)
        self.hold(pool)
        pool.tensor_tensor(out=b[:, slot, 1, 0:up], in0=f[:, s, 0:up], in1=b[:, slot, 0, 0:up], op=ALU.subtract).then_inc(self.low_up, 1)
        pool.wait_ge(self.high_down, use + 1)
        self.hold(pool)
        pool.tensor_tensor(out=b[:, slot, 1, up:down], in0=f[:, s, up:down], in1=b[:, slot, 0, up:down], op=ALU.subtract)
        pool.tensor_tensor(out=b[0:HT1, slot, 1, down:words], in0=f[0:HT1, s, down:words], in1=b[0:HT1, slot, 0, down:words],
                           op=ALU.subtract).then_inc(self.low_down, 1)


def stage_shared0(K, xT, weights, gate, early):
    nc, ins = K.nc, K.ins
    HB = chunks(HID0)
    NH = len(HB)
    with ExitStack() as ctx:
        sb = lambda n, shape, dt=F32: ctx.enter_context(nc.sbuf_tensor("s_" + n, shape, dt))
        wu, wd = weights.wu, weights.wd
        pos = sb("pos", [P, 4, GT])
        hid = sb("hid", [P, 2, NH, GT])
        ps = lambda n: ctx.enter_context(nc.psum_tensor("s_" + n, [P, 512], F32))
        ps_u = [ps(f"u{b}") for b in range(4)]
        ps_d = [ps(f"d{b}") for b in range(TPG)]
        S = {n: K.sem("s_" + n) for n in "up_ps relu_ready hid_ready down_ps added".split()}
        block = ctx.enter_context(nc.Block())

        @block.sync
        def _(sp):
            for e in range(2):
                early.load_weights(sp, ins, tile(e))
            sp.wait_ge(early.gT_ready, 1)
            sp.dma_start(early.gates.rearrange("e (t m) -> (e t) m", t=NT), early.gT[:, :]).then_inc(early.gates_stored, 16)
            sp.wait_ge(early.gates_stored, 16)
            for e in range(2):
                early.load_gates(sp, tile(e))

        @block.tensor
        def _(pe):
            pe.transpose(ps_d[0][:, 0:P], gate[:, :, :].rearrange("p e t -> p (e t)"), K.ident[:, :]).then_inc(early.gT_ps, 1)
            pe.wait_ge(weights.loaded, weights.all)

            def up(g):
                for c, (m, w) in enumerate(HB):
                    q = g * NH + c
                    wait(pe, S["relu_ready"], q - 3)
                    for kc in range(DC):
                        last = pe.matmul(ps_u[q % 4][0:w, :], wu[:, kc, m * P:m * P + w], xT[:, kc, g * GT:(g + 1) * GT],
                                         start=(kc == 0), stop=(kc == DC - 1))
                    last.then_inc(S["up_ps"], 1)

            def down(g):
                pe.wait_ge(S["hid_ready"], g * NH + NH)
                if g == 0:
                    pe.wait_ge(early.gT_ready, 1)
                for j in range(TPG):
                    wait(pe, S["added"], g * TPG + j - 3)
                    for c, (m, w) in enumerate(HB):
                        last = pe.matmul(ps_d[j][:, 0:D], hid[0:w, g % 2, c, j * P:(j + 1) * P], wd[0:w, c, :],
                                         start=(c == 0), stop=(c == NH - 1))
                    last.then_inc(S["down_ps"], 1)
            up(0)
            for g in range(1, NG):
                up(g)
                down(g - 1)
            down(NG - 1)

        @block.scalar
        def _(act):
            act.wait_ge(early.gT_ps, 1)
            act.activation(early.gT[:, :], ps_d[0][:, 0:P], ACT.Copy).then_inc(early.gT_ready, 1)
            for g in range(NG):
                for c, (m, w) in enumerate(HB):
                    q = g * NH + c
                    act.wait_ge(S["up_ps"], q + 1)
                    wait(act, S["hid_ready"], q - 3)
                    act.activation(pos[0:w, q % 4, :], ps_u[q % 4][0:w, :], ACT.Relu).then_inc(S["relu_ready"], 1)

        @block.vector
        def _(dve):
            def square(g):
                for c, (m, w) in enumerate(HB):
                    q = g * NH + c
                    dve.wait_ge(S["relu_ready"], q + 1)
                    if c == 0:
                        wait(dve, S["down_ps"], (g - 1) * TPG)
                    dve.tensor_tensor(out=hid[0:w, g % 2, c, :], in0=pos[0:w, q % 4, :], in1=pos[0:w, q % 4, :],
                                      op=ALU.mult).then_inc(S["hid_ready"], 1)

            def add(g):
                for j in range(TPG):
                    t = g * TPG + j
                    dve.wait_ge(S["down_ps"], t + 1)
                    hs = K.h[:, t * D:(t + 1) * D]
                    dve.tensor_tensor(out=hs, in0=ps_d[j][:, 0:D], in1=hs, op=ALU.add).then_inc(S["added"], 1)
            square(0)
            for g in range(1, NG):
                square(g)
                add(g - 1)
            add(NG - 1)


def stage_experts0(K, xT, early, later):
    nc, ins = K.nc, K.ins
    HB = chunks(HID0)
    NH = len(HB)
    NO = TPG // 2
    with ExitStack() as ctx:
        sb = lambda n, shape, dt=F32: ctx.enter_context(nc.sbuf_tensor("e_" + n, shape, dt))
        wu_f, wd_f, grow = early.wu, early.wd, early.grow
        wu, wd = sb("wu", [P, 2, DC, HID0], BF16), sb("wd", [P, 2, NH, D], BF16)
        xe = sb("xe", [P, 2, DC, GT], BF16)
        pos = sb("pos", [P, 4, GT], BF16)
        hid = sb("hid", [P, 2, NH, GT], BF16)
        rnd = sb("rnd", [P, 4, 2 * D], BF16)
        ps = lambda n: ctx.enter_context(nc.psum_tensor("e_" + n, [P, 512], F32))
        ps_u = [ps(f"u{b}") for b in range(4)]
        ps_d = [ps(f"d{b}") for b in range(4)]
        loaded, grow_loaded = early.loaded, early.grow_loaded
        S = {n: K.sem("e_" + n) for n in
             "cast_up cast xe_ready up_ps relu_ready hid_ready down_ps rnd_ready added".split()}
        block = ctx.enter_context(nc.Block())

        def units(eng, step):
            over(eng, 0, E0 * NG, step, per=2 * NG)

        @block.sync
        def _(sp):
            def load(e):
                wait(sp, S["xe_ready"], (e.t - 1) * NG)
                early.load_gates(sp, e)
                wait(sp, S["cast"], e.t - 1)
                early.load_weights(sp, ins, e)
            over(sp, 2, E0, load)
            for weights in later:
                weights.load(sp, ins)

        @block.gpsimd
        def _(pool):
            def step(n):
                if not (isinstance(n.t, int) and n.t == 0):
                    add(n.at(-1))

            def add(n):
                g = n.k % NG
                for j in range(NO):
                    q, t = n.t * NO + j, g * TPG + 2 * j
                    pool.wait_ge(S["rnd_ready"], q + 1)
                    wait(pool, S["added"], q - NG * NO + 1)
                    hs = K.h[:, t * D:(t + 2) * D]
                    pool.tensor_tensor(out=hs, in0=hs, in1=rnd[:, (n.k * NO + j) % 4, :], op=ALU.add).then_inc(S["added"], 1)
            for weights in later:
                weights.clear(pool)
            units(pool, step)
            add(tile(E0 * NG - 1, 2 * NG))

        @block.tensor
        def _(pe):
            def up(n):
                eb, g = n.k // NG, n.k % NG
                if g == 0:
                    pe.wait_ge(S["cast_up"], n.turn * 2 + eb + 1)
                pe.wait_ge(S["xe_ready"], n.t + 1)
                for c, (m, w) in enumerate(HB):
                    q = n.t * NH + c
                    wait(pe, S["relu_ready"], q - 3)
                    for kc in range(DC):
                        last = pe.matmul(ps_u[(n.k * NH + c) % 4][0:w, :], wu[:, eb, kc, m * P:m * P + w], xe[:, n.b, kc, :],
                                         start=(kc == 0), stop=(kc == DC - 1))
                    last.then_inc(S["up_ps"], 1)

            def down(n):
                eb, g = n.k // NG, n.k % NG
                if g == 0:
                    pe.wait_ge(S["cast"], n.turn * 2 + eb + 1)
                pe.wait_ge(S["hid_ready"], n.t * NH + NH)
                for j in range(NO):
                    wait(pe, S["rnd_ready"], n.t * NO + j - 3)
                    for i in range(2):
                        for c, (m, w) in enumerate(HB):
                            last = pe.matmul(ps_d[(n.k * NO + j) % 4][:, i * D:(i + 1) * D],
                                             hid[0:w, n.b, c, (2 * j + i) * P:(2 * j + i + 1) * P], wd[0:w, eb, c, :],
                                             start=(c == 0), stop=(c == NH - 1))
                    last.then_inc(S["down_ps"], 1)

            def step(n):
                up(n)
                if not (isinstance(n.t, int) and n.t == 0):
                    down(n.at(-1))
            units(pe, step)
            down(tile(E0 * NG - 1, 2 * NG))

        @block.scalar
        def _(act):
            def relus(n):
                for c, (m, w) in enumerate(HB):
                    q, slot = n.t * NH + c, (n.k * NH + c) % 4
                    act.wait_ge(S["up_ps"], q + 1)
                    wait(act, S["hid_ready"], q - 3)
                    act.activation(pos[0:w, slot, :], ps_u[slot][0:w, :], ACT.Relu).then_inc(S["relu_ready"], 1)

            def rounds(n):
                for j in range(NO):
                    q, slot = n.t * NO + j, (n.k * NO + j) % 4
                    act.wait_ge(S["down_ps"], q + 1)
                    wait(act, S["added"], q - 3)
                    act.activation(rnd[:, slot, :], ps_d[slot][:, :], ACT.Copy).then_inc(S["rnd_ready"], 1)

            def step(n):
                relus(n)
                if not (isinstance(n.t, int) and n.t == 0):
                    rounds(n.at(-1))
            units(act, step)
            rounds(tile(E0 * NG - 1, 2 * NG))

        @block.vector
        def _(dve):
            def scale(n):
                eb, g = n.k // NG, n.k % NG
                if g == 0:
                    dve.wait_ge(grow_loaded[eb], n.turn * 16 + 16)
                wait(dve, S["up_ps"], (n.t - 1) * NH)
                dve.tensor_tensor(out=xe[:, n.b, :, :], in0=xT[:, :, g * GT:(g + 1) * GT],
                                  in1=grow[:, eb:eb + 1, g * GT:(g + 1) * GT].broadcast_to([P, DC, GT]),
                                  op=ALU.mult).then_inc(S["xe_ready"], 1)

            def square(n):
                for c, (m, w) in enumerate(HB):
                    q, slot = n.t * NH + c, (n.k * NH + c) % 4
                    dve.wait_ge(S["relu_ready"], q + 1)
                    if c == 0:
                        wait(dve, S["down_ps"], (n.t - 1) * NO)
                    dve.tensor_tensor(out=hid[0:w, n.b, c, :], in0=pos[0:w, slot, :], in1=pos[0:w, slot, :],
                                      op=ALU.mult).then_inc(S["hid_ready"], 1)

            def cast(eb, rounds, units_before):
                dve.wait_ge(loaded[eb], rounds * 48)
                wait(dve, S["down_ps"], units_before * NO)
                K.hold(dve)
                last = HB[-1][1]
                dve.tensor_copy(out=wu[:, eb, :, :], in_=wu_f[:, eb, :, :]).then_inc(S["cast_up"], 1)
                dve.tensor_copy(out=wd[:, eb, 0:NH - 1, :], in_=wd_f[:, eb, 0:NH - 1, :])
                dve.tensor_copy(out=wd[0:last, eb, NH - 1, :], in_=wd_f[0:last, eb, NH - 1, :]).then_inc(S["cast"], 1)

            def step(n):
                eb, g = n.k // NG, n.k % NG
                scale(n)
                if not (isinstance(n.t, int) and n.t == 0):
                    square(n.at(-1))
                if g == 2 and not (isinstance(n.t, int) and n.t == E0 * NG - 2):
                    cast(1 - eb, n.turn + 1 + eb, n.t - 2)
            cast(0, 1, 0)
            over(dve, 0, (E0 - 2) * NG, step, per=2 * NG)
            for n in range((E0 - 2) * NG, E0 * NG):
                step(tile(n, 2 * NG))
            square(tile(E0 * NG - 1, 2 * NG))
            for t in range(NT):
                dve.wait_ge(S["added"], (E0 - 1) * NG * NO + t // 2 + 1)
                dve.bn_stats(out=K.moments[:, t * 6:t * 6 + 6], in_=K.h[:, t * D:(t + 1) * D])


def stage_fused_weights(K, wb, weights):
    nc, ins = K.nc, K.ins
    with ExitStack() as ctx:
        wT, kk, wv = weights.wT, weights.kk, weights.wv
        NP = 4
        ps = [ctx.enter_context(nc.psum_tensor(f"w_ps{b}", [P, 512], F32)) for b in range(NP)]
        ps_ready, high, read, high_v = (K.sem("w_" + n) for n in ("ps_ready", "high", "read", "high_v"))
        block = ctx.enter_context(nc.Block())
        HB = 512 // F1
        banks = [(j, c, hb) for j in range(2) for c in range(DC) for hb in range(H1 // HB)]

        @block.tensor
        def _(pe):
            pe.wait_ge(weights.parts_loaded, weights.all_parts)
            for n, (j, c, hb) in enumerate(banks):
                wait(pe, read, n - NP + 1)
                for i in range(HB // 2):
                    two = hb * HB // 2 + i
                    last = pe.matmul(ps[n % NP][:, i * 2 * F1:(i + 1) * 2 * F1], wT[:, j, two, c * P:(c + 1) * P], kk[:, j, two, :],
                                     start=True, stop=True)
                last.then_inc(ps_ready, 1)

        @block.scalar
        def _(act):
            act.wait_ge(weights.loaded, weights.all)
            for c in range(DC):
                act.activation(wb[:, 0, 2, c, :], wv[:, c, :], ACT.Copy).then_inc(high_v, 1)
            for n, (j, c, hb) in enumerate(banks):
                act.wait_ge(ps_ready, n + 1)
                act.activation(wb[:, 0, j, c, hb * 512:(hb + 1) * 512], ps[n % NP][:, :], ACT.Copy).then_inc(high, 1)

        @block.gpsimd
        def _(pool):
            for c in range(DC):
                pool.wait_ge(high_v, c + 1)
                pool.tensor_tensor(out=wb[:, 1, 2, c, :], in0=wv[:, c, :], in1=wb[:, 0, 2, c, :], op=ALU.subtract)

        @block.vector
        def _(dve):
            for n, (j, c, hb) in enumerate(banks):
                dve.wait_ge(high, n + 1)
                cols = slice(hb * 512, (hb + 1) * 512)
                dve.tensor_tensor(out=wb[:, 1, j, c, cols], in0=ps[n % NP][:, :], in1=wb[:, 0, j, c, cols], op=ALU.subtract).then_inc(read, 1)


def stage_attention1(K, wb, weights, slots):
    nc, ins = K.nc, K.ins
    W = H1 * D1
    VW = D1 + 1
    G, HG = 4, 4
    YC = W // P
    with ExitStack() as ctx:
        sb = lambda n, shape, dt=F32: ctx.enter_context(nc.sbuf_tensor("b_" + n, shape, dt))
        wo = weights.wo
        causal = sb("causal", [P, 4, P])
        xn, xT = sb("xn", [P, 2, D]), sb("xT", [P, 2, D])
        xb = sb("xb", [P, 2, 2, D], BF16)
        fold = sb("fold", [P, 2, 2 * H1, F1 // 2])
        feat = sb("feat", [P, 4, H1, 2, F1])
        ext = sb("ext", [P, 4, 2, H1])
        fsum = sb("fsum", [P, 4, H1 * 2])
        frec = sb("frec", [P, 4, H1 * 2])
        v = sb("v", [P, 2, H1, VW])
        fT = sb("fT", [P, 2, 2, HG, P])
        sc = sb("sc", [P, 2, HG, P])
        den, rden = sb("den", [P, 2, HG]), sb("rden", [P, 2, HG])
        y, yT = sb("y", [P, 2, W]), sb("yT", [P, 2, W])
        ps = lambda n: ctx.enter_context(nc.psum_tensor("b_ps_" + n, [P, 512], F32))
        ps_f = [ctx.enter_context(nc.psum_tensor(f"b_ps_f{b}", [P, 1024], F32)) for b in range(2)]
        ps_t = [ps(f"t{b}") for b in range(2)]
        ps_s, ps_o = ps("s"), ps("o")
        mask, ones_set = K.sem("b_mask"), K.sem("b_ones_set")
        norm = norm_sems(K, "b")
        names = ("xn_ready f_ps f_read ext_ready shift_ready exp_ready rec_ready mul_ready feat_ready v_ready "
                 "t_ps t_read x_read x_low folded s_ps s_ready o_ps o_read y_ready w_ps h_ready steps").split()
        S = {n: K.sem("b_" + n) for n in names}
        block = ctx.enter_context(nc.Block())
        @block.sync
        def _(sp):
            sp.dma_start(slots.rearrange("(n p) m -> p n m", p=P),
                         K.zero[:, :].rearrange("p (a m) -> p a m", a=1).broadcast_to([P, NB * SB // P, 2 * D])).then_inc(K.slots_cleared, 16)

        THROUGH = [("f00", -1), ("f01", -1), ("f10", -1), ("f11", -1), ("y0", -2), ("y1", -2),
                   ("f20", -1), ("f21", -1), ("x", 1), ("f30", -1), ("f31", -1)]

        def use(a, name):
            slot = [n for n, d in THROUGH].index(name)
            count = lambda p: 1 + sum(0 <= q + d < NT for q in range(p + 1) for d in [d for n, d in THROUGH][:slot if q == p else None])
            first = 1
            if isinstance(a.t, int):
                n = count(a.t) + first
                return n, (n - 1) % 2
            rest = count(4) + first - 4 * len(THROUGH)
            return a.t * len(THROUGH) + rest, (a.k * len(THROUGH) + rest - 1) % 2

        @block.gpsimd
        def _(pool):
            batch_mask(pool, causal, NPOS, mask, causal=True)
            pool.memset(v[:, :, :, D1:VW], 1.0).then_inc(ones_set, 1)

            def folds(a, j):
                s, half = a.b * 2 + j, F1 // 2
                pool.wait_ge(S["exp_ready"], a.t * 2 + j + 1)
                wait(pool, S["rec_ready"], a.t * 2 + j - 1)
                f = feat[:, s, :, :, :].rearrange("p h s f -> p (h s) f")
                pool.tensor_tensor(out=fold[:, j, :, :], in0=f[:, :, 0:half], in1=f[:, :, half:F1], op=ALU.add).then_inc(S["folded"], 1)

            def scale(a, j):
                s = a.b * 2 + j
                pool.wait_ge(S["rec_ready"], a.t * 2 + j + 1)
                f = feat[:, s, :, :, :].rearrange("p h s f -> p (h s) f")
                pool.tensor_tensor(out=f, in0=f, in1=frec[:, s, :].rearrange("p (h a) -> p h a", a=1).broadcast_to([P, 2 * H1, F1]),
                                   op=ALU.mult).then_inc(S["mul_ready"], 1)

            def low(a):
                pool.wait_ge(S["x_read"], a.t + 1)
                pool.tensor_tensor(out=xb[:, a.b, 1, :], in0=xT[:, a.b, :], in1=xb[:, a.b, 0, :], op=ALU.subtract).then_inc(S["x_low"], 1)

            def step(a):
                for j in range(2):
                    folds(a, j)
                scale(a, 0)
                if has(a, 1):
                    low(a.at(1))
                scale(a, 1)
            low(tile(0))
            over(pool, 0, NT - 1, step)
            step(tile(NT - 1))

        @block.scalar
        def _(act):
            root_norm(K, act, norm)

            def tokens(a, n, b):
                act.wait_ge(S["t_ps"], n)
                wait(act, S["f_ps"], (a.t - 1) * 3)
                act.activation(xT[:, a.b, :], ps_t[b][:, 0:D], ACT.Copy)
                act.activation(xb[:, a.b, 0, :], ps_t[b][:, 0:D], ACT.Copy).then_inc(S["t_read"], 1)
                act.wait_ge(S["t_read"], n)
                act.sem_inc(S["x_read"], 1)

            def exponential(a, j):
                act.wait_ge(S["shift_ready"], a.t * 2 + j + 1)
                act.activation(feat[:, a.b * 2 + j, :, :, :], feat[:, a.b * 2 + j, :, :, :], ACT.Exp).then_inc(S["exp_ready"], 1)

            def values(a):
                act.wait_ge(S["f_ps"], a.t * 3 + 3)
                wait(act, S["o_ps"], (a.t - 1) * G)
                act.activation(v[:, a.b, :, 0:D1], ps_f[(a.k * 3 + 2) % 2][:, :].rearrange("p (h e) -> p h e", h=H1),
                               ACT.Copy).then_inc(S["v_ready"], 1)

            def features(p, g):
                a = p.at(-1)
                for j in range(2):
                    n, b = use(p, f"f{g}{j}")
                    act.wait_ge(S["t_ps"], n)
                    wait(act, S["s_ps"], a.t * G + g - 1)
                    act.activation(fT[:, g % 2, j, :, :], ps_t[b][:, :].rearrange("p (h m) -> p h m", h=HG),
                                   ACT.Copy).then_inc(S["t_read"], 1)

            def outputs(p):
                a = p.at(-2)
                for j in range(2):
                    n, b = use(p, f"y{j}")
                    act.wait_ge(S["t_ps"], n)
                    wait(act, S["w_ps"], a.t - 1)
                    act.activation(yT[:, a.b, j * 512:(j + 1) * 512], ps_t[b][:, :], ACT.Copy).then_inc(S["t_read"], 1)

            def step(p):
                now, before, done = has(p, 0), has(p, -1), has(p, -2)
                if before:
                    features(p, 0)
                if now:
                    exponential(p, 0)
                if before:
                    features(p, 1)
                if done:
                    outputs(p)
                if now:
                    exponential(p, 1)
                    values(p)
                if before:
                    features(p, 2)
                if has(p, 1):
                    tokens(p.at(1), *use(p, "x"))
                if before:
                    features(p, 3)
            tokens(tile(0), 1, 0)
            passes(act, step)

        @block.tensor
        def _(pe):
            pe.wait_ge(weights.loaded, weights.all)

            def free_t(count):
                wait(pe, S["t_read"], count - 2)

            def tokens(a, n, b):
                pe.wait_ge(S["xn_ready"], a.t + 1)
                free_t(n)
                for c in range(DC):
                    last = pe.transpose(ps_t[b][:, c * P:(c + 1) * P], xn[:, a.b, c * P:(c + 1) * P], K.ident[:, :])
                last.then_inc(S["t_ps"], 1)

            def project(a, j, halves=(0, 1)):
                if j == 2:
                    pe.wait_ge(S["f_read"], a.t * 2 + 1)
                elif j == 0:
                    wait(pe, S["f_read"], a.t * 2)
                else:
                    wait(pe, S["v_ready"], a.t)
                out = ps_f[(a.k * 3 + j) % 2]
                parts = [(xh, wh, c) for xh, wh in ((0, 0), (1, 0), (0, 1)) for c in range(DC)]
                for half in halves:
                    cols = slice(half * 512, (half + 1) * 512)
                    for i, (xh, wh, c) in enumerate(parts):
                        last = pe.matmul(out[:, cols], xb[:, a.b, xh, c * P:(c + 1) * P], wb[:, wh, j, c, cols],
                                         start=(i == 0), stop=(i == len(parts) - 1))
                if halves[-1] == 1:
                    last.then_inc(S["f_ps"], 1)

            def features(p, g):
                a = p.at(-1)
                for j in range(2):
                    n, b = use(p, f"f{g}{j}")
                    free_t(n)
                    for i in range(HG):
                        last = pe.transpose(ps_t[b][:, i * P:(i + 1) * P],
                                            feat[:, a.b * 2 + j, g * HG + i, :, :].rearrange("p s f -> p (s f)"), K.ident[:, :])
                    last.then_inc(S["t_ps"], 1)

            def scores(p, g):
                a = p.at(-1)
                pe.wait_ge(S["t_read"], use(p, f"f{g}1")[0])
                wait(pe, S["s_ready"], a.t * G + g)
                for i in range(HG):
                    last = pe.matmul(ps_s[:, i * P:(i + 1) * P], fT[:, g % 2, 1, i, :], fT[:, g % 2, 0, i, :], start=True, stop=True)
                last.then_inc(S["s_ps"], 1)

            def values(a, g):
                pe.wait_ge(S["s_ready"], a.t * G + g + 1)
                wait(pe, S["o_read"], a.t * G + g)
                if g == 0:
                    wait(pe, S["h_ready"], a.t)
                for i in range(HG):
                    last = pe.matmul(ps_o[:, i * VW:(i + 1) * VW], sc[:, g % 2, i, :], v[:, a.b, g * HG + i, :], start=True, stop=True)
                last.then_inc(S["o_ps"], 1)

            def outputs(p):
                a = p.at(-2)
                pe.wait_ge(S["y_ready"], a.t * G + G)
                for j in range(2):
                    n, b = use(p, f"y{j}")
                    free_t(n)
                    for i in range(4):
                        last = pe.transpose(ps_t[b][:, i * P:(i + 1) * P], y[:, a.b, (j * 4 + i) * P:(j * 4 + i + 1) * P], K.ident[:, :])
                    last.then_inc(S["t_ps"], 1)

            def combine(p):
                a = p.at(-2)
                pe.wait_ge(S["t_read"], use(p, "y1")[0])
                pe.wait_ge(S["o_read"], a.t * G + G)
                for c in range(YC):
                    last = pe.matmul(ps_o[:, 0:D], yT[:, a.b, c * P:(c + 1) * P], wo[:, c, :], start=(c == 0), stop=(c == YC - 1))
                last.then_inc(S["w_ps"], 1)

            def step(p):
                now, before, done = has(p, 0), has(p, -1), has(p, -2)
                a = p.at(-1)
                if now:
                    pe.wait_ge(S["x_low"], p.t + 1)
                    project(p, 0)
                if done:
                    values(p.at(-2), 2)
                if before:
                    pe.wait_ge(S["feat_ready"], a.t * 2 + 2)
                    features(p, 0)
                if now:
                    project(p, 1)
                if done:
                    values(p.at(-2), 3)
                if before:
                    scores(p, 0)
                    features(p, 1)
                if now:
                    project(p, 2, (0,))
                if before:
                    scores(p, 1)
                if done:
                    outputs(p)
                if now:
                    project(p, 2, (1,))
                if before:
                    features(p, 2)
                if done:
                    combine(p)
                if before:
                    scores(p, 2)
                if has(p, 1):
                    tokens(p.at(1), *use(p, "x"))
                if before:
                    pe.wait_ge(S["v_ready"], a.t + 1)
                    values(a, 0)
                    features(p, 3)
                    values(a, 1)
                    scores(p, 3)
            tokens(tile(0), 1, 0)
            passes(pe, step)

        @block.vector
        def _(dve):
            chain = Chain(dve, S["steps"])
            chain2 = Chain(dve, K.sem("b_steps2"))
            prepare_norm(K, dve, norm)
            dve.wait_ge(mask, 3)
            dve.wait_ge(ones_set, 1)

            def tokens(a):
                wait(dve, S["f_ps"], (a.t - 1) * 3)
                normalise(K, dve, a, xn[:, a.b, :]).then_inc(S["xn_ready"], 1)

            def extremes(a, j):
                s = a.b * 2 + j
                f = ps_f[(a.k * 3 + j) % 2][:, :].rearrange("p (h f) -> p h f", h=H1)
                dve.wait_ge(S["f_ps"], a.t * 3 + j + 1)
                dve.tensor_reduce(out=ext[:, s, 0, :], in_=f, axis=AX, op=ALU.max)
                dve.tensor_reduce(out=ext[:, s, 1, :], in_=f, axis=AX, op=ALU.min).then_inc(S["ext_ready"], 1)

            def shifted(a, j):
                s, n = a.b * 2 + j, a.t * 2 + j
                f = ps_f[(a.k * 3 + j) % 2][:, :].rearrange("p (h f) -> p h f", h=H1)
                bc = lambda m: ext[:, s, m, :].rearrange("p (h a) -> p h a", a=1).broadcast_to([P, H1, F1])
                dve.wait_ge(S["ext_ready"], n + 1)
                wait(dve, S["s_ps"], (a.t - 1) * G)
                dve.tensor_tensor(out=feat[:, s, :, 0, :], in0=f, in1=bc(0), op=ALU.subtract)
                dve.tensor_tensor(out=feat[:, s, :, 1, :], in0=bc(1), in1=f, op=ALU.subtract).then_inc(S["shift_ready"], 1)
                dve.wait_ge(S["shift_ready"], n + 1)
                dve.sem_inc(S["f_read"], 1)

            def summed(a, j):
                s, n = a.b * 2 + j, a.t * 2 + j
                dve.wait_ge(S["folded"], n + 1)
                chain.start(n)
                chain.done(dve.tensor_reduce(out=fsum[:, s, :], in_=fold[:, j, :, :], axis=AX, op=ALU.add))
                dve.reciprocal(frec[:, s, :], fsum[:, s, :]).then_inc(S["rec_ready"], 1)

            def bounded(a, j):
                dve.wait_ge(S["mul_ready"], a.t * 2 + j + 1)
                f = feat[:, a.b * 2 + j, :, :, :]
                dve.tensor_scalar(out=f, in0=f, scalar1=FEAT_EPS, scalar2=None, op0=ALU.max).then_inc(S["feat_ready"], 1)

            def masked(a, g):
                n = a.t * G + g
                dve.wait_ge(S["s_ps"], n + 1)
                wait(dve, S["o_ps"], n - 1)
                dve.tensor_tensor(out=sc[:, g % 2, :, :], in0=ps_s[:, :].rearrange("p (h m) -> p h m", h=HG), in1=causal[:, :, :],
                                  op=ALU.mult).then_inc(S["s_ready"], 1)

            def normed(a, g):
                n = a.t * G + g
                dve.wait_ge(S["o_ps"], n + 1)
                if g == 0:
                    wait(dve, S["w_ps"], a.t - 1)
                o = ps_o[:, 0:HG * VW].rearrange("p (h e) -> p h e", h=HG)
                chain2.start(n * 2)
                chain2.done(dve.tensor_scalar(out=den[:, g % 2, :], in0=o[:, :, D1], scalar1=FEAT_EPS, scalar2=None, op0=ALU.add))
                chain2.done(dve.reciprocal(rden[:, g % 2, :], den[:, g % 2, :]))
                dve.tensor_tensor(out=y[:, a.b, g * HG * D1:(g + 1) * HG * D1].rearrange("p (h e) -> p h e", h=HG), in0=o[:, :, 0:D1],
                                  in1=rden[:, g % 2, :].rearrange("p (h a) -> p h a", a=1).broadcast_to([P, HG, D1]),
                                  op=ALU.mult).then_inc(S["y_ready"], 1)
                dve.wait_ge(S["y_ready"], n + 1)
                dve.sem_inc(S["o_read"], 1)

            def combined(a):
                dve.wait_ge(S["w_ps"], a.t + 1)
                hs = K.h[:, ds(a.t * D, D)]
                dve.tensor_tensor(out=hs, in0=ps_o[:, 0:D], in1=hs, op=ALU.add).then_inc(S["h_ready"], 1)
                take_moments(K, dve, a, S["h_ready"], a.t + 1)

            def step(p):
                now, before, done = has(p, 0), has(p, -1), has(p, -2)
                a = p.at(-1)
                if has(p, 1):
                    tokens(p.at(1))
                if now:
                    extremes(p, 0)
                if done:
                    normed(p.at(-2), 2)
                if now:
                    shifted(p, 0)
                if done:
                    normed(p.at(-2), 3)
                if before:
                    masked(a, 0)
                if now:
                    extremes(p, 1)
                    shifted(p, 1)
                if before:
                    masked(a, 1)
                if now:
                    summed(p, 0)
                if done:
                    combined(p.at(-2))
                if now:
                    summed(p, 1)
                if before:
                    normed(a, 0)
                    masked(a, 2)
                if now:
                    bounded(p, 0)
                if before:
                    normed(a, 1)
                    masked(a, 3)
                if now:
                    bounded(p, 1)
            tokens(tile(0))
            passes(dve, step)


def stage_experts1(K, xT, plan, slots, weights):
    nc, ins = K.nc, K.ins
    U = TOK // SB
    HU = U // 2
    N = U + NB
    assert HU % 2 == 0
    NH = HF1 + 1
    TU = SB // P
    FB = 4
    wb = weights.b
    DOWN = weights.DOWN
    with ExitStack() as ctx:
        sb = lambda n, shape, dt=F32: ctx.enter_context(nc.sbuf_tensor("g_" + n, shape, dt))
        xr = sb("xr", [P, 2, TU, 2 * D], BF16)
        xg = sb("xg", [P, 2, 2, DC, SB], BF16)
        silu = sb("silu", [P, 2, SB])
        hf = sb("hf", [P, 2, NH, SB])
        hb = sb("hb", [P, 2, 2, NH, SB], BF16)
        y = sb("y", [P, 2, TU * D])
        fetched = sb("fetched", [P, FB, 2, D])
        ps = lambda n, dt=F32: ctx.enter_context(nc.psum_tensor("g_" + n, [P, 2048 // mybir.dt.size(dt)], dt))
        ps_u = [ps(f"u{b}") for b in range(4)]
        ps_d = [ps(f"d{b}") for b in range(2)]
        ps_t = [ps(f"t{b}", BF16) for b in range(2)]
        outs = nc.dram_tensor("expert_outputs", (NB * SB, D), F32).ap()
        identb = sb("identb", [P, P], BF16)
        stored = K.sem("g_stored")
        xr_loaded = [K.sem(f"g_xr_loaded{b}") for b in range(2)]
        got = [K.sem(f"g_got{b}") for b in range(FB)]
        y_stored = [K.sem(f"g_y_stored{b}") for b in range(2)]
        S = {n: K.sem("g_" + n) for n in
             ("identb_ready sent t_ps xg_ready up_ps silu_ready hf_ready hb_high hb_low down_ps "
              "y_ready combined1 combined").split()}
        block = ctx.enter_context(nc.Block())

        def base_unit(n):
            return n if n < HU else n - NB

        def blocks(eng, step):
            over(eng, HU, HU + NB, step, peel=HU + 4)

        @block.sync
        def _(sp):
            def fetch(n):
                b = n.t - HU
                expert = sp.value_load(plan.expert[0:1, ds(b, 1)], min_val=0, max_val=E1 - 1)
                use = b + 1
                wait(sp, weights.low_down, use - 1)
                wait(sp, weights.high_down, use - 1)
                weights.load(sp, expert, 1 - n.b)
                if isinstance(n.t, int) and n.t == HU:
                    sp.wait_ge(S["sent"], 16 * 2 * NT)
                wait(sp, S["t_ps"], b - 1)
                sp.dma_start(xr[:, n.b, :, :], slots[ds(b * SB, SB), :].rearrange("(p a) m -> p a m", a=TU)).then_inc(xr_loaded[n.b], 16)
            blocks(sp, fetch)
            for q in range(NT // 4):
                sp.wait_ge(S["combined"], q * 4 + 4)
                sp.dma_start(K.out[q * 4 * P:(q + 1) * 4 * P, :].rearrange("(t p) d -> p t d", p=P),
                             K.h[:, q * 4 * D:(q + 1) * 4 * D].rearrange("p (t d) -> p t d", t=4)).then_inc(stored, 16)
            sp.wait_ge(stored, 16 * (NT // 4))

        @block.gpsimd
        def _(pool):
            pool.wait_ge(K.slots_cleared, 16)
            for k in range(2):
                for t in range(NT):
                    pool.indirect_dma_start(out=slots[:, :], out_offset=bass.IndirectOffsetOnAxis(ap=plan.slot[:, k * NT + t:k * NT + t + 1], axis=0),
                                            in_=plan.rows[:, t * 2 * D:(t + 1) * 2 * D], in_offset=None).then_inc(S["sent"], 16)

            def step(n):
                b = n.t - HU
                weights.take_low(pool, b + 1, 1 - n.b, n.b, n.half - HU // 2 + 1 + n.b)
            blocks(pool, step)
            for b in range(2):
                pool.wait_ge(y_stored[b], 16 * ((NB + 1 - b) // 2))
            for t in range(NT):
                wait(pool, S["combined"], t - FB + 1)
                for k in range(2):
                    pool.indirect_dma_start(out=fetched[:, t % FB, k, :], out_offset=None, in_=outs[:, :],
                                            in_offset=bass.IndirectOffsetOnAxis(ap=plan.slot[:, k * NT + t:k * NT + t + 1], axis=0))\
                        .then_inc(got[t % FB], 16)

        @block.tensor
        def _(pe):
            def transposes(n):
                b = n.t - HU
                pe.wait_ge(xr_loaded[n.b], (n.half - HU // 2) * 16 + 16)
                wait(pe, S["xg_ready"], b - 1)
                for hl in range(2):
                    for c in range(DC):
                        for a in range(TU):
                            i = (hl * DC + c) * TU + a
                            last = pe.transpose(ps_t[n.b][:, i * P:(i + 1) * P],
                                                xr[:, n.b, a, hl * D + c * P:hl * D + (c + 1) * P], identb[:, :])
                last.then_inc(S["t_ps"], 1)

            def up(n, x, slot):
                for c in range(NH):
                    q, bank = n.t * NH + c, (n.k * NH + c) % 4
                    wait(pe, S["hf_ready"], q - 3)
                    for half in range(2 if c < HF1 else 1):
                        col = (half * HF1 + c) * P if c < HF1 else 2 * HF1 * P
                        parts = [(wh, xh, kc) for wh, xh in ((0, 0), (1, 0), (0, 1)) for kc in range(DC)]
                        for i, (wh, xh, kc) in enumerate(parts):
                            w0 = kc * 2 * HID1 + col
                            last = pe.matmul(ps_u[bank][:, half * SB:(half + 1) * SB], wb[:, slot, wh, w0:w0 + P], x(xh, kc),
                                             start=(i == 0), stop=(i == len(parts) - 1))
                    last.then_inc(S["up_ps"], 1)

            def down(n, slot):
                if not isinstance(n.t, int) or HU <= n.t < HU + NB:
                    pe.wait_ge(weights.low_down, n.t - HU + 2)
                pe.wait_ge(S["hb_high"], n.t + 1)
                pe.wait_ge(S["hb_low"], n.t + 1)
                wait(pe, S["y_ready"], n.t - 1)
                for a in range(TU):
                    parts = [(hh, wh, c) for hh, wh in ((0, 0), (1, 0), (0, 1)) for c in range(NH)]
                    for i, (hh, wh, c) in enumerate(parts):
                        w, w0 = (P, W1 + c * D) if c < HF1 else (HT1, DOWN)
                        last = pe.matmul(ps_d[n.b][:, a * D:(a + 1) * D], hb[0:w, n.b, hh, c, a * P:(a + 1) * P],
                                         wb[0:w, slot, wh, w0:w0 + D], start=(i == 0), stop=(i == len(parts) - 1))
                last.then_inc(S["down_ps"], 1)

            def up_base(n):
                u = base_unit(n.t)
                up(n, lambda hl, kc: xT[:, hl, kc, u * SB:(u + 1) * SB], 2)

            def up_block(n):
                b = n.t - HU
                pe.wait_ge(weights.low_up, b + 2)
                pe.wait_ge(S["xg_ready"], b + 1)
                up(n, lambda hl, kc: xg[:, n.b, hl, kc, :], n.b)

            pe.wait_ge(S["identb_ready"], 1)
            pe.wait_ge(weights.low_up, 1)
            pe.wait_ge(weights.low_down, 1)
            up_base(tile(0))
            for n in range(1, HU):
                up_base(tile(n))
                down(tile(n - 1), 2)
            transposes(tile(HU))
            up_block(tile(HU))
            transposes(tile(HU + 1))
            down(tile(HU - 1), 2)

            def step(n):
                up_block(n)
                transposes(n.at(1))
                down(n.at(-1), 1 - n.b)
            over(pe, HU + 1, HU + NB - 1, step, peel=HU + 4)
            last = tile(HU + NB - 1)
            up_block(last)
            down(last.at(-1), 1 - last.b)
            for n in range(HU + NB, N):
                up_base(tile(n))
                down(tile(n - 1), last.b if n == HU + NB else 2)
            down(tile(N - 1), 2)

        @block.scalar
        def _(act):
            act.activation(identb[:, :], K.ident[:, :], ACT.Copy).then_inc(S["identb_ready"], 1)

            def prepare_up(n, kc):
                wait(act, S["up_ps"], (n.t - 1) * NH)
                weights.take_high_up(act, 1 - n.b, n.b, n.half - HU // 2 + 1 + n.b, kc)

            def prepare_tokens(n):
                b = n.t - HU
                act.wait_ge(S["t_ps"], b + 1)
                wait(act, S["up_ps"], (n.t - 1) * NH)
                act.activation(xg[:, n.b, :, :, :].rearrange("p h c m -> p (h c m)"), ps_t[n.b][:, :], ACT.Copy).then_inc(S["xg_ready"], 1)

            def prepare_down(n):
                wait(act, S["down_ps"], n.t - 1)
                weights.take_high_down(act, 1 - n.b, n.b)

            def silus(n, between=None):
                if between:
                    between(0)
                for c in range(NH):
                    w = P if c < HF1 else HT1
                    q, bank = n.t * NH + c, (n.k * NH + c) % 4
                    act.wait_ge(S["up_ps"], q + 1)
                    wait(act, S["hf_ready"], q - 1)
                    act.activation(silu[0:w, c % 2, :], ps_u[bank][0:w, 0:SB], ACT.Silu).then_inc(S["silu_ready"], 1)
                    if between and c == 1:
                        between(1)

            def highs(n):
                act.wait_ge(S["hf_ready"], n.t * NH + NH)
                wait(act, S["down_ps"], n.t - 1)
                act.activation(hb[:, n.b, 0, 0:HF1, :], hf[:, n.b, 0:HF1, :], ACT.Copy)
                act.activation(hb[0:HT1, n.b, 0, HF1, :], hf[0:HT1, n.b, HF1, :], ACT.Copy).then_inc(S["hb_high"], 1)

            def store(n):
                b = n.t - HU
                act.wait_ge(S["y_ready"], n.t + 1)
                act.dma_start(outs[ds(b * SB, SB), :].rearrange("(p a) m -> p (a m)", a=TU), y[:, n.b, :]).then_inc(y_stored[n.b], 16)

            for n in range(HU - 1):
                silus(tile(n))
                highs(tile(n))

            def step(n):
                if not isinstance(n.t, int) or n.t >= HU + 2:
                    store(n.at(-2))
                silus(n, lambda kc: prepare_up(n.at(1), kc))
                prepare_tokens(n.at(1))
                highs(n)
                prepare_down(n.at(1))
            over(act, HU - 1, HU + NB - 1, step, peel=HU + 4)
            for n in range(HU + NB - 1, N):
                if n < HU + NB + 2:
                    store(tile(n - 2))
                silus(tile(n))
                highs(tile(n))

        @block.vector
        def _(dve):
            def gated(n):
                for c in range(NH):
                    w = P if c < HF1 else HT1
                    q, bank = n.t * NH + c, (n.k * NH + c) % 4
                    dve.wait_ge(S["silu_ready"], q + 1)
                    if c == 0:
                        wait(dve, S["hb_high"], n.t - 1)
                        wait(dve, S["hb_low"], n.t - 1)
                    other = ps_u[bank][:, SB:2 * SB] if c < HF1 else ps_u[bank][HT1:2 * HT1, 0:SB]
                    dve.tensor_tensor(out=hf[0:w, n.b, c, :], in0=silu[0:w, c % 2, :], in1=other, op=ALU.mult).then_inc(S["hf_ready"], 1)

            def lows(n):
                dve.wait_ge(S["hb_high"], n.t + 1)
                dve.tensor_tensor(out=hb[:, n.b, 1, 0:HF1, :], in0=hf[:, n.b, 0:HF1, :], in1=hb[:, n.b, 0, 0:HF1, :], op=ALU.subtract)
                dve.tensor_tensor(out=hb[0:HT1, n.b, 1, HF1, :], in0=hf[0:HT1, n.b, HF1, :], in1=hb[0:HT1, n.b, 0, HF1, :],
                                  op=ALU.subtract).then_inc(S["hb_low"], 1)

            def take_block(n):
                dve.wait_ge(S["down_ps"], n.t + 1)
                wait(dve, y_stored[n.b], (n.half - HU // 2) * 16)
                dve.tensor_scalar(out=y[:, n.b, :], in0=ps_d[n.b][:, :], scalar1=1.0, scalar2=None, op0=ALU.mult).then_inc(S["y_ready"], 1)

            def take_base(n):
                u = base_unit(n.t)
                dve.wait_ge(S["down_ps"], n.t + 1)
                hs = K.h[:, u * TU * D:(u + 1) * TU * D]
                dve.tensor_tensor(out=hs, in0=ps_d[n.b][:, :], in1=hs, op=ALU.add).then_inc(S["y_ready"], 1)

            def combine(t):
                dve.wait_ge(got[t % FB], (t // FB + 1) * 32)
                u = t // TU
                dve.wait_ge(S["y_ready"], (u if u < HU else u + NB) + 1)
                hs = K.h[:, t * D:(t + 1) * D]
                for k in range(2):
                    wgt = plan.weight[:, k * NT + t:k * NT + t + 1]
                    dve.scalar_tensor_tensor(out=hs, in0=fetched[:, t % FB, k, :], scalar=wgt, in1=hs, op0=ALU.mult, op1=ALU.add)\
                       .then_inc(S["combined1" if k == 0 else "combined"], 1)
                    if k == 0:
                        dve.wait_ge(S["combined1"], t + 1)

            gated(tile(0))
            lows(tile(0))
            for n in range(1, HU):
                gated(tile(n))
                lows(tile(n))
                take_base(tile(n - 1))
            gated(tile(HU))
            lows(tile(HU))
            take_base(tile(HU - 1))

            def step(n):
                gated(n)
                lows(n)
                take_block(n.at(-1))
            over(dve, HU + 1, HU + NB, step, peel=HU + 4)
            for n in range(HU + NB, N):
                gated(tile(n))
                lows(tile(n))
                (take_block if n == HU + NB else take_base)(tile(n - 1))
                if n > HU + NB:
                    for t in range((n - HU - NB - 1) * NT // HU, (n - HU - NB) * NT // HU):
                        combine(t)
            take_base(tile(N - 1))
            for t in range((HU - 1) * NT // HU, NT):
                combine(t)


def build(nc, ins, out):
    with ExitStack() as ctx:
        K = Core(nc, ctx, ins, out)
        slots = nc.dram_tensor("slots", (NB * SB, 2 * D), BF16).ap()
        with ExitStack() as first:
            attention0 = Attention0Weights(nc, first, K)
            with nc.sbuf_tensor("stats", [P, NT * 3 * D], F32) as stats, ExitStack() as tokeniser:
                projection = ProjectionWeights(nc, tokeniser, K)
                stage_statistics(K, stats, (projection, attention0))
                stage_projection(K, stats, projection)
            stage_attention0(K, attention0)
        with ExitStack() as second:
            attention1 = Attention1Weights(nc, second, K)
            with nc.sbuf_tensor("xT", [P, DC, TOK], F32) as xT, nc.sbuf_tensor("gate", [P, E0, NT], F32) as gate, ExitStack() as moe:
                shared = SharedWeights(nc, moe, K)
                early = Experts0Inputs(nc, moe, K)
                stage_gate(K, "f0_", E0, route0(gate), xT, later=(shared,))
                stage_shared0(K, xT, shared, gate, early)
                stage_experts0(K, xT, early, (attention1,))
            with nc.sbuf_tensor("wb", [P, 2, 3, DC, H1 * F1], BF16) as wb:
                stage_fused_weights(K, wb, attention1)
                stage_attention1(K, wb, attention1, slots)
        K.renew_semaphores()
        with nc.sbuf_tensor("xT1", [P, 2, DC, TOK], BF16) as xT, ExitStack() as moe:
            plan = Plan(nc, moe, K)
            weights = ExpertWeights(nc, moe, K)
            stage_gate(K, "f1_", E1, route1(), xT, plan, weights)
            stage_experts1(K, xT, plan, slots, weights)


def arranged(i):
    import numpy as np

    up = np.concatenate([i["L1_ffn_exp_wgu"], i["L1_ffn_base_wgu"][None]])
    down = np.concatenate([i["L1_ffn_exp_wd"], i["L1_ffn_base_wd"][None]])
    whole = HF1 * P
    up = np.concatenate([up[..., :whole], up[..., HID1:HID1 + whole], up[..., whole:HID1], up[..., HID1 + whole:]], axis=-1)
    return {
        "x": i["x"].reshape(TOK, BLK * D),
        "w_proj": i["L0_tok_w_proj_w"].reshape(D),
        "b_proj": i["L0_tok_w_proj_b"],
        "s_proj_w": i["L0_tok_s_proj_w"],
        "s_proj_b": i["L0_tok_s_proj_b"],
        "ln_g": i["L0_tok_ln_g"],
        "ln_b": i["L0_tok_ln_b"],
        "pos_emb": i["L0_tok_pos_emb"],
        **{f"a0_w{n}T": i[f"L0_attn_W{n}"].T for n in "qkvo"},
        **{f"a0_b{n}": i[f"L0_attn_b{n}"] for n in "qkvo"},
        "a1_wqT": i["L1_attn_Wq"].T,
        "a1_wkT": i["L1_attn_Wk"].T,
        "a1_kq": i["L1_attn_Kq"],
        "a1_kk": i["L1_attn_Kk"],
        "a1_wv": i["L1_attn_Wv"],
        "a1_wo": i["L1_attn_Wo"],
        "f1_gate": i["L1_ffn_gate_w"],
        "f1_up": up.reshape(E1 + 1, DC, P, 2 * HID1).transpose(0, 2, 1, 3).reshape((E1 + 1) * P, W1),
        "f1_down": down[:, :whole].reshape(E1 + 1, HF1, P, D).transpose(0, 2, 1, 3).reshape((E1 + 1) * P, HF1 * D),
        "f1_rest": down[:, whole:].reshape((E1 + 1) * HT1, D),
        "f0_gate": i["L0_ffn_gate_w"].T,
        "f0_gate_bias": i["L0_ffn_expert_bias"],
        "f0_up": i["L0_ffn_w_up"].transpose(0, 2, 1).reshape(E0 * D, HID0),
        "f0_down": i["L0_ffn_w_down"].transpose(0, 2, 1).reshape(E0 * HID0, D),
        "f0_shared_up": i["L0_ffn_shared_w_up"].T,
        "f0_shared_down": i["L0_ffn_shared_w_down"].T,
    }


def kernel(**inputs):
    import numpy as np
    from concourse import bacc
    from concourse.bass_utils import run_bass_kernel_spmd

    nc = bacc.Bacc("TRN2", target_bir_lowering=False, num_devices=1)
    arrays, args = {}, {}
    for name, a in arranged({k: np.asarray(v) for k, v in inputs.items()}).items():
        a = np.ascontiguousarray(a)
        arrays["in_" + name] = a
        args[name] = nc.dram_tensor("in_" + name, a.shape, mybir.dt.from_np(a.dtype), kind="ExternalInput").ap()
    out = nc.dram_tensor("out_0_dram", (TOK // NPOS, NPOS, D), F32, kind="ExternalOutput").ap()
    build(nc, args, out.rearrange("b s d -> (b s) d"))
    r = run_bass_kernel_spmd(nc, [arrays], core_ids=[0])
    return r.results[0]["out_0_dram"]
```
